# Optimizing a Trainium2 kernel written in Bass

```python
import numpy as np
import jax
import jax.numpy as jnp

def _softmax(x, axis=-1):
    return jax.nn.softmax(x, axis=axis)

def _gelu(x):
    return jax.nn.gelu(x, approximate=True)

def _silu(x):
    return jax.nn.silu(x)

def _sigmoid(x):
    return jax.nn.sigmoid(x)

def _layernorm(x, axis=-1, eps=1e-05):
    m = jnp.mean(x, axis=axis, keepdims=True)
    v = jnp.var(x, axis=axis, keepdims=True)
    return (x - m) / jnp.sqrt(v + eps)

def _scatter_add(tgt, idx, src, axis=0):
    return tgt.at[idx].add(src)

def _segment_sum(src, seg, n):
    return jax.ops.segment_sum(src, seg, n)
kernel_name = 'mk_vit_tower_postln_d2_tok_img256_r4_8ab9e4'

def setup_inputs(seed: int=0):
    np.random.seed(seed)
    _w = jnp.asarray

    def _rec_inputs():
        import jax
        import jax.numpy as jnp
        _rk = jax.random.key(seed)
        x = -0.000125008 + 0.999885 * jax.random.normal(jax.random.fold_in(_rk, 1), (128, 64, 64, 64), jnp.float32)
        return x
    x = _rec_inputs()

    def _L0_tok_setup():
        import jax, jax.numpy as jnp
        import numpy as np
        B, C, H, W = (32, 64, 64, 64)
        STRIDE, HEADS = (4, 8)

        def _ln(x, w, b):
            mu = x.mean(-1, keepdims=True)
            var = ((x - mu) ** 2).mean(-1, keepdims=True)
            return (x - mu) * jax.lax.rsqrt(var + 1e-05) * w + b
        key = jax.random.key(seed)
        ks = jax.random.split(key, 4)
        return {'features': jax.random.normal(ks[0], (B, C, H, W), dtype=jnp.float32), 'ln_q_w': jnp.ones((C,), jnp.float32), 'ln_q_b': jnp.zeros((C,), jnp.float32), 'Wq': jax.random.normal(ks[1], (C, C), dtype=jnp.float32) * 0.02, 'ln_kv_w': jnp.ones((C,), jnp.float32), 'ln_kv_b': jnp.zeros((C,), jnp.float32), 'Wkv': jax.random.normal(ks[2], (2 * C, C), dtype=jnp.float32) * 0.02, 'proj_w': jax.random.normal(ks[3], (C, C), dtype=jnp.float32) * 0.02, 'proj_b': jnp.zeros((C,), jnp.float32), 'conv_stride': STRIDE, 'num_heads': HEADS}
    _L0_tok_all = _L0_tok_setup()
    _L0_tok_in = {k: v for k, v in _L0_tok_all.items() if k in ('ln_q_w', 'ln_q_b', 'Wq', 'ln_kv_w', 'ln_kv_b', 'Wkv', 'proj_w', 'proj_b')}
    del _L0_tok_all

    def _L0_attn_setup():
        import jax, jax.numpy as jnp
        import numpy as np
        GAMMA = 0.96875
        SCALE_BASE = 512.0

        def xpos_rope(x, downscale=False):
            B, S, D = x.shape
            half = D // 2
            inv_freq = 1.0 / 10000.0 ** (jnp.arange(0, D, 2, dtype=jnp.float32) / D)
            pos = jnp.arange(S, dtype=jnp.float32)
            ang = pos[:, None] * inv_freq[None, :]
            sin, cos = (jnp.sin(ang), jnp.cos(ang))
            base = (jnp.arange(0, D, 2, dtype=jnp.float32) + 0.4 * D) / (1.4 * D)
            scale = base[None, :] ** (pos[:, None] / SCALE_BASE)
            if downscale:
                scale = 1.0 / scale
            x1 = x[..., 0::2]
            x2 = x[..., 1::2]
            r1 = (x1 * cos - x2 * sin) * scale
            r2 = (x1 * sin + x2 * cos) * scale
            out = jnp.stack([r1, r2], axis=-1).reshape(B, S, D)
            return out

        def get_D(gamma, seq_len):
            n = jnp.arange(seq_len, dtype=jnp.float32)
            diff = n[:, None] - n[None, :]
            mask = diff >= 0
            D = jnp.where(mask, gamma ** jnp.where(mask, diff, 0.0), 0.0)
            return D

        def _reference_tuple_inner(x, W_Q, W_K, W_V):
            S = x.shape[1]
            D = get_D(GAMMA, S)
            Q = xpos_rope(x @ W_Q, downscale=False)
            K = xpos_rope(x @ W_K, downscale=True)
            V = x @ W_V
            ret = jnp.einsum('bnd,bmd->bnm', Q, K) * D[None, :, :]
            out = jnp.einsum('bnm,bmv->bnv', ret, V)
            return (out, ret)
        key = jax.random.key(seed)
        k1, k2, k3, k4 = jax.random.split(key, 4)
        B, S, d_model, d_k, d_v = (8, 1024, 64, 64, 64)
        x = jax.random.normal(k1, (B, S, d_model), dtype=jnp.float32)
        W_Q = jax.random.normal(k2, (d_model, d_k), dtype=jnp.float32) / d_model
        W_K = jax.random.normal(k3, (d_model, d_k), dtype=jnp.float32) / d_model
        W_V = jax.random.normal(k4, (d_model, d_v), dtype=jnp.float32) / d_model
        return {'x': x, 'W_Q': W_Q, 'W_K': W_K, 'W_V': W_V}
    _L0_attn_all = _L0_attn_setup()
    _L0_attn_in = {k: v for k, v in _L0_attn_all.items() if k in ('W_Q', 'W_K', 'W_V')}
    del _L0_attn_all

    def _L0_ffn_setup():
        import jax, jax.numpy as jnp
        import numpy as np
        B, N, D = (16, 1024, 64)
        NUM_EXPERTS, TOP_K, HEADS = (4, 2, 4)
        N_EDGES = 262144
        LN_EPS = 1e-05

        def _layernorm(x, g, b):
            mu = x.mean(-1, keepdims=True)
            var = ((x - mu) ** 2).mean(-1, keepdims=True)
            return (x - mu) * jax.lax.rsqrt(var + LN_EPS) * g + b

        def _forward(x, edge_index, W_gat, att_src, att_dst, b_gat, ln_gamma, ln_beta, W1, b1, W2, b2):
            Bc, Nc, Dc = x.shape
            M = Bc * Nc
            x_flat = x.reshape(M, Dc)
            h = (x_flat @ W_gat).reshape(M, HEADS, NUM_EXPERTS)
            loops = jnp.arange(M, dtype=edge_index.dtype)
            src = jnp.concatenate([edge_index[0], loops])
            dst = jnp.concatenate([edge_index[1], loops])
            a_src = (h * att_src).sum(-1)
            a_dst = (h * att_dst).sum(-1)
            e = jax.nn.leaky_relu(a_src[src] + a_dst[dst], negative_slope=0.2)
            e_max = jax.ops.segment_max(e, dst, num_segments=M)
            ee = jnp.exp(e - e_max[dst])
            denom = jax.ops.segment_sum(ee, dst, num_segments=M)
            alpha = ee / (denom[dst] + 1e-16)
            msg = h[src] * alpha[:, :, None]
            agg = jax.ops.segment_sum(msg, dst, num_segments=M).reshape(M, HEADS * NUM_EXPERTS) + b_gat
            scores = _layernorm(agg, ln_gamma, ln_beta).reshape(M, HEADS, NUM_EXPERTS).mean(1)
            scores = scores.reshape(Bc, Nc, NUM_EXPERTS)
            topk_s, topk_i = jax.lax.top_k(scores, TOP_K)
            w = jax.nn.softmax(topk_s, axis=-1)
            out = jnp.zeros_like(x)
            for ei in range(NUM_EXPERTS):
                g = jnp.where(topk_i == ei, w, 0.0).sum(-1)
                hh = jax.nn.gelu(x @ W1[ei] + b1[ei], approximate=False)
                out = out + g[..., None] * (hh @ W2[ei] + b2[ei])
            return out
        key = jax.random.key(seed)
        ks = jax.random.split(key, 8)
        s = 0.05
        return {'x': jax.random.normal(ks[0], (B, N, D), jnp.float32), 'W_gat': jax.random.normal(ks[1], (D, HEADS * NUM_EXPERTS), jnp.float32) * s, 'att_src': jax.random.normal(ks[2], (HEADS, NUM_EXPERTS), jnp.float32) * s, 'att_dst': jax.random.normal(ks[3], (HEADS, NUM_EXPERTS), jnp.float32) * s, 'b_gat': jnp.zeros((HEADS * NUM_EXPERTS,), jnp.float32), 'ln_gamma': jnp.ones((HEADS * NUM_EXPERTS,), jnp.float32), 'ln_beta': jnp.zeros((HEADS * NUM_EXPERTS,), jnp.float32), 'W1': jax.random.normal(ks[4], (NUM_EXPERTS, D, 2 * D), jnp.float32) * s, 'b1': jnp.zeros((NUM_EXPERTS, 2 * D), jnp.float32), 'W2': jax.random.normal(ks[5], (NUM_EXPERTS, 2 * D, D), jnp.float32) * s, 'b2': jnp.zeros((NUM_EXPERTS, D), jnp.float32), 'edge_index': jax.random.randint(ks[6], (2, N_EDGES), 0, B * N, jnp.int32)}
    _L0_ffn_all = _L0_ffn_setup()
    _L0_ffn_in = {k: v for k, v in _L0_ffn_all.items() if k in ('W_gat', 'att_src', 'att_dst', 'b_gat', 'ln_gamma', 'ln_beta', 'W1', 'b1', 'W2', 'b2', 'edge_index')}
    del _L0_ffn_all

    def _L1_attn_setup():
        import jax, jax.numpy as jnp
        import numpy as np
        H = 8
        M = 64
        PINV_ITERS = 6
        PAD = 16

        def layernorm(x, g, b, eps=1e-05):
            mu = x.mean(-1, keepdims=True)
            var = ((x - mu) ** 2).mean(-1, keepdims=True)
            return (x - mu) * jax.lax.rsqrt(var + eps) * g + b

        def moore_penrose_pinv(x, iters=PINV_ITERS):
            abs_x = jnp.abs(x)
            col = abs_x.sum(-1)
            row = abs_x.sum(-2)
            z = jnp.swapaxes(x, -1, -2) / (jnp.max(col) * jnp.max(row))
            eye = jnp.eye(x.shape[-1], dtype=x.dtype)
            for _ in range(iters):
                xz = x @ z
                z = 0.25 * z @ (13.0 * eye - xz @ (15.0 * eye - xz @ (7.0 * eye - xz)))
            return z

        def attn_block(y, ln1_g, ln1_b, w_qkv, w_out, b_out, res_w, ln2_g, ln2_b, w1, b1, w2, b2):
            B, N, D = y.shape
            inner = w_qkv.shape[1] // 3
            dh = inner // H
            xn = layernorm(y, ln1_g, ln1_b)
            qkv = xn @ w_qkv
            q, k, v = jnp.split(qkv, 3, axis=-1)
            to_heads = lambda t: t.reshape(B, N, H, dh).transpose(0, 2, 1, 3)
            q, k, v = map(to_heads, (q, k, v))
            q = q * dh ** (-0.5)
            l = N // M
            q_l = q.reshape(B, H, M, l, dh).mean(3)
            k_l = k.reshape(B, H, M, l, dh).mean(3)
            attn1 = jax.nn.softmax(jnp.einsum('bhnd,bhmd->bhnm', q, k_l), axis=-1)
            attn2 = jax.nn.softmax(jnp.einsum('bhid,bhjd->bhij', q_l, k_l), axis=-1)
            attn3 = jax.nn.softmax(jnp.einsum('bhmd,bhnd->bhmn', q_l, k), axis=-1)
            attn2_inv = moore_penrose_pinv(attn2)
            out = attn1 @ attn2_inv @ (attn3 @ v)
            res = jax.lax.conv_general_dilated(v, res_w, window_strides=(1, 1), padding=[(PAD, PAD), (0, 0)], dimension_numbers=('NCHW', 'OIHW', 'NCHW'), feature_group_count=H)
            out = out + res
            out = out.transpose(0, 2, 1, 3).reshape(B, N, inner)
            y = y + out @ w_out + b_out
            yn = layernorm(y, ln2_g, ln2_b)
            hdn = jax.nn.gelu(yn @ w1 + b1, approximate=False)
            return y + hdn @ w2 + b2
        key = jax.random.key(seed)
        ks = jax.random.split(key, 8)
        B, N, D, NB = (4, 1024, 64, 2)
        inner = D
        p = lambda k, shp: jax.random.normal(k, shp, jnp.float32) * 0.02
        return {'x': jax.random.normal(ks[0], (B, N, D), jnp.float32), 'ln1_g': jnp.ones((NB, D), jnp.float32), 'ln1_b': jnp.zeros((NB, D), jnp.float32), 'w_qkv': p(ks[1], (NB, D, 3 * inner)), 'w_out': p(ks[2], (NB, inner, D)), 'b_out': jnp.zeros((NB, D), jnp.float32), 'res_w': p(ks[3], (NB, H, 1, 33, 1)), 'ln2_g': jnp.ones((NB, D), jnp.float32), 'ln2_b': jnp.zeros((NB, D), jnp.float32), 'w1': p(ks[4], (NB, D, 2 * D)), 'b1': jnp.zeros((NB, 2 * D), jnp.float32), 'w2': p(ks[5], (NB, 2 * D, D)), 'b2': jnp.zeros((NB, D), jnp.float32)}
    _L1_attn_all = _L1_attn_setup()
    _L1_attn_in = {k: v for k, v in _L1_attn_all.items() if k in ('ln1_g', 'ln1_b', 'w_qkv', 'w_out', 'b_out', 'res_w', 'ln2_g', 'ln2_b', 'w1', 'b1', 'w2', 'b2')}
    del _L1_attn_all

    def _L1_ffn_setup():
        import jax, jax.numpy as jnp
        import numpy as np
        B, T, D, H, E = (16, 1024, 64, 128, 8)
        key = jax.random.key(seed)
        ks = jax.random.split(key, 5)
        x = jax.random.normal(ks[0], (B, T, D), dtype=jnp.float32)
        gate_w = jax.random.normal(ks[1], (D, E), dtype=jnp.float32) * 0.02
        gate_b = jnp.zeros((E,), dtype=jnp.float32)
        W1 = jax.random.normal(ks[2], (E, D, H), dtype=jnp.float32) * 0.02
        b1 = jnp.zeros((E, H), dtype=jnp.float32)
        W2 = jax.random.normal(ks[3], (E, H, D), dtype=jnp.float32) * 0.02
        b2 = jnp.zeros((E, D), dtype=jnp.float32)
        return {'x': x, 'gate_w': gate_w, 'gate_b': gate_b, 'W1': W1, 'b1': b1, 'W2': W2, 'b2': b2}
    _L1_ffn_all = _L1_ffn_setup()
    _L1_ffn_in = {k: v for k, v in _L1_ffn_all.items() if k in ('gate_w', 'gate_b', 'W1', 'b1', 'W2', 'b2')}
    del _L1_ffn_all
    return {'x': x, 'L0_tok_ln_q_w': _L0_tok_in['ln_q_w'], 'L0_tok_ln_q_b': _L0_tok_in['ln_q_b'], 'L0_tok_Wq': _L0_tok_in['Wq'], 'L0_tok_ln_kv_w': _L0_tok_in['ln_kv_w'], 'L0_tok_ln_kv_b': _L0_tok_in['ln_kv_b'], 'L0_tok_Wkv': _L0_tok_in['Wkv'], 'L0_tok_proj_w': _L0_tok_in['proj_w'], 'L0_tok_proj_b': _L0_tok_in['proj_b'], 'L0_attn_W_Q': _L0_attn_in['W_Q'], 'L0_attn_W_K': _L0_attn_in['W_K'], 'L0_attn_W_V': _L0_attn_in['W_V'], 'L0_ffn_W_gat': _L0_ffn_in['W_gat'], 'L0_ffn_att_src': _L0_ffn_in['att_src'], 'L0_ffn_att_dst': _L0_ffn_in['att_dst'], 'L0_ffn_b_gat': _L0_ffn_in['b_gat'], 'L0_ffn_ln_gamma': _L0_ffn_in['ln_gamma'], 'L0_ffn_ln_beta': _L0_ffn_in['ln_beta'], 'L0_ffn_W1': _L0_ffn_in['W1'], 'L0_ffn_b1': _L0_ffn_in['b1'], 'L0_ffn_W2': _L0_ffn_in['W2'], 'L0_ffn_b2': _L0_ffn_in['b2'], 'L0_ffn_edge_index': _L0_ffn_in['edge_index'], 'L1_attn_ln1_g': _L1_attn_in['ln1_g'], 'L1_attn_ln1_b': _L1_attn_in['ln1_b'], 'L1_attn_w_qkv': _L1_attn_in['w_qkv'], 'L1_attn_w_out': _L1_attn_in['w_out'], 'L1_attn_b_out': _L1_attn_in['b_out'], 'L1_attn_res_w': _L1_attn_in['res_w'], 'L1_attn_ln2_g': _L1_attn_in['ln2_g'], 'L1_attn_ln2_b': _L1_attn_in['ln2_b'], 'L1_attn_w1': _L1_attn_in['w1'], 'L1_attn_b1': _L1_attn_in['b1'], 'L1_attn_w2': _L1_attn_in['w2'], 'L1_attn_b2': _L1_attn_in['b2'], 'L1_ffn_gate_w': _L1_ffn_in['gate_w'], 'L1_ffn_gate_b': _L1_ffn_in['gate_b'], 'L1_ffn_W1': _L1_ffn_in['W1'], 'L1_ffn_b1': _L1_ffn_in['b1'], 'L1_ffn_W2': _L1_ffn_in['W2'], 'L1_ffn_b2': _L1_ffn_in['b2']}

def reference(x, L0_tok_ln_q_w, L0_tok_ln_q_b, L0_tok_Wq, L0_tok_ln_kv_w, L0_tok_ln_kv_b, L0_tok_Wkv, L0_tok_proj_w, L0_tok_proj_b, L0_attn_W_Q, L0_attn_W_K, L0_attn_W_V, L0_ffn_W_gat, L0_ffn_att_src, L0_ffn_att_dst, L0_ffn_b_gat, L0_ffn_ln_gamma, L0_ffn_ln_beta, L0_ffn_W1, L0_ffn_b1, L0_ffn_W2, L0_ffn_b2, L0_ffn_edge_index, L1_attn_ln1_g, L1_attn_ln1_b, L1_attn_w_qkv, L1_attn_w_out, L1_attn_b_out, L1_attn_res_w, L1_attn_ln2_g, L1_attn_ln2_b, L1_attn_w1, L1_attn_b1, L1_attn_w2, L1_attn_b2, L1_ffn_gate_w, L1_ffn_gate_b, L1_ffn_W1, L1_ffn_b1, L1_ffn_W2, L1_ffn_b2):
    import jax
    import jax.numpy as jnp

    def _L0_tok_ref(features, ln_q_w, ln_q_b, Wq, ln_kv_w, ln_kv_b, Wkv, proj_w, proj_b, conv_stride, num_heads):
        import jax, jax.numpy as jnp
        import numpy as np
        B, C, H, W = (32, 64, 64, 64)
        STRIDE, HEADS = (4, 8)

        def _ln(x, w, b):
            mu = x.mean(-1, keepdims=True)
            var = ((x - mu) ** 2).mean(-1, keepdims=True)
            return (x - mu) * jax.lax.rsqrt(var + 1e-05) * w + b
        s = conv_stride
        b, c, hh, ww = features.shape
        h, w = (hh // s, ww // s)
        hw, n, d = (h * w, s * s, c // num_heads)
        scale = c ** (-0.5)
        x = features.reshape(b, c, h, s, w, s)
        reduce_feats = x.mean((3, 5)).reshape(b, c, hw).transpose(0, 2, 1)
        unf = x.transpose(0, 1, 2, 4, 3, 5).reshape(b, c, hw, n).transpose(0, 2, 3, 1)
        q = _ln(reduce_feats, ln_q_w, ln_q_b) @ Wq.T
        q = q.reshape(b, hw, num_heads, d).transpose(0, 2, 1, 3)
        kv = _ln(unf, ln_kv_w, ln_kv_b) @ Wkv.T
        kv = kv.reshape(b, hw, n, 2, num_heads, d).transpose(3, 0, 4, 1, 2, 5)
        k, v = (kv[0], kv[1])
        attn = jax.nn.softmax(jnp.einsum('bhpd,bhpnd->bhpn', q * scale, k), axis=-1)
        aggre = jnp.einsum('bhpn,bhpnd->bhpd', attn, v)
        aggre = aggre.transpose(0, 2, 1, 3).reshape(b, hw, c)
        return reduce_feats + aggre @ proj_w.T + proj_b

    def _L0_attn_ref(x, W_Q, W_K, W_V):
        import jax, jax.numpy as jnp
        import numpy as np
        GAMMA = 0.96875
        SCALE_BASE = 512.0

        def xpos_rope(x, downscale=False):
            B, S, D = x.shape
            half = D // 2
            inv_freq = 1.0 / 10000.0 ** (jnp.arange(0, D, 2, dtype=jnp.float32) / D)
            pos = jnp.arange(S, dtype=jnp.float32)
            ang = pos[:, None] * inv_freq[None, :]
            sin, cos = (jnp.sin(ang), jnp.cos(ang))
            base = (jnp.arange(0, D, 2, dtype=jnp.float32) + 0.4 * D) / (1.4 * D)
            scale = base[None, :] ** (pos[:, None] / SCALE_BASE)
            if downscale:
                scale = 1.0 / scale
            x1 = x[..., 0::2]
            x2 = x[..., 1::2]
            r1 = (x1 * cos - x2 * sin) * scale
            r2 = (x1 * sin + x2 * cos) * scale
            out = jnp.stack([r1, r2], axis=-1).reshape(B, S, D)
            return out

        def get_D(gamma, seq_len):
            n = jnp.arange(seq_len, dtype=jnp.float32)
            diff = n[:, None] - n[None, :]
            mask = diff >= 0
            D = jnp.where(mask, gamma ** jnp.where(mask, diff, 0.0), 0.0)
            return D

        def _reference_tuple_inner(x, W_Q, W_K, W_V):
            S = x.shape[1]
            D = get_D(GAMMA, S)
            Q = xpos_rope(x @ W_Q, downscale=False)
            K = xpos_rope(x @ W_K, downscale=True)
            V = x @ W_V
            ret = jnp.einsum('bnd,bmd->bnm', Q, K) * D[None, :, :]
            out = jnp.einsum('bnm,bmv->bnv', ret, V)
            return (out, ret)
        return _reference_tuple_inner(x, W_Q, W_K, W_V)[0]

    def _L0_ffn_ref(x, W_gat, att_src, att_dst, b_gat, ln_gamma, ln_beta, W1, b1, W2, b2, edge_index):
        import jax, jax.numpy as jnp
        import numpy as np
        B, N, D = (16, 1024, 64)
        NUM_EXPERTS, TOP_K, HEADS = (4, 2, 4)
        N_EDGES = 262144
        LN_EPS = 1e-05

        def _layernorm(x, g, b):
            mu = x.mean(-1, keepdims=True)
            var = ((x - mu) ** 2).mean(-1, keepdims=True)
            return (x - mu) * jax.lax.rsqrt(var + LN_EPS) * g + b

        def _forward(x, edge_index, W_gat, att_src, att_dst, b_gat, ln_gamma, ln_beta, W1, b1, W2, b2):
            Bc, Nc, Dc = x.shape
            M = Bc * Nc
            x_flat = x.reshape(M, Dc)
            h = (x_flat @ W_gat).reshape(M, HEADS, NUM_EXPERTS)
            loops = jnp.arange(M, dtype=edge_index.dtype)
            src = jnp.concatenate([edge_index[0], loops])
            dst = jnp.concatenate([edge_index[1], loops])
            a_src = (h * att_src).sum(-1)
            a_dst = (h * att_dst).sum(-1)
            e = jax.nn.leaky_relu(a_src[src] + a_dst[dst], negative_slope=0.2)
            e_max = jax.ops.segment_max(e, dst, num_segments=M)
            ee = jnp.exp(e - e_max[dst])
            denom = jax.ops.segment_sum(ee, dst, num_segments=M)
            alpha = ee / (denom[dst] + 1e-16)
            msg = h[src] * alpha[:, :, None]
            agg = jax.ops.segment_sum(msg, dst, num_segments=M).reshape(M, HEADS * NUM_EXPERTS) + b_gat
            scores = _layernorm(agg, ln_gamma, ln_beta).reshape(M, HEADS, NUM_EXPERTS).mean(1)
            scores = scores.reshape(Bc, Nc, NUM_EXPERTS)
            topk_s, topk_i = jax.lax.top_k(scores, TOP_K)
            w = jax.nn.softmax(topk_s, axis=-1)
            out = jnp.zeros_like(x)
            for ei in range(NUM_EXPERTS):
                g = jnp.where(topk_i == ei, w, 0.0).sum(-1)
                hh = jax.nn.gelu(x @ W1[ei] + b1[ei], approximate=False)
                out = out + g[..., None] * (hh @ W2[ei] + b2[ei])
            return out
        return _forward(x, edge_index, W_gat, att_src, att_dst, b_gat, ln_gamma, ln_beta, W1, b1, W2, b2)

    def _L1_attn_ref(x, ln1_g, ln1_b, w_qkv, w_out, b_out, res_w, ln2_g, ln2_b, w1, b1, w2, b2):
        import jax, jax.numpy as jnp
        import numpy as np
        H = 8
        M = 64
        PINV_ITERS = 6
        PAD = 16

        def layernorm(x, g, b, eps=1e-05):
            mu = x.mean(-1, keepdims=True)
            var = ((x - mu) ** 2).mean(-1, keepdims=True)
            return (x - mu) * jax.lax.rsqrt(var + eps) * g + b

        def moore_penrose_pinv(x, iters=PINV_ITERS):
            abs_x = jnp.abs(x)
            col = abs_x.sum(-1)
            row = abs_x.sum(-2)
            z = jnp.swapaxes(x, -1, -2) / (jnp.max(col) * jnp.max(row))
            eye = jnp.eye(x.shape[-1], dtype=x.dtype)
            for _ in range(iters):
                xz = x @ z
                z = 0.25 * z @ (13.0 * eye - xz @ (15.0 * eye - xz @ (7.0 * eye - xz)))
            return z

        def attn_block(y, ln1_g, ln1_b, w_qkv, w_out, b_out, res_w, ln2_g, ln2_b, w1, b1, w2, b2):
            B, N, D = y.shape
            inner = w_qkv.shape[1] // 3
            dh = inner // H
            xn = layernorm(y, ln1_g, ln1_b)
            qkv = xn @ w_qkv
            q, k, v = jnp.split(qkv, 3, axis=-1)
            to_heads = lambda t: t.reshape(B, N, H, dh).transpose(0, 2, 1, 3)
            q, k, v = map(to_heads, (q, k, v))
            q = q * dh ** (-0.5)
            l = N // M
            q_l = q.reshape(B, H, M, l, dh).mean(3)
            k_l = k.reshape(B, H, M, l, dh).mean(3)
            attn1 = jax.nn.softmax(jnp.einsum('bhnd,bhmd->bhnm', q, k_l), axis=-1)
            attn2 = jax.nn.softmax(jnp.einsum('bhid,bhjd->bhij', q_l, k_l), axis=-1)
            attn3 = jax.nn.softmax(jnp.einsum('bhmd,bhnd->bhmn', q_l, k), axis=-1)
            attn2_inv = moore_penrose_pinv(attn2)
            out = attn1 @ attn2_inv @ (attn3 @ v)
            res = jax.lax.conv_general_dilated(v, res_w, window_strides=(1, 1), padding=[(PAD, PAD), (0, 0)], dimension_numbers=('NCHW', 'OIHW', 'NCHW'), feature_group_count=H)
            out = out + res
            out = out.transpose(0, 2, 1, 3).reshape(B, N, inner)
            y = y + out @ w_out + b_out
            yn = layernorm(y, ln2_g, ln2_b)
            hdn = jax.nn.gelu(yn @ w1 + b1, approximate=False)
            return y + hdn @ w2 + b2
        y = x
        for i in range(ln1_g.shape[0]):
            y = attn_block(y, ln1_g[i], ln1_b[i], w_qkv[i], w_out[i], b_out[i], res_w[i], ln2_g[i], ln2_b[i], w1[i], b1[i], w2[i], b2[i])
        return y

    def _L1_ffn_ref(x, gate_w, gate_b, W1, b1, W2, b2):
        import jax, jax.numpy as jnp
        import numpy as np
        B, T, D, H, E = (16, 1024, 64, 128, 8)
        Bb, Tt, Dd = x.shape
        Ee = gate_w.shape[1]
        xf = x.reshape(-1, Dd)
        N = xf.shape[0]
        logits = xf @ gate_w + gate_b
        probs = jax.nn.softmax(logits, axis=-1)
        top2_vals, top2_idx = jax.lax.top_k(probs, 2)
        cw = jnp.zeros((N, Ee), dtype=xf.dtype).at[jnp.arange(N)[:, None], top2_idx].add(top2_vals)

        def step(acc, params):
            w1, bb1, w2, bb2, we = params
            h = jax.nn.gelu(xf @ w1 + bb1, approximate=False)
            y = h @ w2 + bb2
            return (acc + we[:, None] * y, None)
        out, _ = jax.lax.scan(step, jnp.zeros_like(xf), (W1, b1, W2, b2, cw.T))
        return out.reshape(Bb, Tt, Dd)
    h = _L0_tok_ref(x, L0_tok_ln_q_w, L0_tok_ln_q_b, L0_tok_Wq, L0_tok_ln_kv_w, L0_tok_ln_kv_b, L0_tok_Wkv, L0_tok_proj_w, L0_tok_proj_b, 4, 8)
    h = _layernorm(h + _L0_attn_ref(h, L0_attn_W_Q, L0_attn_W_K, L0_attn_W_V), axis=-1)
    h = _layernorm(h + _L0_ffn_ref(h, L0_ffn_W_gat, L0_ffn_att_src, L0_ffn_att_dst, L0_ffn_b_gat, L0_ffn_ln_gamma, L0_ffn_ln_beta, L0_ffn_W1, L0_ffn_b1, L0_ffn_W2, L0_ffn_b2, L0_ffn_edge_index), axis=-1)
    h = _layernorm(h + _L1_attn_ref(h, L1_attn_ln1_g, L1_attn_ln1_b, L1_attn_w_qkv, L1_attn_w_out, L1_attn_b_out, L1_attn_res_w, L1_attn_ln2_g, L1_attn_ln2_b, L1_attn_w1, L1_attn_b1, L1_attn_w2, L1_attn_b2), axis=-1)
    h = _layernorm(h + _L1_ffn_ref(h, L1_ffn_gate_w, L1_ffn_gate_b, L1_ffn_W1, L1_ffn_b1, L1_ffn_W2, L1_ffn_b2), axis=-1)
    return h

_drawn_inputs = setup_inputs


def setup_inputs(seed=0):
    import zlib

    import numpy as np

    out = dict(_drawn_inputs(seed))
    spreads = {'L0_tok_ln_q_w': (1.0, 0.6),
     'L0_tok_ln_q_b': (0.0, 0.8),
     'L0_tok_ln_kv_w': (1.0, 0.6),
     'L0_tok_ln_kv_b': (0.0, 0.637),
     'L0_tok_proj_b': (0.0, 0.1),
     'L0_ffn_b_gat': (0.0, 0.1),
     'L0_ffn_ln_gamma': (1.0, 0.2),
     'L0_ffn_ln_beta': (0.0, 0.368),
     'L0_ffn_b1': (0.0, 0.377),
     'L0_ffn_b2': (0.0, 0.1),
     'L1_attn_ln1_g': (1.0, 0.6),
     'L1_attn_ln1_b': (0.0, 0.8),
     'L1_attn_b_out': (0.0, 0.1),
     'L1_attn_ln2_g': (1.0, 0.6),
     'L1_attn_ln2_b': (0.0, 0.8),
     'L1_attn_b1': (0.0, 0.8),
     'L1_attn_b2': (0.0, 0.1),
     'L1_ffn_gate_b': (0.0, 0.58),
     'L1_ffn_b1': (0.0, 0.8),
     'L1_ffn_b2': (0.0, 0.364)}
    factors = {'L0_tok_Wq': 8.0,
     'L0_attn_W_Q': 8.0,
     'L0_attn_W_K': 7.326,
     'L0_attn_W_V': 7.871,
     'L0_ffn_att_src': 8.0,
     'L0_ffn_att_dst': 8.0,
     'L1_attn_w_qkv': 7.339,
     'L1_attn_w_out': 8.0,
     'L1_attn_res_w': 8.0,
     'L1_attn_w1': 4.299,
     'L1_attn_w2': 3.708,
     'L1_ffn_gate_w': 2.807,
     'L1_ffn_W1': 8.0,
     'L1_ffn_W2': 8.0}
    for name, (base, spread) in spreads.items():
        noise = np.random.default_rng([zlib.crc32(name.encode()), seed]).standard_normal(out[name].shape)
        drawn = base * np.exp(spread * noise) if base else spread * noise
        out[name] = jnp.asarray(drawn.astype(out[name].dtype))
    for name, factor in factors.items():
        out[name] = (out[name] * factor).astype(out[name].dtype)
    return out
```

```python
import concourse.bass as bass
from concourse import mybir
from contextlib import ExitStack
import numpy as np

F32 = mybir.dt.float32
I32 = mybir.dt.int32
ALU = mybir.AluOpType
ACT = mybir.ActivationFunctionType
AX = mybir.AxisListType

B, C, P = 128, 64, 256
T = B * P
N = 16
EPS = 1e-5


class Steps:

    def __init__(self, sem, names):
        self.sem, self.names, self.next = sem, names.split(), 0

    def did(self, ins, name):
        assert self.names[self.next % len(self.names)] == name, (name, self.names[self.next % len(self.names)])
        self.next += 1
        return ins.then_inc(self.sem, 1)

    def wait(self, eng, name, lane):
        if isinstance(lane, int) and lane < 0:
            return
        eng.wait_ge(self.sem, lane * len(self.names) + self.names.index(name) + 1)


class Loads:

    def __init__(self, sem, per=1):
        self.sem, self.per = sem, per

    def inc(self, ins):
        return ins.then_inc(self.sem, 16)

    def wait(self, eng, n):
        if isinstance(n, int) and n < 0:
            return
        eng.wait_ge(self.sem, (n + 1) * 16 * self.per)


def rounds(eng, count, body, sem):
    body(0)
    with eng.Fori(1, count) as i:
        body(i)
        eng.wait_ge(sem, 16)


class Core:

    def __init__(self, nc, phase):
        self.nc, self.phase, self.mem, self.held = nc, phase, ExitStack(), []

    def sb(self, name, shape, dt=F32):
        return self.mem.enter_context(self.nc.sbuf_tensor(f"{self.phase}__{name}", shape, dt))

    def ps(self, name, shape, dt=F32):
        return self.mem.enter_context(self.nc.psum_tensor(f"{self.phase}__{name}", shape, dt))

    def sem(self, name):
        self.held.append(self.nc.alloc_semaphore(f"{self.phase}__{name}"))
        return self.held[-1]

    def close(self):
        self.nc.clear_and_free_semaphores(self.held)
        self.nc.all_engine_barrier()
        self.mem.close()

    def steps(self, name, names):
        return Steps(self.sem(name), names)

    def flag(self, name):
        return Flag(self.sem(name))

    def loads(self, name, per=1):
        return Loads(self.sem(name), per)


class Flag:

    def __init__(self, sem):
        self.sem = sem

    def did(self, ins):
        return ins.then_inc(self.sem, 1)

    def wait(self, eng, lane):
        if isinstance(lane, int) and lane < 0:
            return
        eng.wait_ge(self.sem, lane + 1)


def pipeline(eng, lanes, G, stages, look=4, last=None):
    D = len(stages)
    peeled = -(-(D - 1 + look) // G)

    def slot(i, g):
        for d in reversed(range(D)):
            if stages[d] is None:
                continue
            gg, ii = (g - d) % G, i + (g - d) // G
            lane = ii * G + gg
            if isinstance(lane, int) and not 0 <= lane < lanes:
                continue
            stages[d](ii, gg, lane)

    full = lanes // G
    for s in range(peeled * G):
        slot(s // G, s % G)
    with eng.Fori(peeled, full) as i:
        for g in range(G):
            slot(i, g)
        if last is not None:
            last()
    for s in range(full * G, lanes + D - 1):
        slot(s // G, s % G)


def tokenizer(nc, a, h_out):
    c = Core(nc, "tok")
    PAIRS, G = B // 2, 4
    R = PAIRS * 2 // G
    x = [c.sb(f"x{k}", [128, N, P]) for k in range(2)]
    x2 = c.sb("x2", [128, N, 128])
    half = c.sb("half", [128, 2048])
    feat = c.sb("feat", [128, P])
    prod = c.sb("prod", [128, N, 2, C])
    v = [c.sb(f"v{k}", [128, N, 2, C]) for k in range(2)]
    pv = c.sb("pv", [128, N, 2, C])
    r = [c.sb(f"r{k}", [128, 2, C]) for k in range(2)]
    q = c.sb("q", [128, 2, C])
    st = c.sb("st", [128, 2, 6])
    mv = c.sb("mv", [128, 2, 2])
    spare = c.sb("spare", [128, 1])
    qv = c.sb("qv", [128, 2])
    qrs = c.sb("qrs", [128, 2])
    m2 = c.sb("m2", [128, 32])
    var = c.sb("var", [128, 32])
    rstd = c.sb("rstd", [128, 32])
    lg = c.sb("lg", [128, N, 2, 8])
    ex = c.sb("ex", [128, N, 2, 8])
    w = c.sb("w", [128, N, 2, 8])
    mx = c.sb("mx", [128, 16])
    sm = c.sb("sm", [128, 16])
    rs = c.sb("rs", [128, 2, 16])
    agg = c.sb("agg", [128, 2, C])
    aggT = c.sb("aggT", [128, 128])
    h = [c.sb(f"h{k}", [128, 2, C]) for k in range(2)]
    mh = c.sb("mh", [128, 32])
    ident = c.sb("ident", [128, 128])
    avg = c.sb("avg", [128, 128])
    avg2 = c.sb("avg2", [128, 2])
    kvw = c.sb("kvw", [128, 2, 128])
    qrw = c.sb("qrw", [128, 2, 2, C])
    prj = c.sb("prj", [128, 2, C])
    wvec = c.sb("wvec", [128, 4])
    lhs = c.sb("lhs", [128, 128])
    wv_t = c.sb("wv_t", [C, C])
    cvl = c.sb("cvl", [C, 128])
    wq_t = c.sb("wq_t", [C, C])
    cq = c.sb("cq", [128, C])
    cout = c.sb("cout", [128, C])

    pkv = c.ps("pkv", [128, 2, 4, 2, 128])
    pq = c.ps("pq", [128, 512])
    pst = c.ps("pst", [128, 512])
    pt = c.ps("pt", [128, 512])

    mh_set = c.sem("mh_set")
    w_in, zeroed, prep, prep_pe = c.sem("w_in"), c.sem("zeroed"), c.sem("prep"), c.sem("prep_pe")
    x_in = [c.loads(f"x_in{k}") for k in range(2)]
    h_st = [c.loads(f"h_st{k}") for k in range(2)]
    pe_a = c.steps("pe_a", "q stats kv0 kv1 kv2 kv3")
    pe_t = c.steps("pe_t", "aggT proj")
    act_a = c.steps("act_a", "x2 r m2 v0 v1 v2 v3 exp")
    act_t = c.steps("act_t", "aggT")
    dve_a = c.steps("dve_a", "st0 st1 mv0 mv1 qv var qm q p0 p1 p2 p3 lg lgs mx lgm sum w")
    dve_v = c.steps("dve_v", "red rs agg")
    dve_t = c.steps("dve_t", "add h")
    pool_f = c.steps("pool_f", "h0 h1 h2 feat")
    pool_a = c.steps("pool_a", "qrs rstd")
    pool_v = c.steps("pool_v", "pv")
    NW = 14

    def first_lane(i, g):
        return isinstance(i, int) and i == 0 and g == 0

    def before(i, g):
        return (i, g - 1) if g else (i - 1, G - 1)

    h_pairs = h_out.rearrange("(u b) (k p) c -> u p k b c", b=2, k=2)

    with nc.Block() as block:
        @block.sync
        def _(sp):
            sp.wait_ge(zeroed, 3)
            for k in range(2):
                s = slice(64 * k, 64 * k + 64)
                sp.dma_start(kvw[s, k, :], a["wkv_t"]).then_inc(w_in, 16)
                sp.dma_start(qrw[s, 0, k, :], a["eye16"]).then_inc(w_in, 16)
                sp.dma_start(qrw[s, 1, k, :], a["wq_t"]).then_inc(w_in, 16)
                sp.dma_start(prj[s, k, :], a["proj_t"]).then_inc(w_in, 16)
            sp.dma_start(wvec[:], a["tok_ln"]).then_inc(w_in, 16)
            sp.dma_start(ident[:], a["eye"]).then_inc(w_in, 16)
            sp.dma_start(avg[:], a["avg"]).then_inc(w_in, 16)
            sp.dma_start(wq_t[:], a["wq_t"]).then_inc(w_in, 16)
            sp.dma_start(wv_t[:], a["wkv_t"][:, 64:128]).then_inc(w_in, 16)
            sp.dma_start(cout[:], a["proj_b"].partition_broadcast(128)).then_inc(w_in, 16)

            def body(i):
                for k in range(2):
                    L = i * G + 2 * k
                    for d in (L - 4, L - 3):
                        pe_a.wait(sp, "kv3", d)
                        act_a.wait(sp, "x2", d)
                    pool_f.wait(sp, "feat", i * 2 + k - 2)
                    x_in[k].inc(sp.dma_start(x[k][:].rearrange("p n q -> p (n q)"), a["x"][2 * i + k]))
            rounds(sp, R, body, w_in)

        @block.gpsimd
        def _(pool):
            pool.memset(mh[:], -0.5).then_inc(mh_set, 1)
            pool.wait_ge(mh_set, 1)

            def feats(i, k):
                xk, F = x[k][:].rearrange("p n q -> p (n q)"), i * 2 + k
                x_in[k].wait(pool, i)
                pool_f.did(pool.tensor_tensor(half[:], xk[:, 0:2048], xk[:, 2048:4096], ALU.add), "h0")
                pool_f.wait(pool, "h0", F)
                pool_f.did(pool.tensor_tensor(half[:, 0:1024], half[:, 0:1024], half[:, 1024:2048], ALU.add), "h1")
                pool_f.wait(pool, "h1", F)
                pool_f.did(pool.tensor_tensor(half[:, 0:512], half[:, 0:512], half[:, 512:1024], ALU.add), "h2")
                pool_f.wait(pool, "h2", F)
                pe_a.wait(pool, "q", i * G + 2 * k - 1)
                pool_f.did(pool.tensor_tensor(feat[:], half[:, 0:256], half[:, 256:512], ALU.add), "feat")

            def norms(L):
                dve_a.wait(pool, "qv", L)
                pool_a.did(pool.tensor_tensor(qrs[:], qv[:], mh[:, 0:2], ALU.pow), "qrs")
                dve_a.wait(pool, "var", L)
                pool_v.wait(pool, "pv", L - 1)
                pool_a.did(pool.tensor_tensor(rstd[:], var[:], mh[:], ALU.pow), "rstd")

            def weigh(L, g):
                dve_a.wait(pool, "w", L)
                act_a.wait(pool, "v3", L)
                dve_v.wait(pool, "red", L - 1)
                pool_v.did(pool.tensor_tensor(
                    pv[:].rearrange("p n b (h d) -> p (n b h) d", d=8),
                    v[g % 2][:].rearrange("p n b (h d) -> p (n b h) d", d=8),
                    w[:].rearrange("p n b h -> p (n b h)").unsqueeze(2).to_broadcast([128, 256, 8]),
                    ALU.mult), "pv")

            def body(i):
                for g in range(G):
                    L = i * G + g
                    if g % 2 == 0:
                        feats(i, g // 2)
                    norms(L)
                    weigh(L, g)
            rounds(pool, R, body, w_in)

        @block.scalar
        def _(act):
            act.wait_ge(prep, 9)

            def front(i, g):
                L = i * G + g
                x_in[g // 2].wait(act, i)
                pe_a.wait(act, "stats", L - 1)
                s = slice(128 * (g % 2), 128 * (g % 2) + 128)
                act_a.did(act.activation(x2[:], x[g // 2][:, :, s], ACT.Square), "x2")
                pe_a.wait(act, "q", L)
                dve_t.wait(act, "add", L - 2)
                act_a.did(act.activation(r[g % 2][:].rearrange("p b c -> p (b c)"), pq[:, 0:128], ACT.Copy), "r")
                pe_a.wait(act, "stats", L)
                dve_a.wait(act, "var", L - 1)
                act_a.did(act.activation(m2[:], pst[:, 0:32], ACT.Square), "m2")
                pool_v.wait(act, "pv", L - 2)
                for j in range(4):
                    pe_a.wait(act, f"kv{j}", L)
                    act_a.did(act.activation(v[g % 2][:, 4 * j:4 * j + 4], pkv[:, j % 2, :, :, 64:128], ACT.Copy),
                              f"v{j}")
                dve_a.wait(act, "lgm", L)
                act_a.did(act.activation(ex[:].rearrange("p n b h -> p (n b h)"),
                                         lg[:].rearrange("p n b h -> p (n b h)"), ACT.Exp), "exp")

            def tail(i, g):
                L, k = i * G + g, g % 2
                pe_t.wait(act, "aggT", L)
                act_t.did(act.activation(aggT[:], pt[:, 0:128], ACT.Copy), "aggT")
                dve_t.wait(act, "h", L)
                h_st[k].inc(act.dma_start(h_pairs[2 * i + g // 2, :, k], h[k][:]))

            def body(i):
                for g in range(G):
                    front(i, g)
                    if not first_lane(i, g):
                        tail(*before(i, g))
            rounds(act, R, body, w_in)
            tail(R - 1, G - 1)
            for k in range(2):
                h_st[k].wait(act, R * G // 2 - 1)

        @block.vector
        def _(dve):
            dve.memset(kvw[:], 0.0).then_inc(zeroed, 1)
            dve.memset(qrw[:], 0.0).then_inc(zeroed, 1)
            dve.memset(prj[:], 0.0).then_inc(zeroed, 1)
            dve.wait_ge(w_in, 16 * NW)
            dve.tensor_scalar(kvw[:], kvw[:], wvec[:, 0:1], None, ALU.mult).then_inc(prep, 1)
            dve.tensor_scalar(qrw[:, 1], qrw[:, 1], wvec[:, 1:2], 1 / 128, ALU.mult, ALU.mult).then_inc(prep, 1)
            dve.tensor_copy(avg2[:, 0:1], avg[:, 0:1]).then_inc(prep, 1)
            dve.tensor_copy(avg2[:, 1:2], avg[:, 64:65]).then_inc(prep, 1)
            dve.tensor_copy(lhs[0:64, :], wvec[0:64, 3:4].to_broadcast([64, 128])).then_inc(prep, 1)
            dve.wait_ge(prep_pe, 4)
            dve.tensor_tensor(kvw[:].rearrange("p b n -> p (b n)"), kvw[:].rearrange("p b n -> p (b n)"),
                              pkv[:, 0, 0].rearrange("p b n -> p (b n)"), ALU.subtract).then_inc(prep, 1)
            dve.tensor_tensor(qrw[:, 1].rearrange("p b n -> p (b n)"), qrw[:, 1].rearrange("p b n -> p (b n)"),
                              pst[:, 0:128], ALU.subtract).then_inc(prep, 1)
            dve.tensor_scalar(cq[:], pq[:, 0:64], 0.125, None, ALU.mult).then_inc(prep, 1)
            dve.tensor_copy(cvl[:], pt[0:64, 0:1].to_broadcast([64, 128])).then_inc(prep, 1)
            dve.wait_ge(prep_pe, 5)
            dve.tensor_tensor(cout[:], cout[:], pq[:, 0:64], ALU.add).then_inc(prep, 1)

            def front(L, g):
                act_a.wait(dve, "r", L)
                for b in range(2):
                    dve_a.did(dve.bn_stats(st[:, b, :], r[g % 2][:, b, :]), f"st{b}")
                dve_a.wait(dve, "st1", L)
                dve.memset(spare[:], 0.0)
                for b in range(2):
                    dve_a.did(dve.bn_aggr(mv[:, b, :], st[:, b, :]), f"mv{b}")
                dve_a.wait(dve, "mv1", L)
                dve_a.did(dve.tensor_scalar(qv[:], mv[:, :, 1], EPS, None, ALU.add), "qv")
                act_a.wait(dve, "m2", L)
                pool_a.wait(dve, "rstd", L - 1)
                dve_a.did(dve.scalar_tensor_tensor(var[:], pst[:, 32:64], EPS, m2[:], ALU.add, ALU.subtract), "var")
                pool_a.wait(dve, "qrs", L)
                dve_a.did(dve.tensor_tensor(q[:], pq[:, 128:256].rearrange("p (b c) -> p b c", b=2),
                                            qrs[:].unsqueeze(2).to_broadcast([128, 2, C]), ALU.mult), "qm")
                dve_a.wait(dve, "qm", L)
                dve_a.did(dve.tensor_tensor(q[:], q[:], cq[:].unsqueeze(1).to_broadcast([128, 2, C]), ALU.add), "q")
                dve_a.wait(dve, "q", L)
                for j in range(4):
                    act_a.wait(dve, f"v{j}", L)
                    dve_a.did(dve.tensor_tensor(prod[:, 4 * j:4 * j + 4], pkv[:, j % 2, :, :, 0:64],
                                                q[:].unsqueeze(1).to_broadcast([128, 4, 2, C]), ALU.mult), f"p{j}")
                dve_a.wait(dve, "p3", L)
                dve_a.did(dve.tensor_reduce(lg[:].rearrange("p n b h -> p (n b h)"),
                                            prod[:].rearrange("p n b (h d) -> p (n b h) d", d=8),
                                            AX.X, ALU.add), "lg")

            def softmax(L):
                rst = rstd[:].unsqueeze(2).to_broadcast([128, 32, 8])
                over_n = lambda t: t[:].rearrange("p n b h -> p (b h) n")
                flat = lambda t: t[:].rearrange("p n b h -> p (n b) h")
                pool_a.wait(dve, "rstd", L)
                dve_a.wait(dve, "lg", L)
                dve_a.did(dve.tensor_tensor(flat(lg), flat(lg), rst, ALU.mult), "lgs")
                dve_a.wait(dve, "lgs", L)
                dve_a.did(dve.tensor_reduce(mx[:], over_n(lg), AX.X, ALU.max), "mx")
                dve_a.wait(dve, "mx", L)
                dve_a.did(dve.tensor_tensor(lg[:].rearrange("p n b h -> p n (b h)"),
                                            lg[:].rearrange("p n b h -> p n (b h)"),
                                            mx[:].unsqueeze(1).to_broadcast([128, N, 16]), ALU.subtract), "lgm")
                act_a.wait(dve, "exp", L)
                dve_a.did(dve.tensor_reduce(sm[:], over_n(ex), AX.X, ALU.add), "sum")
                pool_v.wait(dve, "pv", L - 1)
                dve_a.did(dve.tensor_tensor(flat(w), flat(ex), rst, ALU.mult), "w")

            def gather(L, g):
                pool_v.wait(dve, "pv", L)
                dve_a.wait(dve, "sum", L)
                pe_t.wait(dve, "aggT", L - 1)
                dve_v.did(dve.tensor_reduce(agg[:].rearrange("p b c -> p (b c)"),
                                            pv[:].rearrange("p n b c -> p (b c) n"), AX.X, ALU.add), "red")
                dve_v.did(dve.reciprocal(rs[:, g % 2], sm[:]), "rs")
                dve_v.wait(dve, "rs", L)
                dve_v.did(dve.tensor_tensor(agg[:].rearrange("p b (h d) -> p (b h) d", d=8),
                                            agg[:].rearrange("p b (h d) -> p (b h) d", d=8),
                                            rs[:, g % 2].unsqueeze(2).to_broadcast([128, 16, 8]), ALU.mult), "agg")

            def tail(i, g):
                L, k = i * G + g, g % 2
                pe_t.wait(dve, "proj", L)
                act_a.wait(dve, "r", L)
                h_st[k].wait(dve, 2 * i + g // 2 - 1)
                dve_t.did(dve.tensor_tensor(h[k][:].rearrange("p b c -> p (b c)"), pt[:, 128:256],
                                            r[k][:].rearrange("p b c -> p (b c)"), ALU.add), "add")
                dve_t.wait(dve, "add", L)
                dve_t.did(dve.tensor_tensor(h[k][:], h[k][:], cout[:].unsqueeze(1).to_broadcast([128, 2, C]),
                                            ALU.add), "h")

            def body(i):
                for g in range(G):
                    L = i * G + g
                    front(L, g)
                    if not first_lane(i, g):
                        gather(L - 1, (g - 1) % G)
                    softmax(L)
                    if not first_lane(i, g):
                        tail(*before(i, g))
            rounds(dve, R, body, w_in)
            gather(R * G - 1, G - 1)
            tail(R - 1, G - 1)

        @block.tensor
        def _(pe):
            pe.wait_ge(prep, 5)
            pe.matmul(pkv[:, 0, 0].rearrange("p b n -> p (b n)"), avg[:], kvw[:].rearrange("p b n -> p (b n)"),
                      start=True, stop=True).then_inc(prep_pe, 1)
            pe.matmul(pst[:, 0:128], avg[:], qrw[:, 1].rearrange("p b n -> p (b n)"), start=True, stop=True)\
              .then_inc(prep_pe, 1)
            pe.matmul(pq[:, 0:64], lhs[0:64, :], wq_t[:], start=True, stop=True).then_inc(prep_pe, 1)
            pe.matmul(pt[0:64, 0:1], wv_t[:], wvec[0:64, 2:3], start=True, stop=True).then_inc(prep_pe, 1)
            pe.wait_ge(prep, 9)
            pe.matmul(pq[:, 0:64], cvl[:], prj[0:64, 0, :], start=True, stop=True).then_inc(prep_pe, 1)
            pe.wait_ge(prep, 10)

            def front(i, g):
                L, s, xg = i * G + g, slice(128 * (g % 2), 128 * (g % 2) + 128), x[g // 2]
                x_in[g // 2].wait(pe, i)
                pool_f.wait(pe, "feat", i * 2 + g // 2)
                act_a.wait(pe, "r", L - 1)
                dve_a.wait(pe, "qm", L - 1)
                pe_a.did(pe.matmul(pq[:, 0:256], feat[:, s], qrw[:].rearrange("p t b n -> p (t b n)"),
                                   start=True, stop=True), "q")
                act_a.wait(pe, "x2", L)
                act_a.wait(pe, "m2", L - 1)
                dve_a.wait(pe, "var", L - 1)
                for n in range(N):
                    pe.matmul(pst[:, 2 * n:2 * n + 2], xg[:, n, s], avg2[:], start=True, stop=True)
                for n in range(N):
                    mm = pe.matmul(pst[:, 32 + 2 * n:34 + 2 * n], x2[:, n, :], avg2[:], start=True, stop=True)
                pe_a.did(mm, "stats")
                for j in range(4):
                    P_, Lp = (L, j - 2) if j >= 2 else (L - 1, j + 2)
                    act_a.wait(pe, f"v{Lp}", P_)
                    dve_a.wait(pe, f"p{Lp}", P_)
                    for n in range(4):
                        mm = pe.matmul(pkv[:, j % 2, n].rearrange("p b n -> p (b n)"), xg[:, 4 * j + n, s],
                                       kvw[:].rearrange("p b n -> p (b n)"), start=True, stop=True)
                    pe_a.did(mm, f"kv{j}")

            def tail(L):
                dve_v.wait(pe, "agg", L)
                dve_t.wait(pe, "add", L - 1)
                pe_t.did(pe.transpose(pt[:, 0:128], agg[:].rearrange("p b c -> p (b c)"), ident[:]), "aggT")
                act_t.wait(pe, "aggT", L)
                pe_t.did(pe.matmul(pt[:, 128:256], aggT[:], prj[:].rearrange("p b n -> p (b n)"),
                                   start=True, stop=True), "proj")

            def body(i):
                for g in range(G):
                    front(i, g)
                    if not first_lane(i, g):
                        tail(i * G + g - 1)
            rounds(pe, R, body, w_in)
            tail(R * G - 1)
    c.close()


def retention(nc, a, h_in, h_out, gat_out, dst_out, top_out):
    c = Core(nc, "ret")
    G = 4
    h = [c.sb(f"h{k}", [128, 2, C]) for k in range(G)]
    hT = [c.sb(f"hT{k}", [128, 128]) for k in range(2)]
    ca = c.sb("ca", [128, P])
    sa = c.sb("sa", [128, P])
    qt = [c.sb(f"qt{k}", [C, P]) for k in range(2)]
    kt = [c.sb(f"kt{k}", [C, P]) for k in range(2)]
    v = [c.sb(f"v{k}", [128, 2, C]) for k in range(G)]
    ret = [c.sb(f"ret{k}", [128, 384]) for k in range(2)]
    s = [c.sb(f"s{k}", [128, 2, C]) for k in range(2)]
    st = c.sb("st", [128, 2, 6])
    mv = [c.sb(f"mv{k}", [128, 2, 2]) for k in range(2)]
    ve = c.sb("ve", [128, 2])
    rstd = [c.sb(f"rstd{k}", [128, 2]) for k in range(2)]
    y = [c.sb(f"y{k}", [128, 2, C]) for k in range(G)]
    yT = [c.sb(f"yT{k}", [128, 128]) for k in range(2)]
    gt = [c.sb(f"gt{k}", [128, 2, 24]) for k in range(G)]
    top = c.sb("top", [128, 4])
    pair = c.sb("pair", [128, 4])
    mh = c.sb("mh", [128, 2])
    spare = c.sb("spare", [128, 1])
    ident = c.sb("ident", [128, 128])
    wqk = c.sb("wqk", [128, 2, 128])
    wv = c.sb("wv", [128, C])
    cosT = c.sb("cosT", [128, P])
    sinT = c.sb("sinT", [128, P])
    decay = c.sb("decay", [128, 384])
    wg = c.sb("wg", [128, 24])
    att = c.sb("att", [128, 2, 16])
    wa = c.sb("wa", [128, 2, 16])

    phT = c.ps("phT", [128, 512])
    pqk = c.ps("pqk", [128, 2, 512])
    pr = c.ps("pr", [128, 512])
    po = c.ps("po", [128, 512])
    pyT = c.ps("pyT", [128, 512])
    pg = c.ps("pg", [128, 2, 512])

    w_in, prep, mh_set = c.sem("w_in"), c.sem("prep"), c.sem("mh_set")
    h_ld = [c.loads(f"h_ld{k}") for k in range(G)]
    st_h = [c.loads(f"st_h{k}") for k in range(G)]
    st_g = [c.loads(f"st_g{k}", 2) for k in range(G)]
    hT_p, hT_s = c.flag("hT_p"), c.flag("hT_s")
    qkv_p, rope = c.flag("qkv_p"), c.steps("rope", "ca sa v qt kt")
    ret_p, ret_s, out_p = c.flag("ret_p"), c.flag("ret_s"), c.flag("out_p")
    norm, rs_s, y_s = c.steps("norm", "s st0 st1 mv0 mv1 ve"), c.flag("rs_s"), c.steps("y_s", "y0 y1")
    yT_p, yT_s, g_p, g_s = c.flag("yT_p"), c.flag("yT_s"), c.flag("g_p"), c.steps("g_s", "gt pair top")
    h_view = h_in.rearrange("b (k p) c -> b p k c", p=128)
    ho_view = h_out.rearrange("b (k p) c -> b p k c", p=128)
    go_view = gat_out.rearrange("(b k p) c -> b p k c", p=128, k=2)
    do_view = dst_out.rearrange("(b k p) c -> b p k c", p=128, k=2)
    NW = 12

    with nc.Block() as block:
        @block.sync
        def _(sp):
            for dst, src in ((ident, "eye"), (cosT, "cosT"), (sinT, "sinT"),
                             (decay, "decay")):
                sp.dma_start(dst[:], a[src]).then_inc(w_in, 16)
            for k in range(2):
                half = slice(64 * k, 64 * k + 64)
                sp.dma_start(wqk[half], a["wqk"]).then_inc(w_in, 16)
                sp.dma_start(wv[half], a["wv"]).then_inc(w_in, 16)
                sp.dma_start(wg[half, 0:16], a["w_gat"]).then_inc(w_in, 16)
            sp.dma_start(att[:, 0, :], a["att_src"].partition_broadcast(128)).then_inc(w_in, 16)
            sp.dma_start(att[:, 1, :], a["att_dst"].partition_broadcast(128)).then_inc(w_in, 16)

            def load(i, g, L):
                norm.wait(sp, "s", L - G)
                h_ld[g].inc(sp.dma_start(h[g][:], h_view[L]))

            def store(i, g, L):
                y_s.wait(sp, "y1", L)
                st_h[g].inc(sp.dma_start(ho_view[L], y[g][:]))
                g_s.wait(sp, "top", L)
                st_g[g].inc(sp.dma_start(go_view[L], gt[g][:, :, 0:20]))
                st_g[g].inc(sp.dma_start(do_view[L], gt[g][:, :, 20:24]))
            pipeline(sp, B, G, [load, None, None, None, None, None, store])
            for g in range(G):
                st_h[g].wait(sp, B // G - 1)
                st_g[g].wait(sp, B // G - 1)
            sp.dma_start(top_out, top[:]).then_inc(w_in, 16)
            sp.wait_ge(w_in, 16 * NW + 16)

        @block.tensor
        def _(pe):
            pe.wait_ge(w_in, 16 * NW)
            pe.wait_ge(prep, 3)

            def tr(i, g, L):
                h_ld[g].wait(pe, i)
                hT_s.wait(pe, L - 1)
                hT_p.did(pe.transpose(phT[:, 0:128], h[g][:].rearrange("p k c -> p (k c)"), ident[:]))

            def qkv(i, g, L):
                hT_s.wait(pe, L)
                rope.wait(pe, "v", L - 1)
                for k in range(2):
                    half = slice(64 * k, 64 * k + 64)
                    for t in range(2):
                        pe.matmul(pqk[:, k, 128 * t:128 * t + 128], wqk[half, t, :], hT[g % 2][half, :],
                                  start=True, stop=True)
                    mm = pe.matmul(pqk[:, k, 256:320], hT[g % 2][half, :], wv[half, :], start=True, stop=True)
                    qkv_p.did(mm)

            def scores(i, g, L):
                rope.wait(pe, "kt", L)
                ret_s.wait(pe, L - 1)
                pe.matmul(pr[:, 0:256], kt[g % 2][:, 0:128], qt[g % 2][:], start=True, stop=True)
                ret_p.did(pe.matmul(pr[:, 256:384], kt[g % 2][:, 128:256], qt[g % 2][:, 128:256],
                                    start=True, stop=True))

            def out(i, g, L):
                ret_s.wait(pe, L)
                norm.wait(pe, "s", L - 1)
                r = ret[g % 2]
                pe.matmul(po[:, 0:64], r[:, 0:128], v[g][:, 0, :], start=True, stop=True)
                pe.matmul(po[:, 64:128], r[:, 128:256], v[g][:, 0, :], start=True, stop=False)
                out_p.did(pe.matmul(po[:, 64:128], r[:, 256:384], v[g][:, 1, :], start=False, stop=True))

            def tr_y(i, g, L):
                y_s.wait(pe, "y1", L)
                yT_s.wait(pe, L - 1)
                yT_p.did(pe.transpose(pyT[:, 0:128], y[g][:].rearrange("p k c -> p (k c)"), ident[:]))

            def gat(i, g, L):
                yT_s.wait(pe, L)
                g_s.wait(pe, "top", L - 1)
                for k in range(2):
                    mm = pe.matmul(pg[:, k, 0:24], yT[g % 2][64 * k:64 * k + 64, :], wg[64 * k:64 * k + 64, :],
                                   start=True, stop=True)
                    g_p.did(mm)
            pipeline(pe, B, G, [tr, qkv, scores, out, tr_y, gat])

        @block.scalar
        def _(act):
            def copy_hT(i, g, L):
                hT_p.wait(act, L)
                qkv_p.wait(act, 2 * (L - 2) + 1)
                hT_s.did(act.activation(hT[g % 2][:], phT[:, 0:128], ACT.Copy))

            def copy_yT(i, g, L):
                yT_p.wait(act, L)
                g_p.wait(act, 2 * (L - 2) + 1)
                yT_s.did(act.activation(yT[g % 2][:], pyT[:, 0:128], ACT.Copy))
            pipeline(act, B, G, [copy_hT, None, None, None, copy_yT])

        @block.gpsimd
        def _(pool):
            pool.memset(mh[:], -0.5).then_inc(mh_set, 1)
            pool.wait_ge(mh_set, 1)

            def rs(i, g, L):
                norm.wait(pool, "ve", L)
                y_s.wait(pool, "y1", L - 2)
                rs_s.did(pool.tensor_tensor(rstd[g % 2][:], ve[:], mh[:], ALU.pow))
            pipeline(pool, B, G, [None, None, None, rs])

        @block.vector
        def _(dve):
            dve.wait_ge(w_in, 16 * NW)
            dve.tensor_tensor(wa[:], wg[:, 0:16].unsqueeze(1).to_broadcast([128, 2, 16]), att[:], ALU.mult)\
               .then_inc(prep, 1)
            dve.wait_ge(prep, 1)
            dve.tensor_reduce(wg[:, 16:24], wa[:].rearrange("p t (h e) -> p (t h) e", e=4), AX.X, ALU.add)\
               .then_inc(prep, 1)
            dve.memset(top[:], -3.0e38).then_inc(prep, 1)
            dve.wait_ge(prep, 3)

            halves = lambda t: t[:].rearrange("p (k q) -> p k q", k=2)

            def ropes(i, g, L):
                qkv_p.wait(dve, 2 * L + 1)
                rope.wait(dve, "kt", L - 1)
                rope.did(dve.tensor_tensor(halves(ca), pqk[:, :, 0:128], halves(cosT), ALU.mult), "ca")
                rope.did(dve.tensor_tensor(halves(sa), pqk[:, :, 128:256], halves(sinT), ALU.mult), "sa")
                out_p.wait(dve, L - G)
                rope.did(dve.tensor_copy(v[g][:], pqk[:, :, 256:320]), "v")
                rope.wait(dve, "sa", L)
                ret_p.wait(dve, L - 2)
                rope.did(dve.tensor_tensor(qt[g % 2][:], ca[0:64, :], sa[0:64, :], ALU.add), "qt")
                rope.did(dve.tensor_tensor(kt[g % 2][:], ca[64:128, :], sa[64:128, :], ALU.add), "kt")

            def decays(i, g, L):
                ret_p.wait(dve, L)
                out_p.wait(dve, L - 2)
                ret_s.did(dve.tensor_tensor(ret[g % 2][:], pr[:, 0:384], decay[:], ALU.mult))

            def stats(i, g, L):
                out_p.wait(dve, L)
                y_s.wait(dve, "y1", L - 2)
                norm.did(dve.tensor_tensor(s[g % 2][:].rearrange("p k c -> p (k c)"), po[:, 0:128],
                                           h[g][:].rearrange("p k c -> p (k c)"), ALU.add), "s")
                norm.wait(dve, "s", L)
                for k in range(2):
                    norm.did(dve.bn_stats(st[:, k, :], s[g % 2][:, k, :]), f"st{k}")
                norm.wait(dve, "st1", L)
                dve.memset(spare[:], 0.0)
                for k in range(2):
                    norm.did(dve.bn_aggr(mv[g % 2][:, k, :], st[:, k, :]), f"mv{k}")
                norm.wait(dve, "mv1", L)
                rs_s.wait(dve, L - 1)
                norm.did(dve.tensor_scalar(ve[:], mv[g % 2][:, :, 1], EPS, None, ALU.add), "ve")

            def finish(i, g, L):
                rs_s.wait(dve, L)
                st_h[g].wait(dve, i - 1)
                yT_p.wait(dve, L - G)
                for k in range(2):
                    y_s.did(dve.tensor_scalar(y[g][:, k, :], s[g % 2][:, k, :], mv[g % 2][:, k, 0:1],
                                              rstd[g % 2][:, k:k + 1], ALU.subtract, ALU.mult), f"y{k}")

            def gats(i, g, L):
                g_p.wait(dve, 2 * L + 1)
                st_g[g].wait(dve, i - 1)
                g_s.did(dve.tensor_copy(gt[g][:], pg[:, :, 0:24]), "gt")
                g_s.wait(dve, "gt", L)
                g_s.did(dve.tensor_tensor(pair[:], gt[g][:, 0, 16:20], gt[g][:, 1, 16:20], ALU.max), "pair")
                g_s.wait(dve, "pair", L)
                g_s.did(dve.tensor_tensor(top[:], top[:], pair[:], ALU.max), "top")
            pipeline(dve, B, G, [None, ropes, decays, stats, finish, gats])
    c.close()


TABLES = 4
ROWS = T + 128
CH = 16


def edges(nc, a, src_idx, dst_idx, gat, dst_rows, top, tables):
    c = Core(nc, "edge")
    G, E = 2, src_idx.shape[0] * src_idx.shape[1] * src_idx.shape[2]
    LANES = E // (128 * CH)
    si = [c.sb(f"si{k}", [128, CH], I32) for k in range(G)]
    di = [c.sb(f"di{k}", [128, CH], I32) for k in range(G)]
    df = [c.sb(f"df{k}", [128, CH]) for k in range(G)]
    gs = [c.sb(f"gs{k}", [128, CH, 20]) for k in range(G)]
    gd = [c.sb(f"gd{k}", [128, CH, 4]) for k in range(G)]
    eq = [c.sb(f"eq{k}", [128, CH, 128]) for k in range(G)]
    low = c.sb("low", [128, 4, 128])
    eql = c.sb("eql", [128, 4, 128])
    cnt = c.sb("cnt", [128, CH])
    first = c.sb("first", [128, CH])
    tgt = c.sb("tgt", [128, CH])
    ti = [c.sb(f"ti{k}", [128, CH], I32) for k in range(G)]
    z = c.sb("z", [128, CH, 4])
    mz = c.sb("mz", [128, CH, 4])
    ml = c.sb("ml", [128, CH, 4])
    pay = [c.sb(f"pay{k}", [128, CH, 20]) for k in range(G)]
    comb = [c.sb(f"comb{k}", [128, CH, 20]) for k in range(G)]
    ident = c.sb("ident", [128, 128])
    spare_row = c.sb("spare_row", [128, 1])
    tops = c.sb("tops", [128, 128, 4])
    big = c.sb("big", [128, 4])
    zero = c.sb("zero", [128, ROWS * 20 // 128])
    pd = [c.ps(f"pd{k}", [128, 4, 128]) for k in range(2)]
    pc = [c.ps(f"pc{k}", [128, CH, 20]) for k in range(2)]

    turn = c.sem("turn")
    w_in, w_ok, zeroed = c.sem("w_in"), c.sem("w_ok"), c.sem("zeroed")
    idx_in = [c.loads(f"idx_in{k}", 2) for k in range(G)]
    src_in = [c.loads(f"src_in{k}", CH) for k in range(G)]
    dst_in = [c.loads(f"dst_in{k}", CH) for k in range(G)]
    added = [c.loads(f"added{k}") for k in range(TABLES)]
    df_s, pd_p, eqs = c.flag("df_s"), c.flag("pd_p"), c.steps("eqs", " ".join(f"eq{q} el{q} cn{q}" for q in range(4)))
    rows = c.steps("rows", "first d m t i")
    lgt = c.steps("lgt", "z l mz ml sub")
    exp_s, pay_s, pc_p, comb_s = c.flag("exp_s"), c.flag("pay_s"), c.flag("pc_p"), c.flag("comb_s")

    with nc.Block() as block:
        @block.sync
        def _(sp):
            sp.dma_start(ident[:], a["eye"]).then_inc(w_in, 16)
            sp.dma_start(low[:, 0, :], a["low"]).then_inc(w_in, 16)
            sp.dma_start(spare_row[:], a["spare_row"]).then_inc(w_in, 16)
            sp.dma_start(tops[:].rearrange("p a h -> p (a h)"),
                         top.rearrange("p h -> (p h)").partition_broadcast(128)).then_inc(w_in, 16)
            sp.wait_ge(w_ok, 1)
            for table in tables:
                sp.dma_start(table.rearrange("(p r) n -> p (r n)", p=128), zero[:]).then_inc(zeroed, 16)

            def load(i, g, L):
                eqs.wait(sp, "cn3", L - G)
                rows.wait(sp, "i", L - G)
                src_in[g].wait(sp, i - 1)
                dst_in[g].wait(sp, i - 1)
                idx_in[g].inc(sp.dma_start(si[g][:], src_idx[L]))
                idx_in[g].inc(sp.dma_start(di[g][:], dst_idx[L]))
            pipeline(sp, LANES, G, [load], last=lambda: sp.wait_ge(w_in, 16))
            for t in range(TABLES):
                added[t].wait(sp, LANES * CH // TABLES - 1)

        @block.gpsimd
        def _(pool):
            pool.wait_ge(zeroed, 16 * TABLES)

            def gather(g, j):
                src_in[g].inc(pool.indirect_dma_start(
                    out=gs[g][:, j, :], out_offset=None, in_=gat,
                    in_offset=bass.IndirectOffsetOnAxis(ap=si[g][:, j:j + 1], axis=0),
                    bounds_check=T - 1, oob_is_err=True))
                dst_in[g].inc(pool.indirect_dma_start(
                    out=gd[g][:, j, :], out_offset=None, in_=dst_rows,
                    in_offset=bass.IndirectOffsetOnAxis(ap=di[g][:, j:j + 1], axis=0),
                    bounds_check=T - 1, oob_is_err=True))

            def gathers(i, g, L):
                idx_in[g].wait(pool, i)
                pay_s.wait(pool, L - G)
                pool.sem_inc(turn, 1)
                for j in range(CH):
                    gather(g, j)

            def scatters(i, g, L):
                comb_s.wait(pool, L)
                rows.wait(pool, "i", L)
                for j in range(CH):
                    t, n = j % TABLES, j // TABLES
                    per = CH // TABLES
                    k = L * per + n - 1
                    if not (isinstance(k, int) and k < 0):
                        pool.wait_ge(added[t].sem, (L * per + n) * 16)
                        pool.sem_inc(turn, 1)
                    added[t].inc(pool.indirect_dma_start(
                        out=tables[t], out_offset=bass.IndirectOffsetOnAxis(ap=ti[g][:, j:j + 1], axis=0),
                        in_=comb[g][:, j, :], in_offset=None,
                        compute_op=ALU.add, bounds_check=ROWS - 1, oob_is_err=True))
            pipeline(pool, LANES, G, [gathers, None, scatters])

        @block.tensor
        def _(pe):
            pe.wait_ge(w_in, 64)

            def targets(i, g, L):
                df_s.wait(pe, L)
                for q in range(4):
                    m = L * 4 + q - 2
                    if not (isinstance(m, int) and m < 0):
                        eqs.wait(pe, f"eq{(q - 2) % 4}", L if q >= 2 else L - 1)
                    for j in range(4 * q, 4 * q + 4):
                        mm = pe.transpose(pd[q % 2][:, j - 4 * q, :], df[g][:, j:j + 1].to_broadcast([128, 128]),
                                          ident[:])
                    pd_p.did(mm)

            def sums(i, g, L):
                eqs.wait(pe, "eq3", L)
                pay_s.wait(pe, L)
                comb_s.wait(pe, L - G)
                for j in range(CH):
                    mm = pe.matmul(pc[g][:, j, :], eq[g][:, j, :], pay[g][:, j, :], start=True, stop=True)
                pc_p.did(mm)
            pipeline(pe, LANES, G, [targets, sums])

        @block.scalar
        def _(act):
            def exps(i, g, L):
                lgt.wait(act, "sub", L)
                pc_p.wait(act, L - G)
                exp_s.did(act.activation(pay[g][:, :, 16:20], z[:], ACT.Exp))

            def copy(i, g, L):
                pc_p.wait(act, L)
                for t in range(TABLES):
                    added[t].wait(act, (L - 1) * (CH // TABLES) - 1)
                comb_s.did(act.activation(comb[g][:], pc[g][:], ACT.Copy))
            pipeline(act, LANES, G, [None, exps, copy])

        @block.vector
        def _(dve):
            dve.memset(zero[:], 0.0).then_inc(w_ok, 1)
            dve.wait_ge(w_in, 64)
            for q in range(1, 4):
                dve.tensor_copy(low[:, q, :], low[:, 0, :]).then_inc(w_ok, 1)
            dve.tensor_reduce(big[:], tops[:].rearrange("p a h -> p h a"), AX.X, ALU.max).then_inc(w_ok, 1)
            dve.wait_ge(w_ok, 5)

            def targets(i, g, L):
                idx_in[g].wait(dve, i)
                pd_p.wait(dve, 4 * (L - G) + 3)
                rows.wait(dve, "d", L - G)
                df_s.did(dve.tensor_copy(df[g][:], di[g][:]))

            def equal(i, g, L):
                df_s.wait(dve, L)
                pc_p.wait(dve, L - G)
                rows.wait(dve, "first", L - 1)
                for q in range(4):
                    js = slice(4 * q, 4 * q + 4)
                    pd_p.wait(dve, 4 * L + q)
                    eqs.did(dve.tensor_tensor(eq[g][:, js, :], pd[q % 2][:],
                                              df[g][:, js].unsqueeze(2).to_broadcast([128, 4, 128]), ALU.is_equal),
                            f"eq{q}")
                    eqs.wait(dve, f"eq{q}", L)
                    eqs.did(dve.tensor_tensor(eql[:], eq[g][:, js, :], low[:], ALU.mult), f"el{q}")
                    eqs.wait(dve, f"el{q}", L)
                    eqs.did(dve.tensor_reduce(cnt[:, js], eql[:], AX.X, ALU.add), f"cn{q}")
                for t in range(TABLES):
                    added[t].wait(dve, (L - 1) * (CH // TABLES) - 1)
                eqs.wait(dve, "cn3", L)
                rows.did(dve.tensor_scalar(first[:], cnt[:], 0.5, None, ALU.is_lt), "first")
                rows.did(dve.tensor_scalar(tgt[:], df[g][:], spare_row[:, 0:1], None, ALU.subtract), "d")
                rows.wait(dve, "d", L)
                rows.did(dve.tensor_tensor(tgt[:], tgt[:], first[:], ALU.mult), "m")
                rows.wait(dve, "m", L)
                rows.did(dve.tensor_scalar(tgt[:], tgt[:], spare_row[:, 0:1], None, ALU.add), "t")
                rows.wait(dve, "t", L)
                rows.did(dve.tensor_copy(ti[g][:], tgt[:]), "i")

            def logits(i, g, L):
                src_in[g].wait(dve, i)
                dst_in[g].wait(dve, i)
                pay_s.wait(dve, L - 1)
                lgt.did(dve.tensor_tensor(mz[:], gs[g][:, :, 16:20], gd[g][:], ALU.add), "z")
                lgt.wait(dve, "z", L)
                lgt.did(dve.scalar_tensor_tensor(z[:], mz[:], 0.2, mz[:], ALU.mult, ALU.max), "l")
                lgt.wait(dve, "l", L)
                lgt.did(dve.tensor_tensor(mz[:], gd[g][:], big[:].unsqueeze(1).to_broadcast([128, CH, 4]), ALU.add),
                        "mz")
                lgt.wait(dve, "mz", L)
                lgt.did(dve.scalar_tensor_tensor(ml[:], mz[:], 0.2, mz[:], ALU.mult, ALU.max), "ml")
                lgt.wait(dve, "ml", L)
                lgt.did(dve.tensor_tensor(z[:], z[:], ml[:], ALU.subtract), "sub")
                exp_s.wait(dve, L)
                pay_s.did(dve.tensor_tensor(
                    pay[g][:, :, 0:16].rearrange("p j (h e) -> p j h e", e=4),
                    gs[g][:, :, 0:16].rearrange("p j (h e) -> p j h e", e=4),
                    pay[g][:, :, 16:20].unsqueeze(3).to_broadcast([128, CH, 4, 4]), ALU.mult))

            def both(i, g, L):
                equal(i, g, L)
            pipeline(dve, LANES, G, [lambda i, g, L: (targets(i, g, L), equal(i, g, L)), logits])
    c.close()



def gat_gates(nc, a, gat, dst_rows, top, tables, gate_out):
    c = Core(nc, "gate")
    K = T // 128
    acc = c.sb("acc", [128, K, 20])
    part = [c.sb(f"part{k}", [128, K, 20]) for k in range(2)]
    g = c.sb("g", [128, K, 20])
    gd = c.sb("gd", [128, K, 4])
    z = c.sb("z", [128, K, 4])
    mz = c.sb("mz", [128, K, 4])
    ee = c.sb("ee", [128, K, 4])
    m = c.sb("m", [128, K])
    r = c.sb("r", [128, K])
    mh = c.sb("mh", [128, K])
    tops = c.sb("tops", [128, 128, 4])
    big = c.sb("big", [128, 4])
    bg = c.sb("bg", [128, 16])
    gam = c.sb("gam", [128, 16])
    bet = c.sb("bet", [128, 16])
    s = c.sb("s", [128, K, 4])
    gt = c.sb("gt", [128, K, 4])
    w_in, t_in, g_in = c.sem("w_in"), [c.sem(f"t_in{k}") for k in range(TABLES)], c.sem("g_in")
    dv, ex, pw, out_st = c.sem("dve_done"), c.sem("exp_done"), c.sem("pow_done"), c.sem("out_st")
    dve_at = {}

    with nc.Block() as block:
        @block.vector
        def _(dve):
            n = [0]

            def link(ins, name=None):
                n[0] += 1
                ins.then_inc(dv, 1)
                dve.wait_ge(dv, n[0])
                if name:
                    dve_at[name] = n[0]

            link(dve.memset(mh[:], -0.5), "mh")
            dve.wait_ge(w_in, 64)
            link(dve.tensor_reduce(big[:], tops[:].rearrange("p a h -> p h a"), AX.X, ALU.max))
            dve.wait_ge(g_in, 32)
            link(dve.tensor_tensor(mz[:], g[:, :, 16:20], gd[:], ALU.add))
            link(dve.scalar_tensor_tensor(z[:], mz[:], 0.2, mz[:], ALU.mult, ALU.max))
            link(dve.tensor_tensor(mz[:], gd[:], big[:].unsqueeze(1).to_broadcast([128, K, 4]), ALU.add))
            link(dve.scalar_tensor_tensor(gd[:], mz[:], 0.2, mz[:], ALU.mult, ALU.max))
            link(dve.tensor_tensor(z[:], z[:], gd[:], ALU.subtract), "logit")
            dve.wait_ge(t_in[0], 16)
            for k in range(1, TABLES):
                dve.wait_ge(t_in[k], 16)
                link(dve.tensor_tensor(acc[:], acc[:], part[k % 2][:], ALU.add), f"part{k}")
            dve.wait_ge(ex, 1)
            link(dve.tensor_tensor(acc[:, :, 16:20], acc[:, :, 16:20], ee[:], ALU.add))
            per_head = lambda t: t[:, :, 0:16].rearrange("p k (h e) -> p k h e", e=4)
            flat = lambda t: t[:].unsqueeze(3).to_broadcast([128, K, 4, 4])
            link(dve.tensor_tensor(per_head(g), per_head(g), flat(ee), ALU.mult))
            link(dve.tensor_tensor(acc[:, :, 0:16], acc[:, :, 0:16], g[:, :, 0:16], ALU.add))
            link(dve.tensor_scalar(z[:], acc[:, :, 16:20], 1e-37, None, ALU.add))
            link(dve.reciprocal(z[:], z[:]))
            link(dve.tensor_tensor(per_head(acc), per_head(acc), flat(z), ALU.mult))
            along = lambda t: t[:].unsqueeze(1).to_broadcast([128, K, 16])
            agg = acc[:, :, 0:16]
            link(dve.tensor_tensor(agg, agg, along(bg), ALU.add))
            link(dve.tensor_reduce(m[:], agg, AX.X, ALU.add))
            link(dve.tensor_scalar(m[:], m[:], 1 / 16, None, ALU.mult))
            link(dve.tensor_tensor(agg, agg, m[:].unsqueeze(2).to_broadcast([128, K, 16]), ALU.subtract))
            sq = g[:, :, 0:16]
            link(dve.tensor_tensor(sq, agg, agg, ALU.mult))
            link(dve.tensor_reduce(m[:], sq, AX.X, ALU.add))
            link(dve.tensor_scalar(m[:], m[:], 1 / 16, EPS, ALU.mult, ALU.add), "var")
            dve.wait_ge(pw, 1)
            link(dve.tensor_tensor(agg, agg, r[:].unsqueeze(2).to_broadcast([128, K, 16]), ALU.mult))
            link(dve.tensor_tensor(agg, agg, along(gam), ALU.mult))
            link(dve.tensor_tensor(agg, agg, along(bet), ALU.add))
            link(dve.tensor_reduce(s[:], agg.rearrange("p k (h e) -> p k e h", e=4), AX.X, ALU.add))
            link(dve.tensor_scalar(s[:], s[:], 1 / 4, None, ALU.mult))
            best_two(dve, link, s, gt, z, mz, m, 4, K)
            link(dve.tensor_reduce(m[:], s[:], AX.X, ALU.max))
            link(dve.tensor_tensor(s[:], s[:], m[:].unsqueeze(2).to_broadcast([128, K, 4]), ALU.subtract), "best")
            dve.wait_ge(ex, 2)
            link(dve.tensor_tensor(gt[:], gt[:], ee[:], ALU.mult))
            link(dve.tensor_reduce(m[:], gt[:], AX.X, ALU.add))
            link(dve.reciprocal(m[:], m[:]))
            link(dve.tensor_tensor(gt[:], gt[:], m[:].unsqueeze(2).to_broadcast([128, K, 4]), ALU.mult), "gates")

        @block.scalar
        def _(act):
            act.wait_ge(dv, dve_at["logit"])
            act.activation(ee[:], z[:], ACT.Exp).then_inc(ex, 1)
            act.wait_ge(dv, dve_at["best"])
            act.activation(ee[:], s[:], ACT.Exp).then_inc(ex, 1)

        @block.gpsimd
        def _(pool):
            pool.wait_ge(dv, dve_at["var"])
            pool.tensor_tensor(r[:], m[:], mh[:], ALU.pow).then_inc(pw, 1)

        @block.sync
        def _(sp):
            sp.dma_start(tops[:].rearrange("p a h -> p (a h)"),
                         top.rearrange("p h -> (p h)").partition_broadcast(128)).then_inc(w_in, 16)
            for t, src in ((bg, "b_gat"), (gam, "gat_g"), (bet, "gat_b")):
                sp.dma_start(t[:], a[src].partition_broadcast(128)).then_inc(w_in, 16)
            rows = lambda t: t[0:T].rearrange("(p k) n -> p k n", p=128)
            sp.dma_start(g[:], rows(gat)).then_inc(g_in, 16)
            sp.dma_start(gd[:], rows(dst_rows)).then_inc(g_in, 16)
            sp.dma_start(acc[:], rows(tables[0])).then_inc(t_in[0], 16)
            for k in range(1, TABLES):
                if k >= 3:
                    sp.wait_ge(dv, dve_at[f"part{k - 2}"])
                sp.dma_start(part[k % 2][:], rows(tables[k])).then_inc(t_in[k], 16)
            sp.wait_ge(dv, dve_at["gates"])
            sp.dma_start(rows(gate_out), gt[:]).then_inc(out_st, 16)
            sp.wait_ge(out_st, 16)
    c.close()


def best_two(dve, link, s, sel, u, w, one, E, K):
    for i in range(E):
        me = s[:, :, i:i + 1].to_broadcast([128, K, E])
        link(dve.tensor_tensor(u[:], s[:, :, :], me, ALU.is_gt))
        if i:
            link(dve.tensor_tensor(w[:, :, 0:i], s[:, :, 0:i], s[:, :, i:i + 1].to_broadcast([128, K, i]),
                                   ALU.is_equal))
            link(dve.tensor_tensor(u[:, :, 0:i], u[:, :, 0:i], w[:, :, 0:i], ALU.add))
        link(dve.tensor_reduce(one[:], u[:], AX.X, ALU.add))
        link(dve.tensor_scalar(sel[:, :, i], one[:], 1.5, None, ALU.is_lt))


def dense(nc, a, phase, x_in, x_out, E, gate=None, pre=False, extra=None, post=True):
    c = Core(nc, phase)
    G, K, LANES = 4, 4, T // 512
    x = [c.sb(f"x{k}", [128, K, C]) for k in range(G)]
    ex = [c.sb(f"ex{k}", [128, K, C]) for k in range(G)] if extra is not None else None
    gt = [c.sb(f"gt{k}", [128, K, E]) for k in range(G)] if gate is not None else None
    xn = [c.sb(f"xn{k}", [128, K, C]) for k in range(2)] if pre else None
    xT = [c.sb(f"xT{k}", [C, K, 128]) for k in range(2)]
    hid = [c.sb(f"hid{k}", [128, E, K, 128]) for k in range(2)]
    t1 = c.sb("t1", [128, E, C])
    s = [c.sb(f"s{k}", [128, K, C]) for k in range(2)]
    y = [c.sb(f"y{k}", [128, K, C]) for k in range(G)]
    st = c.sb("st", [128, K, 6])
    mv = [c.sb(f"mv{k}", [128, K, 2]) for k in range(2)]
    ve = c.sb("ve", [128, K])
    rstd = [c.sb(f"rstd{k}", [128, K]) for k in range(2)]
    st0 = c.sb("st0", [128, K, 6])
    mv0 = [c.sb(f"mv0{k}", [128, K, 2]) for k in range(2)]
    ve0 = c.sb("ve0", [128, K])
    rstd0 = [c.sb(f"rstd0{k}", [128, K]) for k in range(2)]
    mh = c.sb("mh", [128, K])
    spare = c.sb("spare", [128, 1])
    ident = c.sb("ident", [128, 128])
    w1 = c.sb("w1", [C, E, 128])
    b1 = c.sb("b1", [128, E])
    w2 = c.sb("w2", [128, E, C])
    b2 = c.sb("b2", [128, E, C])
    lnw = c.sb("lnw", [C, 2])

    pT = c.ps("pT", [C, K, 128])
    ph = [c.ps(f"ph{k}", [128, K, 128]) for k in range(2)]
    py = [c.ps(f"py{k}", [128, 512]) for k in range(2)]

    w_in, mh_set, turn = c.sem("w_in"), c.sem("mh_set"), c.sem("turn")
    loads = 1 + (gate is not None) + (extra is not None)
    ld = [c.loads(f"ld{k}", loads) for k in range(G)]
    stores = [c.loads(f"st{k}") for k in range(G)]
    pre_s, pre_r, xn_s = c.steps("pre_s", "s0 s1 s2 s3 m0 m1 m2 m3 ve"), c.flag("pre_r"), \
        c.steps("xn_s", "n0 n1 n2 n3")
    xT_p, xT_s, h_p, hid_s = c.flag("xT_p"), c.flag("xT_s"), c.flag("h_p"), c.flag("hid_s")
    y_p = c.flag("y_p")
    mix = c.steps("mix", " ".join(f"b{k} g{k} r{k}" for k in range(K)) + " add sum")
    norm, rs_s = c.steps("norm", "s0 s1 s2 s3 m0 m1 m2 m3 ve"), c.flag("rs_s")
    y_s = c.steps("y_s", "y0 y1 y2 y3")
    rows = lambda t: t.rearrange("(l p k) c -> l p k c", p=128, k=K)
    NW = 5 + pre

    with nc.Block() as block:
        @block.sync
        def _(sp):
            sp.dma_start(ident[:], a["eye"]).then_inc(w_in, 16)
            sp.dma_start(w1[:], a[phase + "_w1"].rearrange("e c n -> c e n")).then_inc(w_in, 16)
            sp.dma_start(b1[:], a[phase + "_b1"]).then_inc(w_in, 16)
            sp.dma_start(w2[:], a[phase + "_w2"].rearrange("e c n -> c e n")).then_inc(w_in, 16)
            sp.dma_start(b2[:].rearrange("p e c -> p (e c)"),
                         a[phase + "_b2"].rearrange("e c -> (e c)").partition_broadcast(128)).then_inc(w_in, 16)
            if pre:
                sp.dma_start(lnw[:], a[phase + "_ln"]).then_inc(w_in, 16)

            def load(i, g, L):
                mix.wait(sp, "sum", L - G)
                ld[g].inc(sp.dma_start(x[g][:], rows(x_in)[L]))
                if gate is not None:
                    ld[g].inc(sp.dma_start(gt[g][:], rows(gate)[L]))
                if extra is not None:
                    ld[g].inc(sp.dma_start(ex[g][:], rows(extra)[L]))

            def store(i, g, L):
                y_s.wait(sp, "y3", L)
                stores[g].inc(sp.dma_start(rows(x_out)[L], y[g][:]))
            pipeline(sp, LANES, G, [load, None, None, None, None, store])
            for g in range(G):
                stores[g].wait(sp, LANES // G - 1)

        @block.tensor
        def _(pe):
            pe.wait_ge(w_in, 16 * NW)

            def tr(i, g, L):
                if pre:
                    xn_s.wait(pe, "n3", L)
                else:
                    ld[g].wait(pe, i)
                xT_s.wait(pe, L - 1)
                pe.sem_inc(turn, 1)
                src = xn[g % 2] if pre else x[g]
                for k in range(K):
                    mm = pe.transpose(pT[:, k, :], src[:, k, :], ident[:])
                xT_p.did(mm)

            def up(i, g, L):
                xT_s.wait(pe, L)
                for e in range(E):
                    hid_s.wait(pe, L * E + e - 2)
                    h_p.did(pe.matmul(ph[e % 2 if E > 1 else g % 2][:].rearrange("p k n -> p (k n)"), w1[:, e, :],
                                      xT[g % 2][:].rearrange("p k n -> p (k n)"), start=True, stop=True))

            def down(i, g, L):
                hid_s.wait(pe, L * E + E - 1)
                for k in range(K):
                    mix.wait(pe, f"b{(k - 2) % K}", L if k >= 2 else L - 1)
                    for e in range(E):
                        mm = pe.matmul(py[k % 2][:, e * C:e * C + C], hid[g % 2][:, e, k, :], w2[:, e, :],
                                       start=True, stop=True)
                    y_p.did(mm)
            pipeline(pe, LANES, G, [None, tr, up, down])

        @block.scalar
        def _(act):
            act.wait_ge(w_in, 16 * NW)

            def copy_xT(i, g, L):
                xT_p.wait(act, L)
                h_p.wait(act, (L - 2) * E + E - 1)
                if pre:
                    xT_s.did(act.activation(xT[g % 2][:], pT[:], ACT.Identity, bias=lnw[:, 1:2], scale=lnw[:, 0:1]))
                else:
                    xT_s.did(act.activation(xT[g % 2][:], pT[:], ACT.Copy))

            def gelu(i, g, L):
                y_p.wait(act, (L - 2) * K + K - 1)
                for e in range(E):
                    h_p.wait(act, L * E + e)
                    hid_s.did(act.activation(hid[g % 2][:, e], ph[e % 2 if E > 1 else g % 2][:], ACT.Gelu,
                                             bias=b1[:, e:e + 1]))
            pipeline(act, LANES, G, [None, copy_xT, gelu])

        @block.gpsimd
        def _(pool):
            pool.memset(mh[:], -0.5).then_inc(mh_set, 1)
            pool.wait_ge(mh_set, 1)

            def rs0(i, g, L):
                pre_s.wait(pool, "ve", L)
                xn_s.wait(pool, "n3", L - 2)
                pre_r.did(pool.tensor_tensor(rstd0[g % 2][:], ve0[:], mh[:], ALU.pow))

            def rs(i, g, L):
                norm.wait(pool, "ve", L)
                y_s.wait(pool, "y3", L - 2)
                rs_s.did(pool.tensor_tensor(rstd[g % 2][:], ve[:], mh[:], ALU.pow))
            pipeline(pool, LANES, G, [rs0 if pre else None, None, None, rs if post else None])

        @block.vector
        def _(dve):
            def stats(steps, st, mv, ve, src, g, L):
                for k in range(K):
                    steps.did(dve.bn_stats(st[:, k, :], src[:, k, :]), f"s{k}")
                steps.wait(dve, "s3", L)
                dve.memset(spare[:], 0.0)
                for k in range(K):
                    steps.did(dve.bn_aggr(mv[:, k, :], st[:, k, :]), f"m{k}")
                steps.wait(dve, "m3", L)

            def pre_stats(i, g, L):
                ld[g].wait(dve, i)
                xn_s.wait(dve, "n3", L - 2)
                stats(pre_s, st0, mv0[g % 2], ve0, x[g], g, L)
                pre_r.wait(dve, L - 1)
                pre_s.did(dve.tensor_scalar(ve0[:], mv0[g % 2][:, :, 1], EPS, None, ALU.add), "ve")

            def pre_norm(i, g, L):
                pre_r.wait(dve, L)
                xT_p.wait(dve, L - 2)
                for k in range(K):
                    xn_s.did(dve.tensor_scalar(xn[g % 2][:, k, :], x[g][:, k, :], mv0[g % 2][:, k, 0:1],
                                               rstd0[g % 2][:, k:k + 1], ALU.subtract, ALU.mult), f"n{k}")

            def combine(i, g, L):
                y_s.wait(dve, "y3", L - 2)
                ld[g].wait(dve, i)
                for k in range(K):
                    y_p.wait(dve, L * K + k)
                    mix.wait(dve, f"r{(k - 1) % K}", L if k else L - 1)
                    flat = lambda t: t.rearrange("p e c -> p (e c)")
                    mix.did(dve.tensor_tensor(flat(t1[:]), py[k % 2][:, 0:E * C], flat(b2[:]), ALU.add), f"b{k}")
                    mix.wait(dve, f"b{k}", L)
                    if gate is not None:
                        mix.did(dve.tensor_tensor(t1[:], t1[:], gt[g][:, k, :].unsqueeze(2).to_broadcast([128, E, C]),
                                                  ALU.mult), f"g{k}")
                        mix.wait(dve, f"g{k}", L)
                        mix.did(dve.tensor_reduce(s[g % 2][:, k, :], t1[:].rearrange("p e c -> p c e"), AX.X, ALU.add),
                                f"r{k}")
                    else:
                        mix.did(dve.memset(spare[:], 0.0), f"g{k}")
                        mix.did(dve.tensor_copy(s[g % 2][:, k, :], t1[:, 0, :]), f"r{k}")
                mix.wait(dve, "r3", L)
                if extra is not None:
                    mix.did(dve.tensor_tensor(s[g % 2][:], s[g % 2][:], ex[g][:], ALU.add), "add")
                    mix.wait(dve, "add", L)
                else:
                    mix.did(dve.memset(spare[:], 0.0), "add")
                mix.did(dve.tensor_tensor(s[g % 2][:], s[g % 2][:], x[g][:], ALU.add), "sum")
                mix.wait(dve, "sum", L)
                if post:
                    stats(norm, st, mv[g % 2], ve, s[g % 2], g, L)
                    rs_s.wait(dve, L - 1)
                    norm.did(dve.tensor_scalar(ve[:], mv[g % 2][:, :, 1], EPS, None, ALU.add), "ve")

            def finish(i, g, L):
                stores[g].wait(dve, i - 1)
                if post:
                    rs_s.wait(dve, L)
                for k in range(K):
                    if post:
                        y_s.did(dve.tensor_scalar(y[g][:, k, :], s[g % 2][:, k, :], mv[g % 2][:, k, 0:1],
                                                  rstd[g % 2][:, k:k + 1], ALU.subtract, ALU.mult), f"y{k}")
                    else:
                        y_s.did(dve.tensor_copy(y[g][:, k, :], s[g % 2][:, k, :]), f"y{k}")
            pipeline(dve, LANES, G, [pre_stats if pre else None, pre_norm if pre else None, None, combine, finish])
    c.close()


H, DH, M = 8, 8, 64


def landmarks(nc, a, phase, layer, y_in, qk_out, v_out, a2_out, top_out):
    c = Core(nc, phase)
    G = 4
    y = [c.sb(f"y{k}", [128, 2, C]) for k in range(G)]
    st = c.sb("st", [128, 2, 6])
    mv = [c.sb(f"mv{k}", [128, 2, 2]) for k in range(2)]
    ve = c.sb("ve", [128, 2])
    rstd = [c.sb(f"rstd{k}", [128, 2]) for k in range(2)]
    xn = [c.sb(f"xn{k}", [128, 2, C]) for k in range(2)]
    xT = [c.sb(f"xT{k}", [C, 2, 128]) for k in range(2)]
    qk = [c.sb(f"qk{k}", [C, 2, P]) for k in range(G)]
    v = [c.sb(f"v{k}", [128, 2, C]) for k in range(G)]
    lm = c.sb("lm", [C, 2 * M])
    kl = [c.sb(f"kl{k}", [C, M]) for k in range(2)]
    qbd = [c.sb(f"qbd{k}", [C, H, M]) for k in range(2)]
    mx = c.sb("mx", [128, 4])
    lg = [c.sb(f"lg{k}", [128, 4, M]) for k in range(2)]
    e2 = [c.sb(f"e2{k}", [128, 4, M]) for k in range(2)]
    sm = c.sb("sm", [128, 4])
    a2 = [c.sb(f"a2{k}", [128, 4, M]) for k in range(G)]
    rsum = c.sb("rsum", [128, B, 4])
    csum = c.sb("csum", [128, B])
    tops = c.sb("tops", [128, 2])
    mh = c.sb("mh", [128, 2])
    spare = c.sb("spare", [128, 1])
    ident = c.sb("ident", [128, 128])
    ones = c.sb("ones", [128, 128])
    mask = c.sb("mask", [C, H, M])
    w = c.sb("w", [C, 3, C])
    lnw = c.sb("lnw", [C, 2])

    pT = c.ps("pT", [C, 2, 128])
    pqk = c.ps("pqk", [C, 2, P])
    pv = c.ps("pv", [128, 2, C])
    pa = c.ps("pa", [128, 4, M])
    pcs = c.ps("pcs", [128, 4, M])

    w_in, prep, mh_set, turn, turn_d = c.sem("w_in"), c.sem("prep"), c.sem("mh_set"), c.sem("turn"), c.sem("turn_d")
    ld = [c.loads(f"ld{k}") for k in range(G)]
    st_qk, st_v, st_a = ([c.loads(f"{n}{k}") for k in range(G)] for n in ("st_qk", "st_v", "st_a"))
    stat, rs_s, xn_s = c.steps("stat", "s0 s1 m0 m1 ve"), c.flag("rs_s"), c.steps("xn_s", "n0 n1")
    xT_p, xT_s, qk_p, qk_s, v_p, v_s = (c.flag(n) for n in ("xT_p", "xT_s", "qk_p", "qk_s", "v_p", "v_s"))
    lms, a_p, e_s = c.steps("lms", "lm kl qbd"), c.flag("a_p"), c.flag("e_s")
    soft = c.steps("soft", "mx sub")
    done = c.steps("done", "sm rc a2 rsum")
    cs_p, cs_s = c.flag("cs_p"), c.flag("cs_s")
    y_view = y_in.rearrange("(b k p) c -> b p k c", p=128, k=2)
    NW = 5

    with nc.Block() as block:
        @block.sync
        def _(sp):
            sp.dma_start(ident[:], a["eye"]).then_inc(w_in, 16)
            sp.dma_start(ones[:], a["ones_bd"]).then_inc(w_in, 16)
            sp.dma_start(mask[:].rearrange("c h m -> c (h m)"), a["head_mask"]).then_inc(w_in, 16)
            sp.dma_start(w[:], a["w_qkv"][layer]).then_inc(w_in, 16)
            sp.dma_start(lnw[:], a["ln1"][layer]).then_inc(w_in, 16)

            def load(i, g, L):
                xn_s.wait(sp, "n1", L - G)
                ld[g].inc(sp.dma_start(y[g][:], y_view[L]))

            def store_qkv(i, g, L):
                qk_s.wait(sp, L)
                st_qk[g].inc(sp.dma_start(qk_out[L], qk[g][:]))
                v_s.wait(sp, L)
                st_v[g].inc(sp.dma_start(v_out[L], v[g][:]))

            def store_a(i, g, L):
                done.wait(sp, "a2", L)
                st_a[g].inc(sp.dma_start(a2_out[L], a2[g][:]))
            pipeline(sp, B, G, [load, None, None, store_qkv, None, None, store_a])
            for g in range(G):
                for s in (st_qk, st_v, st_a):
                    s[g].wait(sp, B // G - 1)
            sp.wait_ge(turn_d, 2)
            sp.dma_start(top_out, tops[:]).then_inc(w_in, 16)
            sp.wait_ge(w_in, 16 * NW + 16)

        @block.tensor
        def _(pe):
            pe.wait_ge(w_in, 16 * NW)
            pe.wait_ge(prep, 1)

            def tr(i, g, L):
                xn_s.wait(pe, "n1", L)
                xT_s.wait(pe, L - 1)
                pe.sem_inc(turn, 1)
                for k in range(2):
                    mm = pe.transpose(pT[:, k, :], xn[g % 2][:, k, :], ident[:])
                xT_p.did(mm)

            def qkv(i, g, L):
                xT_s.wait(pe, L)
                qk_s.wait(pe, L - 1)
                pe.sem_inc(turn, 1)
                for t in range(2):
                    mm = pe.matmul(pqk[:, t, :], w[:, t, :], xT[g % 2][:].rearrange("c k p -> c (k p)"),
                                   start=True, stop=True)
                qk_p.did(mm)
                v_s.wait(pe, L - 1)
                for k in range(2):
                    mm = pe.matmul(pv[:, k, :], xT[g % 2][:, k, :], w[:, 2, :], start=True, stop=True)
                v_p.did(mm)

            def a2s(i, g, L):
                lms.wait(pe, "qbd", L)
                soft.wait(pe, "sub", L - 1)
                for p in range(4):
                    mm = pe.matmul(pa[:, p, :], qbd[g % 2][:, 2 * p:2 * p + 2, :].rearrange("c h m -> c (h m)"),
                                   kl[g % 2][:], start=True, stop=True)
                a_p.did(mm)

            def columns(i, g, L):
                done.wait(pe, "a2", L)
                cs_s.wait(pe, L - 1)
                cs_p.did(pe.matmul(pcs[:].rearrange("p h m -> p (h m)"), ones[:],
                                   a2[g][:].rearrange("p h m -> p (h m)"), start=True, stop=True))
            pipeline(pe, B, G, [None, tr, qkv, a2s, None, columns])

        @block.scalar
        def _(act):
            act.wait_ge(w_in, 16 * NW)

            def copy_xT(i, g, L):
                xT_p.wait(act, L)
                v_p.wait(act, L - 2)
                xT_s.did(act.activation(xT[g % 2][:], pT[:], ACT.Identity, bias=lnw[:, 1:2], scale=lnw[:, 0:1]))

            def copy_qk(i, g, L):
                qk_p.wait(act, L)
                st_qk[g].wait(act, i - 1)
                lms.wait(act, "lm", L - G)
                qk_s.did(act.activation(qk[g][:], pqk[:], ACT.Copy))

            def exps(i, g, L):
                soft.wait(act, "sub", L)
                done.wait(act, "a2", L - 2)
                e_s.did(act.activation(e2[g % 2][:], lg[g % 2][:], ACT.Exp))
            pipeline(act, B, G, [None, copy_xT, copy_qk, None, exps])

        @block.gpsimd
        def _(pool):
            pool.memset(mh[:], -0.5).then_inc(mh_set, 1)
            pool.wait_ge(mh_set, 1)

            def rs(i, g, L):
                stat.wait(pool, "ve", L)
                xn_s.wait(pool, "n1", L - 2)
                rs_s.did(pool.tensor_tensor(rstd[g % 2][:], ve[:], mh[:], ALU.pow))
            pipeline(pool, B, G, [rs])

        @block.vector
        def _(dve):
            dve.wait_ge(w_in, 16 * NW)
            dve.tensor_scalar(w[:, 0, :], w[:, 0, :], float(DH) ** -0.5, None, ALU.mult).then_inc(prep, 1)

            def stats(i, g, L):
                ld[g].wait(dve, i)
                xn_s.wait(dve, "n1", L - 2)
                for k in range(2):
                    stat.did(dve.bn_stats(st[:, k, :], y[g][:, k, :]), f"s{k}")
                stat.wait(dve, "s1", L)
                dve.memset(spare[:], 0.0)
                for k in range(2):
                    stat.did(dve.bn_aggr(mv[g % 2][:, k, :], st[:, k, :]), f"m{k}")
                stat.wait(dve, "m1", L)
                rs_s.wait(dve, L - 1)
                stat.did(dve.tensor_scalar(ve[:], mv[g % 2][:, :, 1], EPS, None, ALU.add), "ve")

            def normed(i, g, L):
                rs_s.wait(dve, L)
                xT_p.wait(dve, L - 2)
                for k in range(2):
                    xn_s.did(dve.tensor_scalar(xn[g % 2][:, k, :], y[g][:, k, :], mv[g % 2][:, k, 0:1],
                                               rstd[g % 2][:, k:k + 1], ALU.subtract, ALU.mult), f"n{k}")

            def copy_v(i, g, L):
                v_p.wait(dve, L)
                st_v[g].wait(dve, i - 1)
                v_s.did(dve.tensor_copy(v[g][:], pv[:]))

            def means(i, g, L):
                qk_s.wait(dve, L)
                lms.wait(dve, "qbd", L - 1)
                lms.did(dve.tensor_reduce(lm[:], qk[g][:].rearrange("c t (m l) -> c (t m) l", l=4), AX.X, ALU.add),
                        "lm")
                lms.wait(dve, "lm", L)
                a_p.wait(dve, L - 2)
                lms.did(dve.tensor_scalar(kl[g % 2][:], lm[:, M:2 * M], 0.25, None, ALU.mult), "kl")
                lms.did(dve.scalar_tensor_tensor(qbd[g % 2][:], lm[:, 0:M].unsqueeze(1).to_broadcast([C, H, M]), 0.25,
                                                 mask[:], ALU.mult, ALU.mult), "qbd")

            def shift(i, g, L):
                a_p.wait(dve, L)
                soft.wait(dve, "sub", L - 1)
                e_s.wait(dve, L - 2)
                soft.did(dve.tensor_reduce(mx[:], pa[:], AX.X, ALU.max), "mx")
                soft.wait(dve, "mx", L)
                soft.did(dve.tensor_tensor(lg[g % 2][:], pa[:], mx[:].unsqueeze(2).to_broadcast([128, 4, M]),
                                           ALU.subtract), "sub")

            def divide(i, g, L):
                e_s.wait(dve, L)
                st_a[g].wait(dve, i - 1)
                cs_p.wait(dve, L - G)
                done.did(dve.tensor_reduce(sm[:], e2[g % 2][:], AX.X, ALU.add), "sm")
                done.wait(dve, "sm", L)
                done.did(dve.reciprocal(sm[:], sm[:]), "rc")
                done.wait(dve, "rc", L)
                done.did(dve.tensor_tensor(a2[g][:], e2[g % 2][:], sm[:].unsqueeze(2).to_broadcast([128, 4, M]),
                                           ALU.mult), "a2")
                done.wait(dve, "a2", L)
                done.did(dve.tensor_reduce(rsum[:, L] if isinstance(L, int) else rsum[:, bass.ds(L, 1)].rearrange(
                    "p a h -> p (a h)"), a2[g][:], AX.X, ALU.add), "rsum")

            def cmax(i, g, L):
                cs_p.wait(dve, L)
                cs_s.did(dve.tensor_reduce(csum[:, L:L + 1] if isinstance(L, int) else csum[:, bass.ds(L, 1)],
                                           pcs[:].rearrange("p h m -> p (h m)"), AX.X, ALU.max))
            pipeline(dve, B, G, [stats, normed, copy_v, means, shift, divide, cmax])
            done.wait(dve, "rsum", B - 1)
            cs_s.wait(dve, B - 1)
            dve.tensor_reduce(tops[:, 0:1], rsum[:].rearrange("p b h -> p (b h)"), AX.X, ALU.max).then_inc(turn_d, 1)
            dve.tensor_reduce(tops[:, 1:2], csum[:], AX.X, ALU.max).then_inc(turn_d, 1)
    c.close()


def inverse(nc, a, phase, a2_in, top_in, zt_out):
    c = Core(nc, phase)
    G, IT, LANES = 4, 6, B // 4
    last = IT - 1
    wide = lambda n: [c.sb(f"{n}{k}", [128, 4, 128]) for k in range(G)]
    x = [[c.sb(f"x{b}{k}", [128, 4, 128]) for k in range(G)] for b in range(2)]
    xt, p, r, k1, k2, k3 = (wide(n) for n in ("xt", "p", "r", "k1", "k2", "k3"))
    zo = [c.sb(f"zo{k}", [128, 4, M]) for k in range(G)]
    ident = c.sb("ident", [128, 128])
    tops = c.sb("tops", [128, 128, 2])
    big = c.sb("big", [128, 2])
    inv = c.sb("inv", [128, 2])
    ps = [[c.ps(f"p{g}{k}", [128, 4, 128]) for k in range(2)] for g in range(G)]

    w_in, zeroed, ready, chain = c.sem("w_in"), c.sem("zeroed"), c.sem("ready"), c.sem("chain")
    ld = [c.loads(f"ld{b}", 2 * G) for b in range(2)]
    sts = c.loads("sts", G)
    by_image = lambda names: " ".join(f"{n}_{g}" for n in names.split() for g in range(G))
    iters = lambda names, end: by_image(" ".join(f"{n}{t}" for t in range(end) for n in names.split()))
    pe_s = c.steps("pe_s", by_image("xt a") + " " + iters("k1 k2 k3", IT))
    act_s = c.steps("act_s", by_image("xt p") + " " + " ".join(f"r{t}_{g} p{t}_{g}" for t in range(last) for g in range(G)))
    dve_s = c.steps("dve_s", by_image("rp") + " " + iters("k1 k2 k3", IT))
    pool_s = c.steps("pool_s", by_image("ry"))
    turn = c.sem("turn")
    halves = (slice(0, 64), slice(64, 128))

    with nc.Block() as block:
        @block.sync
        def _(sp):
            sp.dma_start(ident[:], a["eye"]).then_inc(w_in, 16)
            sp.dma_start(tops[:].rearrange("p a t -> p (a t)"),
                         top_in.rearrange("p t -> (p t)").partition_broadcast(128)).then_inc(w_in, 16)
            sp.wait_ge(zeroed, 2 * G)

            def load(i, b, L):
                pe_s.wait(sp, "xt_3", L - 2)
                pool_s.wait(sp, "ry_3", L - 2)
                for g in range(G):
                    for s in halves:
                        ld[b].inc(sp.dma_start(x[b][g][s, :, s], a2_in[4 * L + g, s]))

            def store(i, b, L):
                dve_s.wait(sp, f"k3{last}_3", L)
                for g in range(G):
                    sts.inc(sp.dma_start(zt_out[4 * L + g], zo[g][:]))
            pipeline(sp, LANES, 2, [load, store], look=2)
            sts.wait(sp, LANES - 1)

        @block.tensor
        def _(pe):
            pe.wait_ge(w_in, 32)
            pe.wait_ge(ready, 1)

            def group(name, g, k, lhs, rhs):
                for q in range(4):
                    mm = pe.matmul(ps[g][k][:, q], lhs[:, q], rhs[:, q], start=True, stop=True)
                pe_s.did(mm, name)

            def lane(i, b, L):
                for g in range(G):
                    ld[b].wait(pe, i)
                    dve_s.wait(pe, f"k2{last}_{g}", L - 1)
                    for q in range(4):
                        mm = pe.transpose(ps[g][0][:, q], x[b][g][:, q], ident[:])
                    pe_s.did(mm, f"xt_{g}")
                for g in range(G):
                    act_s.wait(pe, f"xt_{g}", L)
                    dve_s.wait(pe, f"k3{last}_{g}", L - 1)
                    group(f"a_{g}", g, 1, xt[g], xt[g])
                for t in range(IT):
                    for g in range(G):
                        if t == 0:
                            pool_s.wait(pe, f"ry_{g}", L)
                            dve_s.wait(pe, f"rp_{g}", L)
                        else:
                            act_s.wait(pe, f"p{t - 1}_{g}", L)
                        group(f"k1{t}_{g}", g, t % 2, p[g], r[g])
                    for g in range(G):
                        dve_s.wait(pe, f"k1{t}_{g}", L)
                        group(f"k2{t}_{g}", g, 1 - t % 2, p[g], k1[g])
                    for g in range(G):
                        dve_s.wait(pe, f"k2{t}_{g}", L)
                        group(f"k3{t}_{g}", g, t % 2, p[g], k2[g])
            pipeline(pe, LANES, 2, [lane], look=2)

        @block.scalar
        def _(act):
            act.wait_ge(ready, 1)

            def lane(i, b, L):
                for g in range(G):
                    pe_s.wait(act, f"xt_{g}", L)
                    act_s.did(act.activation(xt[g][:], ps[g][0][:], ACT.Copy), f"xt_{g}")
                for g in range(G):
                    pe_s.wait(act, f"a_{g}", L)
                    act_s.did(act.activation(p[g][:], ps[g][1][:], ACT.Copy, scale=inv[:, 0:1]), f"p_{g}")
                for t in range(last):
                    for g in range(G):
                        dve_s.wait(act, f"k3{t}_{g}", L)
                        act_s.did(act.activation(r[g][:], k3[g][:], ACT.Copy, scale=0.25), f"r{t}_{g}")
                        for s in halves:
                            cp = act.activation(p[g][s, :, s], k3[g][s, :, 0:64], ACT.Copy)
                        act_s.did(cp, f"p{t}_{g}")
            pipeline(act, LANES, 2, [lane], look=2)

        @block.gpsimd
        def _(pool):
            pool.wait_ge(ready, 1)

            def lane(i, b, L):
                for g in range(G):
                    ld[b].wait(pool, i)
                    dve_s.wait(pool, f"k3{last}_{g}", L - 1)
                    pool.sem_inc(turn, 1)
                    for s in halves:
                        m = pool.tensor_scalar(r[g][s, :, 64:128], x[b][g][s, :, s], inv[s, 1:2], None, ALU.mult)
                    pool_s.did(m, f"ry_{g}")
            pipeline(pool, LANES, 2, [lane], look=2)

        @block.vector
        def _(dve):
            for b in range(2):
                for g in range(G):
                    dve.memset(x[b][g][:], 0.0).then_inc(zeroed, 1)
            dve.wait_ge(w_in, 32)
            dve.tensor_reduce(big[:], tops[:].rearrange("p a t -> p t a"), AX.X, ALU.max).then_inc(chain, 1)
            dve.wait_ge(chain, 1)
            dve.tensor_tensor(inv[:, 1:2], big[:, 0:1], big[:, 1:2], ALU.mult).then_inc(chain, 1)
            dve.wait_ge(chain, 2)
            dve.reciprocal(inv[:, 0:1], inv[:, 1:2]).then_inc(chain, 1)
            dve.wait_ge(chain, 3)
            dve.tensor_scalar(inv[:, 1:2], inv[:, 0:1], 0.25, None, ALU.mult).then_inc(ready, 1)

            def lane(i, b, L):
                def less(dst, scale, bank, cut=slice(0, 128)):
                    return dve.scalar_tensor_tensor(dst[:], r[g][:, :, cut], scale, bank[:, :, cut],
                                                    ALU.mult, ALU.subtract)
                for g in range(G):
                    act_s.wait(dve, f"p_{g}", L)
                    for s in halves:
                        m = dve.tensor_scalar(r[g][s, :, 0:64], p[g][s, :, s], 0.25, None, ALU.mult)
                    dve_s.did(m, f"rp_{g}")
                for t in range(IT):
                    for g in range(G):
                        pe_s.wait(dve, f"k1{t}_{g}", L)
                        dve_s.did(less(k1[g], 7.0, ps[g][t % 2]), f"k1{t}_{g}")
                    for g in range(G):
                        pe_s.wait(dve, f"k2{t}_{g}", L)
                        dve_s.did(less(k2[g], 15.0, ps[g][1 - t % 2]), f"k2{t}_{g}")
                    if t == last:
                        sts.wait(dve, L - 1)
                    for g in range(G):
                        pe_s.wait(dve, f"k3{t}_{g}", L)
                        if t < last:
                            dve_s.did(less(k3[g], 13.0, ps[g][t % 2]), f"k3{t}_{g}")
                        else:
                            dve_s.did(less(zo[g], 13.0, ps[g][t % 2], slice(64, 128)), f"k3{t}_{g}")
            pipeline(dve, LANES, 2, [lane], look=2)
    c.close()


def convolution(nc, a, phase, layer, v_in, res_out):
    c = Core(nc, phase)
    v = c.sb("v", [128, 2, B, C])
    res = c.sb("res", [128, B, C])
    band = c.sb("band", [128, H, 2, P])
    ps = [c.ps(f"p{k}", [128, 64, DH]) for k in range(4)]
    w_in, v_in_s, out_st = c.sem("w_in"), c.sem("v_in"), c.sem("out_st")
    mm_s, cp_v, cp_a = c.sem("mm_s"), c.sem("cp_v"), c.sem("cp_a")
    units = [(n, h, g) for n in range(2) for h in range(H) for g in range(2)]

    with nc.Block() as block:
        @block.sync
        def _(sp):
            sp.dma_start(band[:].rearrange("p h k n -> p (h k n)"), a["band"][layer]).then_inc(w_in, 16)
            for k in range(2):
                sp.dma_start(v[:, k].rearrange("p b c -> p (b c)"), v_in[:, k].rearrange("p b c -> p (b c)"))\
                  .then_inc(v_in_s, 16)
            for n in range(2):
                sp.wait_ge(cp_v, (n + 1) * H)
                sp.wait_ge(cp_a, (n + 1) * H)
                sp.dma_start(res_out[:, n].rearrange("p b c -> p (b c)"), res[:].rearrange("p b c -> p (b c)"))\
                  .then_inc(out_st, 16)
            sp.wait_ge(out_st, 32)

        @block.tensor
        def _(pe):
            pe.wait_ge(w_in, 16)
            pe.wait_ge(v_in_s, 32)
            for u, (n, h, g) in enumerate(units):
                if u >= 4:
                    pe.wait_ge(cp_a if u % 2 else cp_v, (u - 4) // 2 + 1)
                for k in range(2):
                    mm = pe.matmul(ps[u % 4][:], band[:, h, k, 128 * n:128 * n + 128],
                                   v[:, k, 64 * g:64 * g + 64, DH * h:DH * h + DH], start=k == 0, stop=k == 1)
                mm.then_inc(mm_s, 1)

        def copies(eng, copy, odd, done):
            for u, (n, h, g) in enumerate(units):
                if u % 2 != odd:
                    continue
                eng.wait_ge(mm_s, u + 1)
                if n == 1:
                    eng.wait_ge(out_st, 16)
                copy(res[:, 64 * g:64 * g + 64, DH * h:DH * h + DH], ps[u % 4][:]).then_inc(done, 1)

        @block.scalar
        def _(act):
            copies(act, lambda d, s: act.activation(d, s, ACT.Copy), 1, cp_a)

        @block.vector
        def _(dve):
            copies(dve, dve.tensor_copy, 0, cp_v)
    c.close()


def attend(nc, a, phase, layer, y_in, qk_in, v_in, zt_in, res_in, y_out):
    c = Core(nc, phase)
    G = 4
    y = [c.sb(f"y{k}", [128, 2, C]) for k in range(G)]
    qk = [c.sb(f"qk{k}", [C, 2, P]) for k in range(G)]
    v = [c.sb(f"v{k}", [128, 2, C]) for k in range(G)]
    zt = [c.sb(f"zt{k}", [128, 4, M]) for k in range(G)]
    res = [c.sb(f"res{k}", [128, 2, C]) for k in range(G)]
    lm = c.sb("lm", [C, 2 * M])
    qbd = c.sb("qbd", [C, H, M])
    kbd = c.sb("kbd", [C, H, M])
    mx3, nx3 = c.sb("mx3", [128, 4]), c.sb("nx3", [128, 4])
    a3 = [c.sb(f"a3{k}", [128, 4, P]) for k in range(2)]
    sm3 = [c.sb(f"sm3{k}", [128, 4]) for k in range(2)]
    rc3 = c.sb("rc3", [128, 4])
    mx1 = c.sb("mx1", [128, 2, H])
    lg1 = c.sb("lg1", [128, 2, H, M])
    a1 = [c.sb(f"a1{k}", [128, 2, H, M]) for k in range(2)]
    rc1 = [c.sb(f"rc1{k}", [128, 2, H]) for k in range(2)]
    a3T = c.sb("a3T", [128, 2, 4, 128])
    a1T = c.sb("a1T", [128, 2, 4, 128])
    b3 = c.sb("b3", [128, 4, DH])
    wbd = c.sb("wbd", [128, 4, 2, DH])
    ao = c.sb("ao", [128, 2, C])
    aoT = c.sb("aoT", [C, 2, 128])
    yo = [c.sb(f"yo{k}", [128, 2, C]) for k in range(G)]
    ident = c.sb("ident", [128, 128])
    mask = c.sb("mask", [C, H, M])
    wout = c.sb("wout", [C, C])
    bout = c.sb("bout", [128, C])

    ps3 = c.ps("ps3", [128, 4, P])
    ps1 = c.ps("ps1", [128, 2, H, M])
    ptr = [c.ps(f"ptr{k}", [128, 4, 128]) for k in range(2)]
    psm = c.ps("psm", [128, 512])
    pso = c.ps("pso", [128, 512])

    w_in, prep, turn = c.sem("w_in"), c.sem("prep"), c.sem("turn")
    ld = [c.loads(f"ld{k}", 5) for k in range(G)]
    sts = [c.loads(f"sts{k}") for k in range(G)]
    lms = c.steps("lms", "lm qbd kbd")
    s_p = c.steps("s_p", "s3 s1")
    sf3, e3 = c.steps("sf3", "mx nx"), c.flag("e3")
    sf1, e1, n1 = c.steps("sf1", "mx sub"), c.flag("e1"), c.steps("n1", "sum rc")
    tr_p = c.steps("tr_p", "t0 t1 t2 t3")
    tr_a, tr_v = c.steps("tr_a", "t0 t2"), c.steps("tr_v", "t1 t3")
    b_p, b_s = c.flag("b_p"), c.steps("b_s", "rc b0 b1")
    w_p, w_s = c.flag("w_p"), c.steps("w_s", "w0 w1")
    o_p, o_s = c.flag("o_p"), c.steps("o_s", "div res")
    oT_p, oT_s, y_p, y_s = c.flag("oT_p"), c.flag("oT_s"), c.flag("y_p"), c.steps("y_s", "proj bias")
    view = lambda t: t.rearrange("(b k p) c -> b p k c", p=128, k=2)
    NW = 4

    with nc.Block() as block:
        @block.sync
        def _(sp):
            sp.dma_start(ident[:], a["eye"]).then_inc(w_in, 16)
            sp.dma_start(mask[:].rearrange("c h m -> c (h m)"), a["head_mask"]).then_inc(w_in, 16)
            sp.dma_start(wout[:], a["w_out"][layer]).then_inc(w_in, 16)
            sp.dma_start(bout[:], a["b_out"][layer].partition_broadcast(128)).then_inc(w_in, 16)

            def load(i, g, L):
                y_s.wait(sp, "bias", L - G)
                for dst, src in ((y, view(y_in)[L]), (qk, qk_in[L]), (v, v_in[L]), (zt, zt_in[L]), (res, res_in[L])):
                    ld[g].inc(sp.dma_start(dst[g][:], src))

            def store(i, g, L):
                y_s.wait(sp, "bias", L)
                sts[g].inc(sp.dma_start(view(y_out)[L], yo[g][:]))
            pipeline(sp, B, G, [load, None, None, None, store])
            for g in range(G):
                sts[g].wait(sp, B // G - 1)

        @block.tensor
        def _(pe):
            pe.wait_ge(w_in, 16 * NW)
            pe.wait_ge(prep, 1)

            def scores(i, g, L):
                lms.wait(pe, "qbd", L)
                e3.wait(pe, 4 * (L - 1) + 3)
                for p in range(4):
                    mm = pe.matmul(ps3[:, p, :], qbd[:, 2 * p:2 * p + 2, :].rearrange("c h m -> c (h m)"),
                                   qk[g][:, 1, :], start=True, stop=True)
                s_p.did(mm, "s3")
                lms.wait(pe, "kbd", L)
                sf1.wait(pe, "sub", L - 1)
                for k in range(2):
                    mm = pe.matmul(ps1[:, k].rearrange("p h m -> p (h m)"), qk[g][:, 0, 128 * k:128 * k + 128],
                                   kbd[:].rearrange("c h m -> c (h m)"), start=True, stop=True)
                s_p.did(mm, "s1")

            def mixed(i, g, L):
                e3.wait(pe, 4 * L + 3)
                for k in range(2):
                    (tr_a if k == 0 else tr_v).wait(pe, "t2" if k == 0 else "t3", L - 1)
                    for p in range(4):
                        mm = pe.transpose(ptr[k][:, p, :], a3[g % 2][:, p, 128 * k:128 * k + 128], ident[:])
                    tr_p.did(mm, f"t{k}")
                e1.wait(pe, L)
                for k in range(2):
                    (tr_a if k == 0 else tr_v).wait(pe, "t0" if k == 0 else "t1", L)
                    for p in range(4):
                        mm = pe.transpose(ptr[k][:, p, :], a1[g % 2][:, k, 2 * p:2 * p + 2, :].rearrange(
                            "p h m -> p (h m)"), ident[:])
                    tr_p.did(mm, f"t{k + 2}")
                w_s.wait(pe, "w1", L - 1)
                for p in range(4):
                    for k in range(2):
                        mm = pe.matmul(psm[:, 16 * p:16 * p + 16], a3T[:, k, p, :], v[g][:, k, 16 * p:16 * p + 16],
                                       start=k == 0, stop=k == 1)
                b_p.did(mm)
                b_s.wait(pe, "b1", L)
                pe.sem_inc(turn, 1)
                for p in range(4):
                    for h in range(2):
                        r = slice(64 * h, 64 * h + 64)
                        mm = pe.matmul(psm[r, 128 + 8 * p:136 + 8 * p], zt[g][r, p, :], b3[r, p, :],
                                       start=True, stop=True)
                w_p.did(mm)

            def outs(i, g, L):
                w_s.wait(pe, "w1", L)
                tr_a.wait(pe, "t2", L)
                tr_v.wait(pe, "t3", L)
                y_s.wait(pe, "proj", L - 1)
                for k in range(2):
                    for p in range(4):
                        mm = pe.matmul(pso[:, 64 * k + 16 * p:64 * k + 16 * p + 16], a1T[:, k, p, :],
                                       wbd[:, p].rearrange("p h d -> p (h d)"), start=True, stop=True)
                o_p.did(mm)

            def project(i, g, L):
                o_s.wait(pe, "res", L)
                pe.sem_inc(turn, 1)
                for k in range(2):
                    mm = pe.transpose(pso[0:64, 128 + 128 * k:256 + 128 * k], ao[:, k, :], ident[:])
                oT_p.did(mm)
                oT_s.wait(pe, L)
                for k in range(2):
                    mm = pe.matmul(pso[:, 384 + 64 * k:448 + 64 * k], aoT[:, k, :], wout[:], start=True, stop=True)
                y_p.did(mm)
            pipeline(pe, B, G, [None, scores, mixed, lambda i, g, L: (outs(i, g, L), project(i, g, L))])

        @block.scalar
        def _(act):
            def exps(i, g, L):
                sf3.wait(act, "nx", L)
                tr_p.wait(act, "t1", L - 2)
                b_s.wait(act, "rc", L - 2)
                for p in range(4):
                    e3.did(act.activation(a3[g % 2][:, p, :], ps3[:, p, :], ACT.Exp, bias=nx3[:, p:p + 1],
                                          accum_out=sm3[g % 2][:, p:p + 1]))
                sf1.wait(act, "sub", L)
                tr_p.wait(act, "t3", L - 2)
                n1.wait(act, "sum", L - 2)
                e1.did(act.activation(a1[g % 2][:], lg1[:], ACT.Exp))

            def copies(i, g, L):
                tr_p.wait(act, "t0", L)
                b_p.wait(act, L - 1)
                tr_a.did(act.activation(a3T[:, 0], ptr[0][:], ACT.Copy), "t0")
                tr_p.wait(act, "t2", L)
                o_p.wait(act, L - 1)
                tr_a.did(act.activation(a1T[:, 0], ptr[0][:], ACT.Copy), "t2")

            def copy_oT(i, g, L):
                oT_p.wait(act, L)
                y_p.wait(act, L - 1)
                oT_s.did(act.activation(aoT[:].rearrange("c k p -> c (k p)"), pso[0:64, 128:384], ACT.Copy))
            pipeline(act, B, G, [None, exps, copies, copy_oT])

        @block.vector
        def _(dve):
            dve.memset(wbd[:], 0.0).then_inc(prep, 1)
            dve.wait_ge(w_in, 16 * NW)

            def means(i, g, L):
                ld[g].wait(dve, i)
                lms.wait(dve, "kbd", L - 1)
                lms.did(dve.tensor_reduce(lm[:], qk[g][:].rearrange("c t (m l) -> c (t m) l", l=4), AX.X, ALU.add),
                        "lm")
                lms.wait(dve, "lm", L)
                s_p.wait(dve, "s1", L - 1)
                for n, (t, dst) in enumerate((("qbd", qbd), ("kbd", kbd))):
                    lms.did(dve.scalar_tensor_tensor(dst[:], lm[:, M * n:M * n + M].unsqueeze(1)
                                                     .to_broadcast([C, H, M]), 0.25, mask[:], ALU.mult, ALU.mult), t)

            def maxima(i, g, L):
                s_p.wait(dve, "s3", L)
                e3.wait(dve, 4 * (L - 1) + 3)
                sf3.did(dve.tensor_reduce(mx3[:], ps3[:], AX.X, ALU.max), "mx")
                sf3.wait(dve, "mx", L)
                sf3.did(dve.tensor_scalar(nx3[:], mx3[:], -1.0, None, ALU.mult), "nx")
                s_p.wait(dve, "s1", L)
                e1.wait(dve, L - 1)
                sf1.did(dve.tensor_reduce(mx1[:], ps1[:], AX.X, ALU.max), "mx")
                sf1.wait(dve, "mx", L)
                sf1.did(dve.tensor_tensor(lg1[:].rearrange("p k h m -> p (k h) m"),
                                          ps1[:].rearrange("p k h m -> p (k h) m"),
                                          mx1[:].rearrange("p k h -> p (k h)").unsqueeze(2)
                                          .to_broadcast([128, 2 * H, M]), ALU.subtract), "sub")

            def middle(i, g, L):
                tr_p.wait(dve, "t1", L)
                b_p.wait(dve, L - 1)
                tr_v.did(dve.tensor_copy(a3T[:, 1], ptr[1][:]), "t1")
                tr_p.wait(dve, "t3", L)
                o_p.wait(dve, L - 1)
                tr_v.did(dve.tensor_copy(a1T[:, 1], ptr[1][:]), "t3")
                e3.wait(dve, 4 * L + 3)
                b_s.did(dve.reciprocal(rc3[:], sm3[g % 2][:]), "rc")
                b_s.wait(dve, "rc", L)
                b_p.wait(dve, L)
                w_p.wait(dve, L - 1)
                for h in range(2):
                    r = slice(64 * h, 64 * h + 64)
                    b_s.did(dve.tensor_tensor(
                        b3[r], psm[r, 0:64].rearrange("p (q h d) -> p q h d", h=2, d=DH)[:, :, h, :],
                        rc3[r].unsqueeze(2).to_broadcast([64, 4, DH]), ALU.mult), f"b{h}")
                w_p.wait(dve, L)
                o_p.wait(dve, L - 1)
                for h in range(2):
                    r = slice(64 * h, 64 * h + 64)
                    w_s.did(dve.tensor_copy(wbd[r, :, h, :], psm[r, 128:160].rearrange("p (q d) -> p q d", d=DH)),
                            f"w{h}")
                e1.wait(dve, L)
                o_s.wait(dve, "div", L - 2)
                n1.did(dve.tensor_reduce(rc1[g % 2][:], a1[g % 2][:], AX.X, ALU.add), "sum")
                n1.wait(dve, "sum", L)
                n1.did(dve.reciprocal(rc1[g % 2][:], rc1[g % 2][:]), "rc")

            def last(i, g, L):
                o_p.wait(dve, L)
                n1.wait(dve, "rc", L)
                oT_p.wait(dve, L - 1)
                o_s.did(dve.tensor_tensor(ao[:].rearrange("p k (h d) -> p (k h) d", d=DH),
                                          pso[:, 0:128].rearrange("p (n d) -> p n d", d=DH),
                                          rc1[g % 2][:].rearrange("p k h -> p (k h)").unsqueeze(2)
                                          .to_broadcast([128, 2 * H, DH]), ALU.mult), "div")
                o_s.wait(dve, "div", L)
                o_s.did(dve.tensor_tensor(ao[:], ao[:], res[g][:], ALU.add), "res")
                y_p.wait(dve, L)
                sts[g].wait(dve, i - 1)
                y_s.did(dve.tensor_tensor(yo[g][:].rearrange("p k c -> p (k c)"), pso[:, 384:512],
                                          y[g][:].rearrange("p k c -> p (k c)"), ALU.add), "proj")
                y_s.wait(dve, "proj", L)
                y_s.did(dve.tensor_tensor(yo[g][:], yo[g][:], bout[:].unsqueeze(1).to_broadcast([128, 2, C]),
                                          ALU.add), "bias")
            pipeline(dve, B, G, [means, maxima, middle, last])
    c.close()


def moe_gates(nc, a, x_in, gate_out):
    c = Core(nc, "gate8")
    G, K, E = 4, 4, 8
    LANES = T // 512
    KT = LANES * K
    x = [c.sb(f"x{k}", [128, K, C]) for k in range(G)]
    xT = [c.sb(f"xT{k}", [C, K, 128]) for k in range(2)]
    lg = c.sb("lg", [128, LANES, K, E])
    sel = c.sb("sel", [128, KT, E])
    u = c.sb("u", [128, KT, E])
    w = c.sb("w", [128, KT, E])
    m = c.sb("m", [128, KT])
    ident = c.sb("ident", [128, 128])
    gw = c.sb("gw", [C, E])
    gb = c.sb("gb", [128, E])
    pT = c.ps("pT", [C, K, 128])
    pl = c.ps("pl", [128, K, E])
    w_in, turn, dv, ex, st = c.sem("w_in"), c.sem("turn"), c.sem("dve_done"), c.sem("exp_done"), c.sem("st")
    ld = [c.loads(f"ld{k}") for k in range(G)]
    xT_p, xT_s, l_p, l_s = (c.flag(n) for n in ("xT_p", "xT_s", "l_p", "l_s"))
    rows = lambda t: t.rearrange("(l p k) c -> l p k c", p=128, k=K)

    with nc.Block() as block:
        @block.sync
        def _(sp):
            sp.dma_start(ident[:], a["eye"]).then_inc(w_in, 16)
            sp.dma_start(gw[:], a["gate_w"]).then_inc(w_in, 16)
            sp.dma_start(gb[:], a["gate_b"].partition_broadcast(128)).then_inc(w_in, 16)

            def load(i, g, L):
                xT_p.wait(sp, L - G)
                ld[g].inc(sp.dma_start(x[g][:], rows(x_in)[L]))
            pipeline(sp, LANES, G, [load])

        @block.tensor
        def _(pe):
            pe.wait_ge(w_in, 48)

            def tr(i, g, L):
                ld[g].wait(pe, i)
                xT_s.wait(pe, L - 1)
                pe.sem_inc(turn, 1)
                for k in range(K):
                    mm = pe.transpose(pT[:, k, :], x[g][:, k, :], ident[:])
                xT_p.did(mm)

            def logits(i, g, L):
                xT_s.wait(pe, L)
                l_s.wait(pe, L - 1)
                for k in range(K):
                    mm = pe.matmul(pl[:, k, :], xT[g % 2][:, k, :], gw[:], start=True, stop=True)
                l_p.did(mm)
            pipeline(pe, LANES, G, [tr, logits])

        @block.scalar
        def _(act):
            def copy(i, g, L):
                xT_p.wait(act, L)
                l_p.wait(act, L - 2)
                xT_s.did(act.activation(xT[g % 2][:], pT[:], ACT.Copy))
            pipeline(act, LANES, G, [copy])

        @block.vector
        def _(dve):
            dve.wait_ge(w_in, 48)

            def bias(i, g, L):
                l_p.wait(dve, L)
                out = lg[:, L] if isinstance(L, int) else lg[:, bass.ds(L, 1)].rearrange("p a k e -> p (a k) e")
                l_s.did(dve.tensor_tensor(out, pl[:], gb[:].unsqueeze(1).to_broadcast([128, K, E]), ALU.add))
            pipeline(dve, LANES, G, [None, bias])

    with nc.Block() as block:
        s = lg[:].rearrange("p l k e -> p (l k) e")
        rest = {}

        @block.vector
        def _(dve):
            n = [0]

            def link(ins):
                n[0] += 1
                ins.then_inc(dv, 1)
                dve.wait_ge(dv, n[0])

            wide = lambda t: t[:].unsqueeze(2).to_broadcast([128, KT, E])
            link(dve.tensor_reduce(m[:], s, AX.X, ALU.max))
            link(dve.tensor_tensor(s, s, wide(m), ALU.subtract))
            rest["logits"] = n[0]
            dve.wait_ge(ex, 1)
            link(dve.tensor_reduce(m[:], s, AX.X, ALU.add))
            link(dve.reciprocal(m[:], m[:]))
            link(dve.tensor_tensor(s, s, wide(m), ALU.mult))
            best_two(dve, link, s, sel, u, w, m, E, KT)
            link(dve.tensor_tensor(sel[:], sel[:], s, ALU.mult))
            rest["gates"] = n[0]

        @block.scalar
        def _(act):
            act.wait_ge(dv, rest["logits"])
            act.activation(s, s, ACT.Exp).then_inc(ex, 1)

        @block.sync
        def _(sp):
            sp.wait_ge(dv, rest["gates"])
            sp.dma_start(gate_out.rearrange("(l p k) e -> p l (k e)", p=128, k=K),
                         sel[:].rearrange("p (l k) e -> p l (k e)", k=K)).then_inc(st, 16)
            sp.wait_ge(st, 16)
    c.close()


def vit_tower(nc, a, out):
    def dram(name, *shape):
        return nc.dram_tensor(name, shape, F32).ap()

    images = lambda t: t.rearrange("(b p) c -> b p c", b=B)
    h = [dram(f"h{n}", T, C) for n in range(4)]
    gat, dst_rows, top = dram("gat", T, 20), dram("dst_rows", T, 4), dram("top", 128, 4)
    tables = [dram(f"table{n}", ROWS, 20) for n in range(TABLES)]
    gate4, gate8 = dram("gate4", T, 4), dram("gate8", T, 8)
    ya, yb = dram("ya", T, C), dram("yb", T, C)
    qk, a2, zt = dram("qk", B, C, 2, P), dram("a2", B, 128, 4, M), dram("zt", B, 128, 4, M)
    v, res, sums = dram("v", 128, 2, B, C), dram("res", 128, 2, B, C), dram("sums", 128, 2)
    by_image = lambda t: t.rearrange("p k b c -> b p k c")

    tokenizer(nc, a, images(h[0]))
    retention(nc, a, images(h[0]), images(h[1]), gat, dst_rows, top)
    edges(nc, a, a["src_idx"], a["dst_idx"], gat, dst_rows, top, tables)
    gat_gates(nc, a, gat, dst_rows, top, tables, gate4)
    dense(nc, a, "moe4", h[1], h[2], 4, gate=gate4)
    for layer, y in ((0, h[2]), (1, yb)):
        landmarks(nc, a, f"lmk{layer}", layer, y, qk, by_image(v), a2, sums)
        inverse(nc, a, f"inv{layer}", a2, sums, zt)
        convolution(nc, a, f"conv{layer}", layer, v, res)
        attend(nc, a, f"att{layer}", layer, y, qk, by_image(v), zt, by_image(res), ya)
        if layer == 0:
            dense(nc, a, "mlp0", ya, yb, 1, pre=True, post=False)
        else:
            dense(nc, a, "mlp1", ya, h[3], 1, pre=True, extra=h[2])
    moe_gates(nc, a, h[3], gate8)
    dense(nc, a, "moe8", h[3], out, 8, gate=gate8)


def constants():
    d = {}
    eye = np.eye(128)
    d["eye"] = eye
    d["eye16"] = eye[:64, :64] / 16
    d["avg"] = np.kron(np.eye(2), np.full((64, 64), 1 / 64))
    d["ones_bd"] = np.kron(np.eye(2), np.ones((64, 64)))
    d["head_mask"] = np.repeat(np.repeat(np.eye(8), 8, 0), 64, 1)
    two = np.concatenate([np.eye(64)] * 2)
    d["eye2"] = np.tile(two, 4)
    d["eyes"] = np.stack([np.tile(two, 4) * k for k in (7, 15, 13)], 1)
    d["low"] = np.tril(np.ones((128, 128)), -1)
    d["spare_row"] = T + np.arange(128.0)[:, None]
    pos, even = np.arange(float(P)), np.arange(0, C, 2)
    ang = np.float32(pos)[:, None] * np.float32(1.0 / 10000.0 ** (even / C))[None]
    zoom = ((even + 0.4 * C) / (1.4 * C))[None] ** (pos[:, None] / 512.0)
    sign = np.where(np.arange(C) % 2, 1.0, -1.0)[:, None]
    rows = lambda t: np.repeat(t, 2, 1).T
    d["cosT"] = np.concatenate([rows(np.cos(ang) * zoom), rows(np.cos(ang) / zoom)])
    d["sinT"] = np.concatenate([rows(np.sin(ang) * zoom) * sign, rows(np.sin(ang) / zoom) * sign])
    diff = np.arange(P)[None] - np.arange(128)[:, None]
    fade = np.where(diff >= 0, 0.96875 ** np.maximum(diff, 0), 0.0)
    d["decay"] = np.concatenate([fade, fade[:, :128]], 1)
    return {k: v.astype(np.float32) for k, v in d.items()}


def lay_out(i):
    d = constants()
    x = i["x"].reshape(B // 2, 128, 16, 4, 16, 4).transpose(0, 1, 3, 5, 2, 4)
    d["x"] = x.reshape(B // 2, 128, N * P)
    d["wkv_t"] = i["L0_tok_Wkv"].T
    d["wq_t"] = i["L0_tok_Wq"].T
    d["proj_t"] = i["L0_tok_proj_w"].T
    d["proj_b"] = i["L0_tok_proj_b"]
    two = lambda v: np.concatenate([v, v])
    d["tok_ln"] = np.stack([two(i[f"L0_tok_ln_{k}"]) for k in ("kv_w", "q_w", "kv_b", "q_b")], 1)
    wq, wk = i["L0_attn_W_Q"], i["L0_attn_W_K"]
    swap = np.arange(C) ^ 1
    d["wqk"] = np.stack([np.concatenate([wq, wk], 1), np.concatenate([wq[:, swap], wk[:, swap]], 1)], 1)
    d["wv"] = i["L0_attn_W_V"]
    d["w_gat"] = i["L0_ffn_W_gat"]
    d["att_src"], d["att_dst"] = i["L0_ffn_att_src"].reshape(16), i["L0_ffn_att_dst"].reshape(16)
    d["b_gat"], d["gat_g"], d["gat_b"] = i["L0_ffn_b_gat"], i["L0_ffn_ln_gamma"], i["L0_ffn_ln_beta"]
    e = i["L0_ffn_edge_index"].reshape(2, 128, -1, CH).transpose(0, 2, 1, 3)
    d["src_idx"], d["dst_idx"] = e[0], e[1]
    for phase, name in (("moe4", "L0_ffn_"), ("moe8", "L1_ffn_")):
        for n in ("W1", "W2", "b2"):
            d[f"{phase}_{n.lower()}"] = i[name + n]
        d[phase + "_b1"] = i[name + "b1"].T
    for l in range(2):
        for n in ("w1", "w2", "b2"):
            d[f"mlp{l}_{n}"] = i["L1_attn_" + n][l:l + 1]
        d[f"mlp{l}_b1"] = i["L1_attn_b1"][l:l + 1].T
        d[f"mlp{l}_ln"] = np.stack([i["L1_attn_ln2_g"][l], i["L1_attn_ln2_b"][l]], 1)
    d["w_qkv"] = i["L1_attn_w_qkv"].reshape(2, C, 3, C)
    d["ln1"] = np.stack([i["L1_attn_ln1_g"], i["L1_attn_ln1_b"]], 2)
    pad = np.zeros((2, H, 2 * P - 1), np.float32)
    pad[:, :, P - 17:P + 16] = i["L1_attn_res_w"].reshape(2, H, 33)
    at = np.arange(P)[:, None] - np.arange(P)[None] + P - 1
    d["band"] = pad[:, :, at].reshape(2, H, 2, 128, P).transpose(0, 3, 1, 2, 4).reshape(2, 128, H * 2 * P)
    d["w_out"], d["b_out"] = i["L1_attn_w_out"], i["L1_attn_b_out"]
    d["gate_w"], d["gate_b"] = i["L1_ffn_gate_w"], i["L1_ffn_gate_b"]
    return {k: np.ascontiguousarray(v) for k, v in d.items()}


def kernel(**inputs):
    import concourse.bacc as bacc
    from concourse.bass_utils import run_bass_kernel_spmd

    nc = bacc.Bacc("TRN2", target_bir_lowering=False, num_devices=1)
    arrays = lay_out({k: np.asarray(v) for k, v in inputs.items()})
    a = {k: nc.dram_tensor(f"in_{k}", v.shape, mybir.dt.from_np(v.dtype), kind="ExternalInput").ap()
         for k, v in arrays.items()}
    out = nc.dram_tensor("out", (T, C), F32, kind="ExternalOutput").ap()
    vit_tower(nc, a, out)
    r = run_bass_kernel_spmd(nc, [{f"in_{k}": v for k, v in arrays.items()}], core_ids=[0])
    return r.results[0]["out"].reshape(B, P, C)
```

```python
import concourse.bass as bass
from concourse import mybir
from contextlib import ExitStack
import numpy as np

F32 = mybir.dt.float32
I32 = mybir.dt.int32
BF16 = mybir.dt.bfloat16
ALU = mybir.AluOpType
ACT = mybir.ActivationFunctionType
AX = mybir.AxisListType

B, C, P = 128, 64, 256
T = B * P
N = 16
EPS = 1e-5


class Steps:

    def __init__(self, sem, names):
        self.sem, self.names, self.next = sem, names.split(), 0

    def did(self, ins, name):
        assert self.names[self.next % len(self.names)] == name, (name, self.names[self.next % len(self.names)])
        self.next += 1
        return ins.then_inc(self.sem, 1)

    def wait(self, eng, name, lane):
        if isinstance(lane, int) and lane < 0:
            return
        eng.wait_ge(self.sem, lane * len(self.names) + self.names.index(name) + 1)


class Loads:

    def __init__(self, sem, per=1):
        self.sem, self.per = sem, per

    def inc(self, ins):
        return ins.then_inc(self.sem, 16)

    def wait(self, eng, n):
        if isinstance(n, int) and n < 0:
            return
        eng.wait_ge(self.sem, (n + 1) * 16 * self.per)


def rounds(eng, count, body, sem):
    body(0)
    with eng.Fori(1, count) as i:
        body(i)
        eng.wait_ge(sem, 16)


class Core:

    def __init__(self, nc, phase):
        self.nc, self.phase, self.mem, self.held = nc, phase, ExitStack(), []

    def sb(self, name, shape, dt=F32):
        return self.mem.enter_context(self.nc.sbuf_tensor(f"{self.phase}__{name}", shape, dt))

    def ps(self, name, shape, dt=F32):
        return self.mem.enter_context(self.nc.psum_tensor(f"{self.phase}__{name}", shape, dt))

    def sem(self, name):
        self.held.append(self.nc.alloc_semaphore(f"{self.phase}__{name}"))
        return self.held[-1]

    def close(self):
        self.nc.clear_and_free_semaphores(self.held)
        self.nc.all_engine_barrier()
        self.mem.close()

    def steps(self, name, names):
        return Steps(self.sem(name), names)

    def flag(self, name):
        return Flag(self.sem(name))

    def loads(self, name, per=1):
        return Loads(self.sem(name), per)


class Flag:

    def __init__(self, sem):
        self.sem = sem

    def did(self, ins):
        return ins.then_inc(self.sem, 1)

    def wait(self, eng, lane):
        if isinstance(lane, int) and lane < 0:
            return
        eng.wait_ge(self.sem, lane + 1)


def pipeline(eng, lanes, G, stages, look=4, last=None):
    if stages and not isinstance(stages[0], tuple):
        stages = [(d, stage) for d, stage in reversed(list(enumerate(stages))) if stage is not None]
    D = max((d for d, stage in stages), default=0) + 1
    peeled = -(-(D - 1 + look) // G)

    def slot(i, g):
        for d, stage in stages:
            gg, ii = (g - d) % G, i + (g - d) // G
            lane = ii * G + gg
            if isinstance(lane, int) and not 0 <= lane < lanes:
                continue
            stage(ii, gg, lane)

    full = lanes // G
    for s in range(peeled * G):
        slot(s // G, s % G)
    with eng.Fori(peeled, full) as i:
        for g in range(G):
            slot(i, g)
        if last is not None:
            last()
    for s in range(full * G, lanes + D - 1):
        slot(s // G, s % G)


def tokenizer(nc, a, h_out):
    c = Core(nc, "tok")
    LANES, G = B, 8
    x = [c.sb(f"x{k}", [128, N, P]) for k in range(4)]
    x2 = [c.sb(f"x2{k}", [128, N, 128]) for k in range(2)]
    half = c.sb("half", [128, 2048])
    feat = [c.sb(f"feat{k}", [128, P]) for k in range(2)]
    rq = [c.sb(f"rq{k}", [128, 2, 2, C]) for k in range(G)]
    st = c.sb("st", [128, 2, 6])
    mv = c.sb("mv", [128, 2, 2])
    spare = c.sb("spare", [128, 1])
    m2 = c.sb("m2", [128, 32])
    var = [c.sb(f"var{k}", [128, 34]) for k in range(2)]
    nt = c.sb("nt", [128, 34])
    rstd = [c.sb(f"rstd{k}", [128, 34]) for k in range(4)]
    q = c.sb("q", [128, 2, C])
    prod = c.sb("prod", [128, N, 2, C])
    v = [c.sb(f"v{k}", [128, N, 2, C]) for k in range(2)]
    lg = c.sb("lg", [128, N, 2, 8])
    mx = c.sb("mx", [128, 16])
    ex = c.sb("ex", [128, N, 2, 8])
    sm = [c.sb(f"sm{k}", [128, 16]) for k in range(2)]
    w = [c.sb(f"w{k}", [128, N, 2, 8]) for k in range(2)]
    pv = [c.sb(f"pv{k}", [128, N, 2, C]) for k in range(2)]
    rs = c.sb("rs", [128, 16])
    agg = c.sb("agg", [128, 2, C])
    aggT = c.sb("aggT", [128, 128])
    h = [c.sb(f"h{k}", [128, 2, C]) for k in range(4)]
    ident = c.sb("ident", [128, 128])
    avg = c.sb("avg", [128, 128])
    pick = c.sb("pick", [128, 2, N, 4 * N])
    stT = c.sb("stT", [4 * N, 128])
    kvw = c.sb("kvw", [128, 2, 128])
    qrw = c.sb("qrw", [128, 2, 2, C])
    prj = c.sb("prj", [128, 2, C])
    wvec = c.sb("wvec", [128, 4])
    lhs = c.sb("lhs", [128, 128])
    wv_t = c.sb("wv_t", [C, C])
    cvl = c.sb("cvl", [C, 128])
    wq_t = c.sb("wq_t", [C, C])
    cq = c.sb("cq", [128, C])
    cout = c.sb("cout", [128, C])

    pkv = c.ps("pkv", [128, 2, 4, 2, 128])
    pq = c.ps("pq", [128, 512])
    pst = c.ps("pst", [128, 512])
    pt = c.ps("pt", [128, 512])
    pr = c.ps("pr", [128, 512])

    w_in, zeroed, prep, prep_pe, turn = (c.sem(n) for n in ("w_in", "zeroed", "prep", "prep_pe", "turn"))
    x_in = [c.loads(f"x_in{k}") for k in range(4)]
    h_st = [c.loads(f"h_st{k}") for k in range(4)]
    feat_s = c.steps("feat_s", "h0 h1 h2 feat")
    x2_s = c.flag("x2_s")
    st_p, stT_s, q_p, rq_s = c.flag("st_p"), c.flag("stT_s"), c.steps("q_p", "q stats"), c.steps("rq_s", "rq m2")
    var_s, rstd_s = c.steps("var_s", "st0 st1 mv0 mv1 qv var"), c.steps("rstd_s", "y s0 t0 u0 y0 s1 t1 u1 y1 s2 t2 u2 y2")
    kv_p, v_s = c.steps("kv_p", "kv0 kv1 kv2 kv3"), c.steps("v_s", "v0 v1 v2 v3")
    lg_s = c.steps("lg_s", "qm q p0 p1 p2 p3 lg lgs mx lgm")
    ex_s, w_s, pv_s = c.flag("ex_s"), c.steps("w_s", "sum w"), c.flag("pv_s")
    agg_s, aggT_p, aggT_s = c.steps("agg_s", "red rs agg"), c.flag("aggT_p"), c.flag("aggT_s")
    proj_p, h_s = c.flag("proj_p"), c.steps("h_s", "add h")
    NW = 15

    def spot(g):
        return g // 2, slice(128 * (g % 2), 128 * (g % 2) + 128)

    h_pairs = h_out.rearrange("(u b) (k p) c -> u p k b c", b=2, k=2)

    with nc.Block() as block:
        @block.sync
        def _(sp):
            sp.wait_ge(zeroed, 3)
            for k in range(2):
                s = slice(64 * k, 64 * k + 64)
                sp.dma_start(kvw[s, k, :], a["wkv_t"]).then_inc(w_in, 16)
                sp.dma_start(qrw[s, 0, k, :], a["eye16"]).then_inc(w_in, 16)
                sp.dma_start(qrw[s, 1, k, :], a["wq_t"]).then_inc(w_in, 16)
                sp.dma_start(prj[s, k, :], a["proj_t"]).then_inc(w_in, 16)
            sp.dma_start(wvec[:], a["tok_ln"]).then_inc(w_in, 16)
            sp.dma_start(pick[:].rearrange("p t n m -> p (t n m)"), a["pick"]).then_inc(w_in, 16)
            sp.dma_start(ident[:], a["eye"]).then_inc(w_in, 16)
            sp.dma_start(avg[:], a["avg"]).then_inc(w_in, 16)
            sp.dma_start(wq_t[:], a["wq_t"]).then_inc(w_in, 16)
            sp.dma_start(wv_t[:], a["wkv_t"][:, 64:128]).then_inc(w_in, 16)
            sp.dma_start(cout[:], a["proj_b"].partition_broadcast(128)).then_inc(w_in, 16)

            def load(i, g, L):
                if g % 2 == 0:
                    k = g // 2
                    x2_s.wait(sp, L - 7)
                    kv_p.wait(sp, "kv3", L - 7)
                    feat_s.wait(sp, "h0", 4 * i + k - 4)
                    x_in[k].inc(sp.dma_start(x[k][:].rearrange("p n q -> p (n q)"), a["x"][4 * i + k]))
            pipeline(sp, LANES, G, [load], look=8, last=lambda: sp.wait_ge(w_in, 16))

        @block.gpsimd
        def _(pool):
            def feats(i, g, L):
                k, F = g // 2, 4 * i + g // 2
                xk = x[k][:].rearrange("p n q -> p (n q)")
                if g % 2 == 0:
                    feat_s.wait(pool, "feat", F - 1)
                    x_in[k].wait(pool, i)
                    feat_s.did(pool.tensor_tensor(half[:], xk[:, 0:2048], xk[:, 2048:4096], ALU.add), "h0")
                    return
                feat_s.wait(pool, "h0", F)
                feat_s.did(pool.tensor_tensor(half[:, 0:1024], half[:, 0:1024], half[:, 1024:2048], ALU.add), "h1")
                feat_s.wait(pool, "h1", F)
                feat_s.did(pool.tensor_tensor(half[:, 0:512], half[:, 0:512], half[:, 512:1024], ALU.add), "h2")
                feat_s.wait(pool, "h2", F)
                q_p.wait(pool, "q", L - 4)
                feat_s.did(pool.tensor_tensor(feat[k % 2][:], half[:, 0:256], half[:, 256:512], ALU.add), "feat")

            def rsqrt(i, g, L):
                vr, y = var[g % 2], rstd[g % 4]
                var_s.wait(pool, "var", L)
                w_s.wait(pool, "w", L - 4)
                pool.sem_inc(turn, 1)
                rstd_s.did(pool.tensor_scalar(y[:].bitcast(I32), vr[:].bitcast(I32), -0.5, 1597463007.0,
                                              ALU.mult, ALU.add), "y")
                for n in range(3):
                    rstd_s.wait(pool, f"y{n - 1}" if n else "y", L)
                    rstd_s.did(pool.tensor_tensor(nt[:], y[:], y[:], ALU.mult), f"s{n}")
                    rstd_s.wait(pool, f"s{n}", L)
                    rstd_s.did(pool.tensor_tensor(nt[:], nt[:], vr[:], ALU.mult), f"t{n}")
                    rstd_s.wait(pool, f"t{n}", L)
                    pool.sem_inc(turn, 1)
                    rstd_s.did(pool.tensor_scalar(nt[:], nt[:], -0.5, 1.5, ALU.mult, ALU.add), f"u{n}")
                    rstd_s.wait(pool, f"u{n}", L)
                    rstd_s.did(pool.tensor_tensor(y[:], y[:], nt[:], ALU.mult), f"y{n}")

            def weigh(i, g, L):
                w_s.wait(pool, "w", L)
                v_s.wait(pool, "v3", L)
                agg_s.wait(pool, "red", L - 2)
                pv_s.did(pool.tensor_tensor(
                    pv[g % 2][:].rearrange("p n b (h d) -> p (n b h) d", d=8),
                    v[g % 2][:].rearrange("p n b (h d) -> p (n b h) d", d=8),
                    w[g % 2][:].rearrange("p n b h -> p (n b h)").unsqueeze(2).to_broadcast([128, 256, 8]),
                    ALU.mult))
            pipeline(pool, LANES, G, [feats, None, None, rsqrt, None, weigh], look=8)

        @block.scalar
        def _(act):
            act.wait_ge(prep, 7)

            def squares(i, g, L):
                k, s = spot(g)
                x_in[k].wait(act, i)
                st_p.wait(act, L - 2)
                x2_s.did(act.activation(x2[g % 2][:], x[k][:, :, s], ACT.Square))

            def query(i, g, L):
                q_p.wait(act, "stats", L)
                h_s.wait(act, "add", L - G)
                rq_s.did(act.activation(rq[g][:].rearrange("p t b c -> p (t b c)"), pq[:, 0:256], ACT.Copy), "rq")
                var_s.wait(act, "var", L - 1)
                rq_s.did(act.activation(m2[:], pq[:, 256:288], ACT.Square), "m2")

            def stats(i, g, L):
                st_p.wait(act, L)
                q_p.wait(act, "stats", L - 1)
                stT_s.did(act.activation(stT[:], pst[0:64, 0:128], ACT.Copy))

            def values(i, g, L):
                pv_s.wait(act, L - 2)
                for j in range(4):
                    kv_p.wait(act, f"kv{j}", L)
                    v_s.did(act.activation(v[g % 2][:, 4 * j:4 * j + 4], pkv[:, j % 2, :, :, 64:128], ACT.Copy),
                            f"v{j}")

            def exps(i, g, L):
                lg_s.wait(act, "lgm", L)
                w_s.wait(act, "w", L - 1)
                ex_s.did(act.activation(ex[:].rearrange("p n b h -> p (n b h)"),
                                        lg[:].rearrange("p n b h -> p (n b h)"), ACT.Exp))

            def turned(i, g, L):
                aggT_p.wait(act, L)
                proj_p.wait(act, L - 1)
                aggT_s.did(act.activation(aggT[:], pt[:, 0:128], ACT.Copy))

            def store(i, g, L):
                h_s.wait(act, "h", L)
                h_st[g % 4].inc(act.dma_start(h_pairs[4 * i + g // 2, :, g % 2], h[g % 4][:]))
            pipeline(act, LANES, G, [(5, exps), (4, values), (7, turned), (9, store), (2, query), (0, squares), (1, stats)],
                     look=7)
            for k in range(4):
                h_st[k].wait(act, LANES // 4 - 1)

        @block.vector
        def _(dve):
            dve.memset(kvw[:], 0.0).then_inc(zeroed, 1)
            dve.memset(qrw[:], 0.0).then_inc(zeroed, 1)
            dve.memset(prj[:], 0.0).then_inc(zeroed, 1)
            dve.wait_ge(w_in, 16 * NW)
            dve.tensor_scalar(kvw[:], kvw[:], wvec[:, 0:1], None, ALU.mult).then_inc(prep, 1)
            dve.tensor_scalar(qrw[:, 1], qrw[:, 1], wvec[:, 1:2], 1 / 128, ALU.mult, ALU.mult).then_inc(prep, 1)
            dve.tensor_copy(lhs[0:64, :], wvec[0:64, 3:4].to_broadcast([64, 128])).then_inc(prep, 1)
            dve.wait_ge(prep_pe, 4)
            dve.tensor_tensor(kvw[:].rearrange("p b n -> p (b n)"), kvw[:].rearrange("p b n -> p (b n)"),
                              pkv[:, 0, 0].rearrange("p b n -> p (b n)"), ALU.subtract).then_inc(prep, 1)
            dve.tensor_tensor(qrw[:, 1].rearrange("p b n -> p (b n)"), qrw[:, 1].rearrange("p b n -> p (b n)"),
                              pst[:, 0:128], ALU.subtract).then_inc(prep, 1)
            dve.tensor_scalar(cq[:], pq[:, 0:64], 0.125, None, ALU.mult).then_inc(prep, 1)
            dve.tensor_copy(cvl[:], pt[0:64, 0:1].to_broadcast([64, 128])).then_inc(prep, 1)
            dve.wait_ge(prep_pe, 5)
            dve.tensor_tensor(cout[:], cout[:], pq[:, 0:64], ALU.add).then_inc(prep, 1)

            def variances(i, g, L):
                rq_s.wait(dve, "rq", L)
                for b in range(2):
                    var_s.did(dve.bn_stats(st[:, b, :], rq[g][:, 0, b, :]), f"st{b}")
                var_s.wait(dve, "st1", L)
                dve.memset(spare[:], 0.0)
                for b in range(2):
                    var_s.did(dve.bn_aggr(mv[:, b, :], st[:, b, :]), f"mv{b}")
                var_s.wait(dve, "mv1", L)
                rstd_s.wait(dve, "y2", L - 2)
                var_s.did(dve.tensor_scalar(var[g % 2][:, 0:2], mv[:, :, 1], EPS, None, ALU.add), "qv")
                rq_s.wait(dve, "m2", L)
                var_s.did(dve.scalar_tensor_tensor(var[g % 2][:, 2:34], pq[:, 288:320], EPS, m2[:],
                                                   ALU.add, ALU.subtract), "var")

            over_n = lambda t: t[:].rearrange("p n b h -> p (b h) n")
            flat = lambda t: t[:].rearrange("p n b h -> p (n b) h")
            pixels = lambda g: rstd[g % 4][:, 2:34].unsqueeze(2).to_broadcast([128, 32, 8])

            def query(i, g, L):
                rstd_s.wait(dve, "y2", L)
                lg_s.did(dve.tensor_tensor(q[:], rq[g][:, 1], rstd[g % 4][:, 0:2].unsqueeze(2)
                                           .to_broadcast([128, 2, C]), ALU.mult), "qm")
                lg_s.wait(dve, "qm", L)
                lg_s.did(dve.tensor_tensor(q[:], q[:], cq[:].unsqueeze(1).to_broadcast([128, 2, C]), ALU.add), "q")
                lg_s.wait(dve, "q", L)
                products(L, 0)
                products(L, 1)

            def products(L, j):
                v_s.wait(dve, f"v{j}", L)
                lg_s.did(dve.tensor_tensor(prod[:, 4 * j:4 * j + 4], pkv[:, j % 2, :, :, 0:64],
                                           q[:].unsqueeze(1).to_broadcast([128, 4, 2, C]), ALU.mult), f"p{j}")

            def logits(i, g, L):
                products(L, 2)
                products(L, 3)
                lg_s.wait(dve, "p3", L)
                ex_s.wait(dve, L - 1)
                lg_s.did(dve.tensor_reduce(lg[:].rearrange("p n b h -> p (n b h)"),
                                           prod[:].rearrange("p n b (h d) -> p (n b h) d", d=8),
                                           AX.X, ALU.add), "lg")
                lg_s.wait(dve, "lg", L)
                lg_s.did(dve.tensor_tensor(flat(lg), flat(lg), pixels(g), ALU.mult), "lgs")
                lg_s.wait(dve, "lgs", L)
                lg_s.did(dve.tensor_reduce(mx[:], over_n(lg), AX.X, ALU.max), "mx")
                lg_s.wait(dve, "mx", L)
                lg_s.did(dve.tensor_tensor(lg[:].rearrange("p n b h -> p n (b h)"),
                                           lg[:].rearrange("p n b h -> p n (b h)"),
                                           mx[:].unsqueeze(1).to_broadcast([128, N, 16]), ALU.subtract), "lgm")

            def weights(i, g, L):
                ex_s.wait(dve, L)
                agg_s.wait(dve, "rs", L - 2)
                w_s.did(dve.tensor_reduce(sm[g % 2][:], over_n(ex), AX.X, ALU.add), "sum")
                pv_s.wait(dve, L - 2)
                w_s.did(dve.tensor_tensor(flat(w[g % 2]), flat(ex), pixels(g), ALU.mult), "w")

            def gather(i, g, L):
                w_s.wait(dve, "sum", L)
                agg_s.wait(dve, "agg", L - 1)
                pv_s.wait(dve, L)
                aggT_p.wait(dve, L - 1)
                agg_s.did(dve.tensor_reduce(agg[:].rearrange("p b c -> p (b c)"),
                                            pv[g % 2][:].rearrange("p n b c -> p (b c) n"), AX.X, ALU.add), "red")
                agg_s.did(dve.reciprocal(rs[:], sm[g % 2][:]), "rs")
                agg_s.wait(dve, "rs", L)
                agg_s.did(dve.tensor_tensor(agg[:].rearrange("p b (h d) -> p (b h) d", d=8),
                                            agg[:].rearrange("p b (h d) -> p (b h) d", d=8),
                                            rs[:].unsqueeze(2).to_broadcast([128, 16, 8]), ALU.mult), "agg")

            def result(i, g, L):
                k = g % 4
                proj_p.wait(dve, L)
                h_st[k].wait(dve, (L - 4) // 4 if isinstance(L, int) else 2 * i + g // 4 - 1)
                h_s.did(dve.tensor_tensor(h[k][:].rearrange("p b c -> p (b c)"), pr[:, 0:128],
                                          rq[g][:, 0].rearrange("p b c -> p (b c)"), ALU.add), "add")
                h_s.wait(dve, "add", L)
                h_s.did(dve.tensor_tensor(h[k][:], h[k][:], cout[:].unsqueeze(1).to_broadcast([128, 2, C]),
                                          ALU.add), "h")
            pipeline(dve, LANES, G, [(4, query), (5, weights), (8, result), (6, gather), (4, logits), (2, variances)],
                     look=8)

        @block.tensor
        def _(pe):
            pe.wait_ge(prep, 3)
            pe.matmul(pkv[:, 0, 0].rearrange("p b n -> p (b n)"), avg[:], kvw[:].rearrange("p b n -> p (b n)"),
                      start=True, stop=True).then_inc(prep_pe, 1)
            pe.matmul(pst[:, 0:128], avg[:], qrw[:, 1].rearrange("p b n -> p (b n)"), start=True, stop=True)\
              .then_inc(prep_pe, 1)
            pe.matmul(pq[:, 0:64], lhs[0:64, :], wq_t[:], start=True, stop=True).then_inc(prep_pe, 1)
            pe.matmul(pt[0:64, 0:1], wv_t[:], wvec[0:64, 2:3], start=True, stop=True).then_inc(prep_pe, 1)
            pe.wait_ge(prep, 7)
            pe.matmul(pq[:, 0:64], cvl[:], prj[0:64, 0, :], start=True, stop=True).then_inc(prep_pe, 1)
            pe.wait_ge(prep, 8)

            def query(i, g, L):
                k, s = spot(g)
                feat_s.wait(pe, "feat", 4 * i + k)
                rq_s.wait(pe, "rq", L - 1)
                var_s.wait(pe, "var", L - 1)
                q_p.did(pe.matmul(pq[:, 0:256], feat[k % 2][:, s], qrw[:].rearrange("p t b n -> p (t b n)"),
                                  start=True, stop=True), "q")
                stT_s.wait(pe, L)
                pe.sem_inc(turn, 1)
                q_p.did(pe.transpose(pq[:, 256:320], stT[:], ident[0:64, 0:64]), "stats")

            def stats(i, g, L):
                k, s = spot(g)
                x_in[k].wait(pe, i)
                x2_s.wait(pe, L)
                stT_s.wait(pe, L - 1)
                for t, src in enumerate((x[k][:, :, s], x2[g % 2][:])):
                    for n in range(N):
                        mm = pe.matmul(pst[0:64, 0:128], pick[:, t, n], src[:, n], start=t + n == 0,
                                       stop=t + n == N)
                st_p.did(mm)

            def keys_values(i, g, L):
                k, s = spot(g)
                for j in range(4):
                    at, other = (L, j - 2) if j >= 2 else (L - 1, j + 2)
                    v_s.wait(pe, f"v{other}", at)
                    lg_s.wait(pe, f"p{other}", at)
                    for n in range(4):
                        mm = pe.matmul(pkv[:, j % 2, n].rearrange("p b n -> p (b n)"), x[k][:, 4 * j + n, s],
                                       kvw[:].rearrange("p b n -> p (b n)"), start=True, stop=True)
                    kv_p.did(mm, f"kv{j}")

            def turned(i, g, L):
                agg_s.wait(pe, "agg", L)
                aggT_s.wait(pe, L - 1)
                aggT_p.did(pe.transpose(pt[:, 0:128], agg[:].rearrange("p b c -> p (b c)"), ident[:]))

            def project(i, g, L):
                aggT_s.wait(pe, L)
                h_s.wait(pe, "add", L - 1)
                proj_p.did(pe.matmul(pr[:, 0:128], aggT[:], prj[:].rearrange("p b n -> p (b n)"),
                                     start=True, stop=True))
            pipeline(pe, LANES, G, [(8, project), (4, keys_values), (7, turned), (2, query), (1, stats)], look=8)
    c.close()


def retention(nc, a, h_in, h_out, gat_out, dst_out, top_out):
    c = Core(nc, "ret")
    G = 8
    h = [c.sb(f"h{k}", [128, 2, C]) for k in range(G)]
    hT = [c.sb(f"hT{k}", [128, 128]) for k in range(2)]
    ca = c.sb("ca", [128, P])
    sa = c.sb("sa", [128, P])
    qt = [c.sb(f"qt{k}", [C, P]) for k in range(2)]
    kt = [c.sb(f"kt{k}", [C, P]) for k in range(2)]
    v = [c.sb(f"v{k}", [128, 2, C]) for k in range(G)]
    ret = [c.sb(f"ret{k}", [128, 384]) for k in range(2)]
    s = [c.sb(f"s{k}", [128, 2, C]) for k in range(2)]
    st = c.sb("st", [128, 2, 6])
    mv = [c.sb(f"mv{k}", [128, 2, 2]) for k in range(2)]
    ve = c.sb("ve", [128, 2])
    rstd = [c.sb(f"rstd{k}", [128, 2]) for k in range(2)]
    y = [c.sb(f"y{k}", [128, 2, C]) for k in range(G)]
    yT = [c.sb(f"yT{k}", [128, 128]) for k in range(2)]
    gt = [c.sb(f"gt{k}", [128, 2, 24]) for k in range(G)]
    top = c.sb("top", [128, 4])
    pair = c.sb("pair", [128, 4])
    mh = c.sb("mh", [128, 2])
    spare = c.sb("spare", [128, 1])
    ident = c.sb("ident", [128, 128])
    wqk = c.sb("wqk", [128, 2, 128])
    wv = c.sb("wv", [128, C])
    cosT = c.sb("cosT", [128, P])
    sinT = c.sb("sinT", [128, P])
    decay = c.sb("decay", [128, 384])
    wg = c.sb("wg", [128, 24])
    att = c.sb("att", [128, 2, 16])
    wa = c.sb("wa", [128, 2, 16])

    phT = c.ps("phT", [128, 512])
    pqk = c.ps("pqk", [128, 2, 512])
    pr = c.ps("pr", [128, 512])
    po = c.ps("po", [128, 512])
    pyT = c.ps("pyT", [128, 512])
    pg = c.ps("pg", [128, 2, 512])

    w_in, prep, mh_set = c.sem("w_in"), c.sem("prep"), c.sem("mh_set")
    h_ld = [c.loads(f"h_ld{k}") for k in range(G)]
    st_h = [c.loads(f"st_h{k}") for k in range(G)]
    st_g = [c.loads(f"st_g{k}", 2) for k in range(G)]
    hT_p, hT_s = c.flag("hT_p"), c.flag("hT_s")
    qkv_p, rope = c.flag("qkv_p"), c.steps("rope", "ca sa v qt kt")
    ret_p, ret_s, out_p = c.flag("ret_p"), c.flag("ret_s"), c.flag("out_p")
    norm, rs_s, y_s = c.steps("norm", "s st0 st1 mv0 mv1 ve"), c.flag("rs_s"), c.steps("y_s", "y0 y1")
    yT_p, yT_s, g_p, g_s = c.flag("yT_p"), c.flag("yT_s"), c.flag("g_p"), c.steps("g_s", "gt pair top")
    h_view = h_in.rearrange("b (k p) c -> b p k c", p=128)
    ho_view = h_out.rearrange("b (k p) c -> b p k c", p=128)
    go_view = gat_out.rearrange("(b k p) c -> b p k c", p=128, k=2)
    do_view = dst_out.rearrange("(b k p) c -> b p k c", p=128, k=2)
    NW = 12

    with nc.Block() as block:
        @block.sync
        def _(sp):
            for dst, src in ((ident, "eye"), (cosT, "cosT"), (sinT, "sinT"),
                             (decay, "decay")):
                sp.dma_start(dst[:], a[src]).then_inc(w_in, 16)
            for k in range(2):
                half = slice(64 * k, 64 * k + 64)
                sp.dma_start(wqk[half], a["wqk"]).then_inc(w_in, 16)
                sp.dma_start(wv[half], a["wv"]).then_inc(w_in, 16)
                sp.dma_start(wg[half, 0:16], a["w_gat"]).then_inc(w_in, 16)
            sp.dma_start(att[:, 0, :], a["att_src"].partition_broadcast(128)).then_inc(w_in, 16)
            sp.dma_start(att[:, 1, :], a["att_dst"].partition_broadcast(128)).then_inc(w_in, 16)

            def load(i, g, L):
                norm.wait(sp, "s", L - G)
                h_ld[g].inc(sp.dma_start(h[g][:], h_view[L]))

            def store(i, g, L):
                y_s.wait(sp, "y1", L)
                st_h[g].inc(sp.dma_start(ho_view[L], y[g][:]))
                g_s.wait(sp, "top", L)
                st_g[g].inc(sp.dma_start(go_view[L], gt[g][:, :, 0:20]))
                st_g[g].inc(sp.dma_start(do_view[L], gt[g][:, :, 20:24]))
            pipeline(sp, B, G, [(0, load), (11, store)], look=8)
            for g in range(G):
                st_h[g].wait(sp, B // G - 1)
                st_g[g].wait(sp, B // G - 1)
            sp.dma_start(top_out, top[:]).then_inc(w_in, 16)
            sp.wait_ge(w_in, 16 * NW + 16)

        @block.tensor
        def _(pe):
            pe.wait_ge(w_in, 16 * NW)
            pe.wait_ge(prep, 3)

            def tr(i, g, L):
                h_ld[g].wait(pe, i)
                hT_s.wait(pe, L - 1)
                hT_p.did(pe.transpose(phT[:, 0:128], h[g][:].rearrange("p k c -> p (k c)"), ident[:]))

            def qkv(i, g, L):
                hT_s.wait(pe, L)
                rope.wait(pe, "v", L - 1)
                for k in range(2):
                    half = slice(64 * k, 64 * k + 64)
                    for t in range(2):
                        pe.matmul(pqk[:, k, 128 * t:128 * t + 128], wqk[half, t, :], hT[g % 2][half, :],
                                  start=True, stop=True)
                    mm = pe.matmul(pqk[:, k, 256:320], hT[g % 2][half, :], wv[half, :], start=True, stop=True)
                    qkv_p.did(mm)

            def scores(i, g, L):
                rope.wait(pe, "kt", L)
                ret_s.wait(pe, L - 1)
                pe.matmul(pr[:, 0:256], kt[g % 2][:, 0:128], qt[g % 2][:], start=True, stop=True)
                ret_p.did(pe.matmul(pr[:, 256:384], kt[g % 2][:, 128:256], qt[g % 2][:, 128:256],
                                    start=True, stop=True))

            def out(i, g, L):
                ret_s.wait(pe, L)
                norm.wait(pe, "s", L - 1)
                r = ret[g % 2]
                pe.matmul(po[:, 0:64], r[:, 0:128], v[g][:, 0, :], start=True, stop=True)
                pe.matmul(po[:, 64:128], r[:, 128:256], v[g][:, 0, :], start=True, stop=False)
                out_p.did(pe.matmul(po[:, 64:128], r[:, 256:384], v[g][:, 1, :], start=False, stop=True))

            def tr_y(i, g, L):
                y_s.wait(pe, "y1", L)
                yT_s.wait(pe, L - 1)
                yT_p.did(pe.transpose(pyT[:, 0:128], y[g][:].rearrange("p k c -> p (k c)"), ident[:]))

            def gat(i, g, L):
                yT_s.wait(pe, L)
                g_s.wait(pe, "top", L - 1)
                for k in range(2):
                    mm = pe.matmul(pg[:, k, 0:24], yT[g % 2][64 * k:64 * k + 64, :], wg[64 * k:64 * k + 64, :],
                                   start=True, stop=True)
                    g_p.did(mm)
            pipeline(pe, B, G, [(3, scores), (5, out), (8, tr_y), (1, qkv), (0, tr), (9, gat)], look=8)

        @block.scalar
        def _(act):
            def copy_hT(i, g, L):
                hT_p.wait(act, L)
                qkv_p.wait(act, 2 * (L - 2) + 1)
                hT_s.did(act.activation(hT[g % 2][:], phT[:, 0:128], ACT.Copy))

            def copy_yT(i, g, L):
                yT_p.wait(act, L)
                g_p.wait(act, 2 * (L - 2) + 1)
                yT_s.did(act.activation(yT[g % 2][:], pyT[:, 0:128], ACT.Copy))
            pipeline(act, B, G, [(0, copy_hT), (8, copy_yT)], look=8)

        @block.gpsimd
        def _(pool):
            pool.memset(mh[:], -0.5).then_inc(mh_set, 1)
            pool.wait_ge(mh_set, 1)

            def rs(i, g, L):
                norm.wait(pool, "ve", L)
                y_s.wait(pool, "y1", L - 2)
                rs_s.did(pool.tensor_tensor(rstd[g % 2][:], ve[:], mh[:], ALU.pow))
            pipeline(pool, B, G, [(6, rs)], look=8)

        @block.vector
        def _(dve):
            dve.wait_ge(w_in, 16 * NW)
            dve.tensor_tensor(wa[:], wg[:, 0:16].unsqueeze(1).to_broadcast([128, 2, 16]), att[:], ALU.mult)\
               .then_inc(prep, 1)
            dve.wait_ge(prep, 1)
            dve.tensor_reduce(wg[:, 16:24], wa[:].rearrange("p t (h e) -> p (t h) e", e=4), AX.X, ALU.add)\
               .then_inc(prep, 1)
            dve.memset(top[:], -3.0e38).then_inc(prep, 1)
            dve.wait_ge(prep, 3)

            halves = lambda t: t[:].rearrange("p (k q) -> p k q", k=2)

            def ropes(i, g, L):
                qkv_p.wait(dve, 2 * L + 1)
                rope.wait(dve, "kt", L - 1)
                rope.did(dve.tensor_tensor(halves(ca), pqk[:, :, 0:128], halves(cosT), ALU.mult), "ca")
                rope.did(dve.tensor_tensor(halves(sa), pqk[:, :, 128:256], halves(sinT), ALU.mult), "sa")
                out_p.wait(dve, L - G)
                rope.did(dve.tensor_copy(v[g][:], pqk[:, :, 256:320]), "v")
                rope.wait(dve, "sa", L)
                ret_p.wait(dve, L - 2)
                rope.did(dve.tensor_tensor(qt[g % 2][:], ca[0:64, :], sa[0:64, :], ALU.add), "qt")
                rope.did(dve.tensor_tensor(kt[g % 2][:], ca[64:128, :], sa[64:128, :], ALU.add), "kt")

            def decays(i, g, L):
                ret_p.wait(dve, L)
                out_p.wait(dve, L - 2)
                ret_s.did(dve.tensor_tensor(ret[g % 2][:], pr[:, 0:384], decay[:], ALU.mult))

            def stats(i, g, L):
                out_p.wait(dve, L)
                y_s.wait(dve, "y1", L - 2)
                norm.did(dve.tensor_tensor(s[g % 2][:].rearrange("p k c -> p (k c)"), po[:, 0:128],
                                           h[g][:].rearrange("p k c -> p (k c)"), ALU.add), "s")
                norm.wait(dve, "s", L)
                for k in range(2):
                    norm.did(dve.bn_stats(st[:, k, :], s[g % 2][:, k, :]), f"st{k}")
                norm.wait(dve, "st1", L)
                dve.memset(spare[:], 0.0)
                for k in range(2):
                    norm.did(dve.bn_aggr(mv[g % 2][:, k, :], st[:, k, :]), f"mv{k}")
                norm.wait(dve, "mv1", L)
                rs_s.wait(dve, L - 1)
                norm.did(dve.tensor_scalar(ve[:], mv[g % 2][:, :, 1], EPS, None, ALU.add), "ve")

            def finish(i, g, L):
                rs_s.wait(dve, L)
                st_h[g].wait(dve, i - 1)
                yT_p.wait(dve, L - G)
                for k in range(2):
                    y_s.did(dve.tensor_scalar(y[g][:, k, :], s[g % 2][:, k, :], mv[g % 2][:, k, 0:1],
                                              rstd[g % 2][:, k:k + 1], ALU.subtract, ALU.mult), f"y{k}")

            def gats(i, g, L):
                g_p.wait(dve, 2 * L + 1)
                st_g[g].wait(dve, i - 1)
                g_s.did(dve.tensor_copy(gt[g][:], pg[:, :, 0:24]), "gt")
                g_s.wait(dve, "gt", L)
                g_s.did(dve.tensor_tensor(pair[:], gt[g][:, 0, 16:20], gt[g][:, 1, 16:20], ALU.max), "pair")
                g_s.wait(dve, "pair", L)
                g_s.did(dve.tensor_tensor(top[:], top[:], pair[:], ALU.max), "top")
            pipeline(dve, B, G, [(4, decays), (6, stats), (2, ropes), (10, gats), (7, finish)], look=8)
    c.close()


TABLES = 4
ROWS = T + 128
CH = 16


def edges(nc, a, src_idx, dst_idx, gat, dst_rows, top, tables):
    c = Core(nc, "edge")
    G, E = 4, src_idx.shape[0] * src_idx.shape[1] * src_idx.shape[2]
    LANES = E // (128 * CH)
    si = [c.sb(f"si{k}", [128, CH], I32) for k in range(G)]
    di = [c.sb(f"di{k}", [128, CH], I32) for k in range(G)]
    df = [c.sb(f"df{k}", [128, CH]) for k in range(G)]
    gs = [c.sb(f"gs{k}", [128, CH, 20]) for k in range(G)]
    gd = [c.sb(f"gd{k}", [128, CH, 4]) for k in range(G)]
    eq = [c.sb(f"eq{k}", [128, CH, 128]) for k in range(G)]
    low = c.sb("low", [128, 4, 128])
    eql = c.sb("eql", [128, 4, 128])
    cnt = [c.sb(f"cnt{k}", [128, CH]) for k in range(G)]
    hi_i, lo_i = c.sb("hi_i", [128, CH], I32), c.sb("lo_i", [128, CH], I32)
    hi, lo = c.sb("hi", [128, CH]), c.sb("lo", [128, CH])
    row_no = c.sb("row_no", [128, 2])
    col_no = c.sb("col_no", [128, 128])
    hot = [c.sb(f"hot{k}", [128, 2, 4, 128], BF16) for k in range(2)]
    mlo = [c.sb(f"mlo{k}", [128, 4, 128]) for k in range(2)]
    pick = [c.sb(f"pick{k}", [128, 4, 128]) for k in range(2)]
    dst_rd = c.sb("dst_rd", [128, 2, 128, 4])
    left = c.sb("left", [128, 2, 4, 128])
    part = [c.sb(f"part{k}", [128, 2, 4, 128], BF16) for k in range(3)]
    first = c.sb("first", [128, CH])
    tgt = c.sb("tgt", [128, CH])
    ti = [c.sb(f"ti{k}", [128, CH], I32) for k in range(G)]
    z = c.sb("z", [128, CH, 4])
    mz = c.sb("mz", [128, CH, 4])
    ml = c.sb("ml", [128, CH, 4])
    pay = [c.sb(f"pay{k}", [128, CH, 20]) for k in range(G)]
    comb = [c.sb(f"comb{k}", [128, CH, 20]) for k in range(G)]
    ident = c.sb("ident", [128, 128])
    spare_row = c.sb("spare_row", [128, 1])
    tops = c.sb("tops", [128, 128, 4])
    big = c.sb("big", [128, 4])
    zero = c.sb("zero", [128, ROWS * 20 // 128])
    pd = c.ps("pd", [128, 4, 128])
    ph = [c.ps(f"ph{k}", [128, 4, 128]) for k in range(2)]
    pk = [c.ps(f"pk{k}", [128, 4, 128]) for k in range(2)]
    pc = [c.ps(f"pc{k}", [128, CH, 20]) for k in range(2)]

    turn = c.sem("turn")
    w_in, w_ok, zeroed = c.sem("w_in"), c.sem("w_ok"), c.sem("zeroed")
    idx_in = [c.loads(f"idx_in{k}", 2) for k in range(G)]
    src_in = [c.loads(f"src_in{k}", CH) for k in range(G)]
    added = [c.loads(f"added{k}") for k in range(TABLES)]
    split, cast = c.sem("split"), c.steps("cast", "df hi_i lo_i hi lo")
    hot_s = c.steps("hot_s", " ".join(f"a{q} b{q} m{q}" for q in range(4)))
    ph_p, pk_p, pick_s, gd_s = c.flag("ph_p"), c.flag("pk_p"), c.flag("pick_s"), c.flag("gd_s")
    pd_p, eqs = c.flag("pd_p"), c.steps("eqs", " ".join(f"eq{q} el{q} cn{q}" for q in range(4)))
    rows = c.steps("rows", "first d m t i")
    lgt = c.steps("lgt", "z l mz ml sub")
    exp_s, pay_s, pc_p, comb_s = c.flag("exp_s"), c.flag("pay_s"), c.flag("pc_p"), c.flag("comb_s")

    NW = 6
    bank = lambda q, j: j % 2

    with nc.Block() as block:
        @block.sync
        def _(sp):
            sp.dma_start(ident[:], a["eye"]).then_inc(w_in, 16)
            sp.dma_start(low[:, 0, :], a["low"]).then_inc(w_in, 16)
            sp.dma_start(spare_row[:], a["spare_row"]).then_inc(w_in, 16)
            sp.dma_start(tops[:].rearrange("p a h -> p (a h)"),
                         top.rearrange("p h -> (p h)").partition_broadcast(128)).then_inc(w_in, 16)
            sp.dma_start(col_no[:], a["col_no"].partition_broadcast(128)).then_inc(w_in, 16)
            sp.dma_start(dst_rd[:], dst_rows.rearrange("(u p l) h -> p u l h", u=2, p=128)).then_inc(w_in, 16)
            sp.wait_ge(w_ok, 1)
            for table in tables:
                sp.dma_start(table.rearrange("(p r) n -> p (r n)", p=128), zero[:]).then_inc(zeroed, 16)

            def load(i, g, L):
                cast.wait(sp, "lo_i", L - G)
                src_in[g].wait(sp, i - 1)
                idx_in[g].inc(sp.dma_start(si[g][:], src_idx[L]))
                idx_in[g].inc(sp.dma_start(di[g][:], dst_idx[L]))
            pipeline(sp, LANES, G, [load], last=lambda: sp.wait_ge(w_in, 16))
            for t in range(TABLES):
                added[t].wait(sp, LANES * CH // TABLES - 1)

        @block.gpsimd
        def _(pool):
            pool.wait_ge(zeroed, 16 * TABLES)

            def gather(g, j):
                src_in[g].inc(pool.indirect_dma_start(
                    out=gs[g][:, j, :], out_offset=None, in_=gat,
                    in_offset=bass.IndirectOffsetOnAxis(ap=si[g][:, j:j + 1], axis=0),
                    bounds_check=T - 1, oob_is_err=True))

            def gathers(i, g, L):
                idx_in[g].wait(pool, i)
                pay_s.wait(pool, L - G)
                pool.sem_inc(turn, 1)
                for j in range(CH):
                    gather(g, j)

            def scatters(i, g, L):
                comb_s.wait(pool, L)
                rows.wait(pool, "i", L)
                for j in range(CH):
                    t, n = j % TABLES, j // TABLES
                    per = CH // TABLES
                    k = L * per + n - 1
                    if not (isinstance(k, int) and k < 0):
                        pool.wait_ge(added[t].sem, (L * per + n) * 16)
                        pool.sem_inc(turn, 1)
                    added[t].inc(pool.indirect_dma_start(
                        out=tables[t], out_offset=bass.IndirectOffsetOnAxis(ap=ti[g][:, j:j + 1], axis=0),
                        in_=comb[g][:, j, :], in_offset=None,
                        compute_op=ALU.add, bounds_check=ROWS - 1, oob_is_err=True))
            pipeline(pool, LANES, G, [(4, scatters), (0, gathers)])

        @block.tensor
        def _(pe):
            pe.wait_ge(w_in, 16 * NW)
            pe.wait_ge(split, 7)

            def spread(g, L, q):
                cast.wait(pe, "hi", L)
                hot_s.wait(pe, f"b{(q - 2) % 4}", L if q >= 2 else L - 1)
                for j in range(4 * q, 4 * q + 4):
                    mm = pe.transpose(ph[q % 2][:, j - 4 * q, :], hi[:, j:j + 1].to_broadcast([128, 128]), ident[:])
                ph_p.did(mm)
                eqs.wait(pe, f"eq{(q - 1) % 4}", L if q else L - 1)
                for j in range(4 * q, 4 * q + 4):
                    mm = pe.transpose(pd[:, j - 4 * q, :], df[g][:, j:j + 1].to_broadcast([128, 128]), ident[:])
                pd_p.did(mm)

            def take(L, q, js):
                hot_s.wait(pe, f"b{q}", L)
                for j in js:
                    n = 16 * L + 4 * q + j
                    pick_s.wait(pe, n - 2)
                    for u in range(2):
                        for t in range(3):
                            mm = pe.matmul(pk[bank(q, j)][:].rearrange("p h l -> p (h l)"), hot[q % 2][:, u, j, :],
                                           part[t][:, u].rearrange("p h l -> p (h l)"), start=u + t == 0,
                                           stop=u + t == 3)
                    pk_p.did(mm)

            def begin(i, g, L):
                spread(g, L, 0)

            def middle(i, g, L):
                for q in range(1, 4):
                    take(L, q - 1, (0, 1))
                    spread(g, L, q)
                    take(L, q - 1, (2, 3))

            def sums(i, g, L):
                eqs.wait(pe, "eq3", L)
                pay_s.wait(pe, L)
                comb_s.wait(pe, L - 2)
                for j in range(CH):
                    mm = pe.matmul(pc[g % 2][:, j, :], eq[g][:, j, :], pay[g][:, j, :], start=True, stop=True)
                pc_p.did(mm)
            pipeline(pe, LANES, G, [(1, lambda i, g, L: take(L, 3, (0, 1))), (0, begin),
                                    (1, lambda i, g, L: take(L, 3, (2, 3))), (3, sums), (0, middle)])

        @block.scalar
        def _(act):
            def gather_dst(g, L, qs):
                for j in range(4 * qs.start, 4 * qs.stop):
                    pick_s.wait(act, 16 * L + j)
                    for h in range(4):
                        cp = act.activation(pick[j % 2][:, h], pick[j % 2][:, h], ACT.Copy,
                                            accum_out=gd[g][:, j, h:h + 1])
                    gd_s.did(cp)

            def first_three(i, g, L):
                lgt.wait(act, "sub", L - G)
                gather_dst(g, L, slice(0, 3))

            def exps(i, g, L):
                lgt.wait(act, "sub", L)
                pc_p.wait(act, L - G)
                exp_s.did(act.activation(pay[g][:, :, 16:20], z[:], ACT.Exp))

            def copy(i, g, L):
                pc_p.wait(act, L)
                for t in range(TABLES):
                    added[t].wait(act, (L - G + 1) * (CH // TABLES) - 1)
                comb_s.did(act.activation(comb[g][:], pc[g % 2][:], ACT.Copy))
            pipeline(act, LANES, G, [(1, lambda i, g, L: gather_dst(g, L, slice(3, 4))), (0, first_three), (3, copy),
                                     (2, exps)])

        @block.vector
        def _(dve):
            dve.memset(zero[:], 0.0).then_inc(w_ok, 1)
            dve.wait_ge(w_in, 16 * NW)
            for q in range(1, 4):
                dve.tensor_copy(low[:, q, :], low[:, 0, :]).then_inc(w_ok, 1)
            dve.tensor_reduce(big[:], tops[:].rearrange("p a h -> p h a"), AX.X, ALU.max).then_inc(w_ok, 1)
            dve.wait_ge(w_ok, 5)
            dve.tensor_scalar(row_no[:, 0:1], spare_row[:], float(-T), None, ALU.add).then_inc(w_ok, 1)
            dve.tensor_scalar(row_no[:, 1:2], spare_row[:], float(128 - T), None, ALU.add).then_inc(w_ok, 1)
            dve.wait_ge(w_ok, 7)
            for u in range(2):
                dve.tensor_copy(left[:, u], dst_rd[:, u].rearrange("p l h -> p h l")).then_inc(split, 1)
            dve.wait_ge(split, 2)
            dve.tensor_copy(part[0][:], left[:]).then_inc(split, 1)
            for t in (1, 2):
                dve.wait_ge(split, 2 * t + 1)
                dve.tensor_tensor(left[:], left[:], part[t - 1][:], ALU.subtract).then_inc(split, 1)
                dve.wait_ge(split, 2 * t + 2)
                dve.tensor_copy(part[t][:], left[:]).then_inc(split, 1)

            def casts(i, g, L):
                idx_in[g].wait(dve, i)
                pd_p.wait(dve, 4 * (L - G) + 3)
                rows.wait(dve, "d", L - G)
                cast.did(dve.tensor_copy(df[g][:], di[g][:]), "df")
                cast.did(dve.tensor_scalar(hi_i[:], di[g][:], 7, None, ALU.arith_shift_right), "hi_i")
                cast.did(dve.tensor_scalar(lo_i[:], di[g][:], 127, None, ALU.bitwise_and), "lo_i")
                ph_p.wait(dve, 4 * L - 1)
                cast.wait(dve, "lo_i", L)
                cast.did(dve.tensor_copy(hi[:], hi_i[:]), "hi")
                hot_s.wait(dve, "m3", L - 1)
                cast.did(dve.tensor_copy(lo[:], lo_i[:]), "lo")

            def masks(g, L, q):
                js = slice(4 * q, 4 * q + 4)
                ph_p.wait(dve, 4 * L + q)
                pk_p.wait(dve, 16 * L + 4 * q - 5)
                for u in range(2):
                    hot_s.did(dve.tensor_scalar(hot[q % 2][:, u], ph[q % 2][:], row_no[:, u:u + 1], None,
                                                ALU.is_equal), f"{'ab'[u]}{q}")
                cast.wait(dve, "lo", L)
                pick_s.wait(dve, 16 * L + 4 * q - 5)
                hot_s.did(dve.tensor_tensor(mlo[q % 2][:], col_no[:].unsqueeze(1).to_broadcast([128, 4, 128]),
                                            lo[:, js].unsqueeze(2).to_broadcast([128, 4, 128]), ALU.is_equal),
                          f"m{q}")

            def picks(L, q, js):
                hot_s.wait(dve, f"m{q}", L)
                for j in js:
                    n = 16 * L + 4 * q + j
                    pk_p.wait(dve, n)
                    gd_s.wait(dve, n - 2)
                    pick_s.did(dve.tensor_tensor(pick[j % 2][:], pk[bank(q, j)][:], mlo[q % 2][:, j].unsqueeze(1)
                                                 .to_broadcast([128, 4, 128]), ALU.mult))

            def equal(g, L, q):
                js = slice(4 * q, 4 * q + 4)
                if q == 0:
                    pc_p.wait(dve, L - G)
                    rows.wait(dve, "first", L - G)
                pd_p.wait(dve, 4 * L + q)
                eqs.did(dve.tensor_tensor(eq[g][:, js, :], pd[:], df[g][:, js].unsqueeze(2)
                                          .to_broadcast([128, 4, 128]), ALU.is_equal), f"eq{q}")
                eqs.wait(dve, f"eq{q}", L)
                eqs.did(dve.tensor_tensor(eql[:], eq[g][:, js, :], low[:], ALU.mult), f"el{q}")
                eqs.wait(dve, f"el{q}", L)
                eqs.did(dve.tensor_reduce(cnt[g][:, js], eql[:], AX.X, ALU.add), f"cn{q}")

            def middle(i, g, L):
                for q in range(1, 4):
                    picks(L, q - 1, (0, 1))
                    masks(g, L, q)
                    picks(L, q - 1, (2, 3))
                    equal(g, L, q)

            def targets(i, g, L):
                for t in range(TABLES):
                    added[t].wait(dve, (L - G + 1) * (CH // TABLES) - 1)
                eqs.wait(dve, "cn3", L)
                rows.wait(dve, "i", L - 1)
                rows.did(dve.tensor_scalar(first[:], cnt[g][:], 0.5, None, ALU.is_lt), "first")
                rows.did(dve.tensor_scalar(tgt[:], df[g][:], spare_row[:, 0:1], None, ALU.subtract), "d")
                rows.wait(dve, "d", L)
                rows.did(dve.tensor_tensor(tgt[:], tgt[:], first[:], ALU.mult), "m")
                rows.wait(dve, "m", L)
                rows.did(dve.tensor_scalar(tgt[:], tgt[:], spare_row[:, 0:1], None, ALU.add), "t")
                rows.wait(dve, "t", L)
                rows.did(dve.tensor_copy(ti[g][:], tgt[:]), "i")

            def logits(i, g, L):
                src_in[g].wait(dve, i)
                gd_s.wait(dve, 16 * L + 15)
                pay_s.wait(dve, L - 1)
                lgt.did(dve.tensor_tensor(mz[:], gs[g][:, :, 16:20], gd[g][:], ALU.add), "z")
                lgt.wait(dve, "z", L)
                lgt.did(dve.scalar_tensor_tensor(z[:], mz[:], 0.2, mz[:], ALU.mult, ALU.max), "l")
                lgt.wait(dve, "l", L)
                lgt.did(dve.tensor_tensor(mz[:], gd[g][:], big[:].unsqueeze(1).to_broadcast([128, CH, 4]), ALU.add),
                        "mz")
                lgt.wait(dve, "mz", L)
                lgt.did(dve.scalar_tensor_tensor(ml[:], mz[:], 0.2, mz[:], ALU.mult, ALU.max), "ml")
                lgt.wait(dve, "ml", L)
                lgt.did(dve.tensor_tensor(z[:], z[:], ml[:], ALU.subtract), "sub")
                exp_s.wait(dve, L)
                pay_s.did(dve.tensor_tensor(
                    pay[g][:, :, 0:16].rearrange("p j (h e) -> p j h e", e=4),
                    gs[g][:, :, 0:16].rearrange("p j (h e) -> p j h e", e=4),
                    pay[g][:, :, 16:20].unsqueeze(3).to_broadcast([128, CH, 4, 4]), ALU.mult))

            pipeline(dve, LANES, G, [(0, casts), (1, lambda i, g, L: picks(L, 3, (0, 1))),
                                     (0, lambda i, g, L: masks(g, L, 0)), (1, lambda i, g, L: picks(L, 3, (2, 3))),
                                     (0, lambda i, g, L: equal(g, L, 0)), (0, middle), (3, targets), (2, logits)])
    c.close()



def gat_gates(nc, a, gat, dst_rows, top, tables, gate_out):
    c = Core(nc, "gate")
    K = T // 128
    acc = c.sb("acc", [128, K, 20])
    part = [c.sb(f"part{k}", [128, K, 20]) for k in range(2)]
    g = c.sb("g", [128, K, 20])
    gd = c.sb("gd", [128, K, 4])
    z = c.sb("z", [128, K, 4])
    mz = c.sb("mz", [128, K, 4])
    ee = c.sb("ee", [128, K, 4])
    m = c.sb("m", [128, K])
    r = c.sb("r", [128, K])
    mh = c.sb("mh", [128, K])
    tops = c.sb("tops", [128, 128, 4])
    big = c.sb("big", [128, 4])
    bg = c.sb("bg", [128, 16])
    gam = c.sb("gam", [128, 16])
    bet = c.sb("bet", [128, 16])
    s = c.sb("s", [128, K, 4])
    gt = c.sb("gt", [128, K, 4])
    w_in, t_in, g_in = c.sem("w_in"), [c.sem(f"t_in{k}") for k in range(TABLES)], c.sem("g_in")
    dv, ex, pw, out_st = c.sem("dve_done"), c.sem("exp_done"), c.sem("pow_done"), c.sem("out_st")
    dve_at = {}

    with nc.Block() as block:
        @block.vector
        def _(dve):
            n = [0]

            def link(ins, name=None):
                n[0] += 1
                ins.then_inc(dv, 1)
                dve.wait_ge(dv, n[0])
                if name:
                    dve_at[name] = n[0]

            link(dve.memset(mh[:], -0.5), "mh")
            dve.wait_ge(w_in, 64)
            link(dve.tensor_reduce(big[:], tops[:].rearrange("p a h -> p h a"), AX.X, ALU.max))
            dve.wait_ge(g_in, 32)
            link(dve.tensor_tensor(mz[:], g[:, :, 16:20], gd[:], ALU.add))
            link(dve.scalar_tensor_tensor(z[:], mz[:], 0.2, mz[:], ALU.mult, ALU.max))
            link(dve.tensor_tensor(mz[:], gd[:], big[:].unsqueeze(1).to_broadcast([128, K, 4]), ALU.add))
            link(dve.scalar_tensor_tensor(gd[:], mz[:], 0.2, mz[:], ALU.mult, ALU.max))
            link(dve.tensor_tensor(z[:], z[:], gd[:], ALU.subtract), "logit")
            dve.wait_ge(t_in[0], 16)
            for k in range(1, TABLES):
                dve.wait_ge(t_in[k], 16)
                link(dve.tensor_tensor(acc[:], acc[:], part[k % 2][:], ALU.add), f"part{k}")
            dve.wait_ge(ex, 1)
            link(dve.tensor_tensor(acc[:, :, 16:20], acc[:, :, 16:20], ee[:], ALU.add))
            per_head = lambda t: t[:, :, 0:16].rearrange("p k (h e) -> p k h e", e=4)
            flat = lambda t: t[:].unsqueeze(3).to_broadcast([128, K, 4, 4])
            link(dve.tensor_tensor(per_head(g), per_head(g), flat(ee), ALU.mult))
            link(dve.tensor_tensor(acc[:, :, 0:16], acc[:, :, 0:16], g[:, :, 0:16], ALU.add))
            link(dve.tensor_scalar(z[:], acc[:, :, 16:20], 1e-37, None, ALU.add))
            link(dve.reciprocal(z[:], z[:]))
            link(dve.tensor_tensor(per_head(acc), per_head(acc), flat(z), ALU.mult))
            along = lambda t: t[:].unsqueeze(1).to_broadcast([128, K, 16])
            agg = acc[:, :, 0:16]
            link(dve.tensor_tensor(agg, agg, along(bg), ALU.add))
            link(dve.tensor_reduce(m[:], agg, AX.X, ALU.add))
            link(dve.tensor_scalar(m[:], m[:], 1 / 16, None, ALU.mult))
            link(dve.tensor_tensor(agg, agg, m[:].unsqueeze(2).to_broadcast([128, K, 16]), ALU.subtract))
            sq = g[:, :, 0:16]
            link(dve.tensor_tensor(sq, agg, agg, ALU.mult))
            link(dve.tensor_reduce(m[:], sq, AX.X, ALU.add))
            link(dve.tensor_scalar(m[:], m[:], 1 / 16, EPS, ALU.mult, ALU.add), "var")
            dve.wait_ge(pw, 1)
            link(dve.tensor_tensor(agg, agg, r[:].unsqueeze(2).to_broadcast([128, K, 16]), ALU.mult))
            link(dve.tensor_tensor(agg, agg, along(gam), ALU.mult))
            link(dve.tensor_tensor(agg, agg, along(bet), ALU.add))
            link(dve.tensor_reduce(s[:], agg.rearrange("p k (h e) -> p k e h", e=4), AX.X, ALU.add))
            link(dve.tensor_scalar(s[:], s[:], 1 / 4, None, ALU.mult))
            best_two(dve, link, s, gt, z, mz, m, 4, K)
            link(dve.tensor_reduce(m[:], s[:], AX.X, ALU.max))
            link(dve.tensor_tensor(s[:], s[:], m[:].unsqueeze(2).to_broadcast([128, K, 4]), ALU.subtract), "best")
            dve.wait_ge(ex, 2)
            link(dve.tensor_tensor(gt[:], gt[:], ee[:], ALU.mult))
            link(dve.tensor_reduce(m[:], gt[:], AX.X, ALU.add))
            link(dve.reciprocal(m[:], m[:]))
            link(dve.tensor_tensor(gt[:], gt[:], m[:].unsqueeze(2).to_broadcast([128, K, 4]), ALU.mult), "gates")

        @block.scalar
        def _(act):
            act.wait_ge(dv, dve_at["logit"])
            act.activation(ee[:], z[:], ACT.Exp).then_inc(ex, 1)
            act.wait_ge(dv, dve_at["best"])
            act.activation(ee[:], s[:], ACT.Exp).then_inc(ex, 1)

        @block.gpsimd
        def _(pool):
            pool.wait_ge(dv, dve_at["var"])
            pool.tensor_tensor(r[:], m[:], mh[:], ALU.pow).then_inc(pw, 1)

        @block.sync
        def _(sp):
            sp.dma_start(tops[:].rearrange("p a h -> p (a h)"),
                         top.rearrange("p h -> (p h)").partition_broadcast(128)).then_inc(w_in, 16)
            for t, src in ((bg, "b_gat"), (gam, "gat_g"), (bet, "gat_b")):
                sp.dma_start(t[:], a[src].partition_broadcast(128)).then_inc(w_in, 16)
            rows = lambda t: t[0:T].rearrange("(p k) n -> p k n", p=128)
            sp.dma_start(g[:], rows(gat)).then_inc(g_in, 16)
            sp.dma_start(gd[:], rows(dst_rows)).then_inc(g_in, 16)
            sp.dma_start(acc[:], rows(tables[0])).then_inc(t_in[0], 16)
            for k in range(1, TABLES):
                if k >= 3:
                    sp.wait_ge(dv, dve_at[f"part{k - 2}"])
                sp.dma_start(part[k % 2][:], rows(tables[k])).then_inc(t_in[k], 16)
            sp.wait_ge(dv, dve_at["gates"])
            sp.dma_start(rows(gate_out), gt[:]).then_inc(out_st, 16)
            sp.wait_ge(out_st, 16)
    c.close()


def best_two(dve, link, s, sel, u, w, one, E, K):
    for i in range(E):
        me = s[:, :, i:i + 1].to_broadcast([128, K, E])
        link(dve.tensor_tensor(u[:], s[:, :, :], me, ALU.is_gt))
        if i:
            link(dve.tensor_tensor(w[:, :, 0:i], s[:, :, 0:i], s[:, :, i:i + 1].to_broadcast([128, K, i]),
                                   ALU.is_equal))
            link(dve.tensor_tensor(u[:, :, 0:i], u[:, :, 0:i], w[:, :, 0:i], ALU.add))
        link(dve.tensor_reduce(one[:], u[:], AX.X, ALU.add))
        link(dve.tensor_scalar(sel[:, :, i], one[:], 1.5, None, ALU.is_lt))


def dense(nc, a, phase, x_in, x_out, E, gate=None, pre=False, extra=None, post=True):
    c = Core(nc, phase)
    G, K, LANES = 8, 4, T // 512
    x = [c.sb(f"x{k}", [128, K, C]) for k in range(G)]
    ex = [c.sb(f"ex{k}", [128, K, C]) for k in range(G)] if extra is not None else None
    gt = [c.sb(f"gt{k}", [128, K, E]) for k in range(G)] if gate is not None else None
    xn = [c.sb(f"xn{k}", [128, K, C]) for k in range(2)] if pre else None
    xT = [c.sb(f"xT{k}", [C, K, 128]) for k in range(2)]
    hid = [c.sb(f"hid{k}", [128, E, K, 128]) for k in range(2)]
    yT = [c.sb(f"yT{k}", [128, K, 128]) for k in range(2)]
    t1 = c.sb("t1", [128, K, 2, C])
    t2 = c.sb("t2", [128, K, C])
    s = [c.sb(f"s{k}", [128, K, C]) for k in range(2)]
    y = [c.sb(f"y{k}", [128, K, C]) for k in range(G)]
    st = c.sb("st", [128, K, 6])
    mv = [c.sb(f"mv{k}", [128, K, 2]) for k in range(2)]
    ve = c.sb("ve", [128, K])
    rstd = [c.sb(f"rstd{k}", [128, K]) for k in range(2)]
    st0 = c.sb("st0", [128, K, 6])
    mv0 = [c.sb(f"mv0{k}", [128, K, 2]) for k in range(2)]
    ve0 = c.sb("ve0", [128, K])
    rstd0 = [c.sb(f"rstd0{k}", [128, K]) for k in range(2)]
    mh = c.sb("mh", [128, K])
    spare = c.sb("spare", [128, 1])
    ident = c.sb("ident", [128, 128])
    w1 = c.sb("w1", [C, E, 128])
    b1 = c.sb("b1", [128, E])
    w2 = c.sb("w2", [128, E, C])
    b2 = c.sb("b2", [128, E, C])
    lnw = c.sb("lnw", [C, 2])

    pT = c.ps("pT", [C, K, 128])
    ph = [c.ps(f"ph{k}", [128, K, 128]) for k in range(2)]
    py = [c.ps(f"py{k}", [128, 512]) for k in range(2)]
    pyT = [c.ps(f"pyT{k}", [128, K, 128]) for k in range(2)]

    w_in, mh_set, turn = c.sem("w_in"), c.sem("mh_set"), c.sem("turn")
    loads = 1 + (gate is not None) + (extra is not None)
    ld = [c.loads(f"ld{k}", loads) for k in range(G)]
    stores = [c.loads(f"st{k}") for k in range(G)]
    pre_s, pre_r, xn_s = c.steps("pre_s", "s0 s1 s2 s3 m0 m1 m2 m3 ve"), c.flag("pre_r"), \
        c.steps("xn_s", "n0 n1 n2 n3")
    xT_p, xT_s, h_p, hid_s = c.flag("xT_p"), c.flag("xT_s"), c.flag("h_p"), c.flag("hid_s")
    PR = E // 2
    y_p, yT_p, yT_s = c.flag("y_p"), c.flag("yT_p"), c.flag("yT_s")
    mix = c.steps("mix", ("b" if E == 1 else "b0 g0 r0 " + " ".join(f"b{j} g{j} r{j} a{j}" for j in range(1, PR)))
                  + " add sum")
    norm, rs_s = c.steps("norm", "s0 s1 s2 s3 m0 m1 m2 m3 ve"), c.flag("rs_s")
    y_s = c.steps("y_s", "y0 y1 y2 y3")
    rows = lambda t: t.rearrange("(l p k) c -> l p k c", p=128, k=K)
    NW = 5 + pre

    with nc.Block() as block:
        @block.sync
        def _(sp):
            sp.dma_start(ident[:], a["eye"]).then_inc(w_in, 16)
            sp.dma_start(w1[:], a[phase + "_w1"].rearrange("e c n -> c e n")).then_inc(w_in, 16)
            sp.dma_start(b1[:], a[phase + "_b1"]).then_inc(w_in, 16)
            sp.dma_start(w2[:], a[phase + "_w2"].rearrange("e c n -> c e n")).then_inc(w_in, 16)
            sp.dma_start(b2[:].rearrange("p e c -> p (e c)"),
                         a[phase + "_b2"].rearrange("e c -> (e c)").partition_broadcast(128)).then_inc(w_in, 16)
            if pre:
                sp.dma_start(lnw[:], a[phase + "_ln"]).then_inc(w_in, 16)

            def load(i, g, L):
                mix.wait(sp, "sum", L - G)
                ld[g].inc(sp.dma_start(x[g][:], rows(x_in)[L]))
                if gate is not None:
                    ld[g].inc(sp.dma_start(gt[g][:], rows(gate)[L]))
                if extra is not None:
                    ld[g].inc(sp.dma_start(ex[g][:], rows(extra)[L]))

            def store(i, g, L):
                y_s.wait(sp, "y3", L)
                stores[g].inc(sp.dma_start(rows(x_out)[L], y[g][:]))
            pipeline(sp, LANES, G, [(0, load), (6, store)], look=8)
            for g in range(G):
                stores[g].wait(sp, LANES // G - 1)

        @block.tensor
        def _(pe):
            pe.wait_ge(w_in, 16 * NW)

            def tr(i, g, L):
                if pre:
                    xn_s.wait(pe, "n3", L)
                else:
                    ld[g].wait(pe, i)
                xT_s.wait(pe, L - 1)
                pe.sem_inc(turn, 1)
                src = xn[g % 2] if pre else x[g]
                for k in range(K):
                    mm = pe.transpose(pT[:, k, :], src[:, k, :], ident[:])
                xT_p.did(mm)

            def up(i, g, L):
                xT_s.wait(pe, L)
                for e in range(E):
                    hid_s.wait(pe, L * E + e - 2)
                    h_p.did(pe.matmul(ph[e % 2 if E > 1 else g % 2][:].rearrange("p k n -> p (k n)"), w1[:, e, :],
                                      xT[g % 2][:].rearrange("p k n -> p (k n)"), start=True, stop=True))

            def down(i, g, L):
                hid_s.wait(pe, L * E + E - 1)
                if E == 1:
                    mix.wait(pe, "b", L - 2)
                    for k in range(K):
                        mm = pe.matmul(py[g % 2][:, k * C:k * C + C], hid[g % 2][:, 0, k, :], w2[:, 0, :],
                                       start=True, stop=True)
                    y_p.did(mm)
                    return
                for j in range(PR):
                    n = L * PR + j
                    yT_s.wait(pe, n - 2)
                    for e in range(2):
                        mm = pe.matmul(pyT[j % 2][64 * e:64 * e + 64].rearrange("c k p -> c (k p)"),
                                       w2[:, 2 * j + e, :], hid[g % 2][:, 2 * j + e].rearrange("h k p -> h (k p)"),
                                       start=True, stop=True)
                    yT_p.did(mm)
                    if j:
                        turned(L, j - 1)
                turned(L, PR - 1)

            def turned(L, j):
                yT_s.wait(pe, L * PR + j)
                mix.wait(pe, f"b{(j - 2) % PR}", L if j >= 2 else L - 1)
                for k in range(K):
                    mm = pe.transpose(py[j % 2][:, 128 * k:128 * k + 128], yT[j % 2][:, k, :], ident[:])
                y_p.did(mm)

            pipeline(pe, LANES, G, [(4, down), (3, up), (2, tr)], look=8)

        @block.scalar
        def _(act):
            act.wait_ge(w_in, 16 * NW)

            def copy_xT(i, g, L):
                xT_p.wait(act, L)
                h_p.wait(act, (L - 2) * E + E - 1)
                if pre:
                    xT_s.did(act.activation(xT[g % 2][:], pT[:], ACT.Identity, bias=lnw[:, 1:2], scale=lnw[:, 0:1]))
                else:
                    xT_s.did(act.activation(xT[g % 2][:], pT[:], ACT.Copy))

            def gelu(i, g, L):
                if E == 1:
                    y_p.wait(act, L - 2)
                else:
                    yT_p.wait(act, (L - 2) * PR + PR - 1)
                for e in range(E):
                    h_p.wait(act, L * E + e)
                    hid_s.did(act.activation(hid[g % 2][:, e], ph[e % 2 if E > 1 else g % 2][:], ACT.Gelu,
                                             bias=b1[:, e:e + 1]))
            def copy_yT(i, g, L):
                for j in range(PR):
                    n = L * PR + j
                    yT_p.wait(act, n)
                    y_p.wait(act, n - 2)
                    yT_s.did(act.activation(yT[j % 2][:], pyT[j % 2][:], ACT.Copy))
            pipeline(act, LANES, G, [(4, copy_yT), (3, gelu), (2, copy_xT)], look=8)

        @block.gpsimd
        def _(pool):
            pool.memset(mh[:], -0.5).then_inc(mh_set, 1)
            pool.wait_ge(mh_set, 1)

            def rs0(i, g, L):
                pre_s.wait(pool, "ve", L)
                xn_s.wait(pool, "n3", L - 2)
                pre_r.did(pool.tensor_tensor(rstd0[g % 2][:], ve0[:], mh[:], ALU.pow))

            def rs(i, g, L):
                norm.wait(pool, "ve", L)
                y_s.wait(pool, "y3", L - 2)
                rs_s.did(pool.tensor_tensor(rstd[g % 2][:], ve[:], mh[:], ALU.pow))
            pipeline(pool, LANES, G, [(4, rs)] * post + [(0, rs0)] * pre, look=8)

        @block.vector
        def _(dve):
            def stats(steps, st, mv, ve, src, g, L):
                for k in range(K):
                    steps.did(dve.bn_stats(st[:, k, :], src[:, k, :]), f"s{k}")
                steps.wait(dve, "s3", L)
                dve.memset(spare[:], 0.0)
                for k in range(K):
                    steps.did(dve.bn_aggr(mv[:, k, :], st[:, k, :]), f"m{k}")
                steps.wait(dve, "m3", L)

            def pre_stats(i, g, L):
                ld[g].wait(dve, i)
                xn_s.wait(dve, "n3", L - 2)
                stats(pre_s, st0, mv0[g % 2], ve0, x[g], g, L)
                pre_r.wait(dve, L - 1)
                pre_s.did(dve.tensor_scalar(ve0[:], mv0[g % 2][:, :, 1], EPS, None, ALU.add), "ve")

            def pre_norm(i, g, L):
                pre_r.wait(dve, L)
                xT_p.wait(dve, L - 2)
                for k in range(K):
                    xn_s.did(dve.tensor_scalar(xn[g % 2][:, k, :], x[g][:, k, :], mv0[g % 2][:, k, 0:1],
                                               rstd0[g % 2][:, k:k + 1], ALU.subtract, ALU.mult), f"n{k}")

            def combine(i, g, L):
                y_s.wait(dve, "y3", L - 2)
                ld[g].wait(dve, i)
                if E == 1:
                    y_p.wait(dve, L)
                    mix.did(dve.tensor_tensor(s[g % 2][:], py[g % 2][:, 0:K * C].rearrange("p (k c) -> p k c", k=K),
                                              b2[:].to_broadcast([128, K, C]), ALU.add), "b")
                    mix.wait(dve, "b", L)
                for j in range(PR):
                    y_p.wait(dve, L * PR + j)
                    mix.wait(dve, (f"a{j - 1}" if j > 1 else "r0") if j else (f"a{PR - 1}"), L if j else L - 1)
                    pair = slice(2 * j, 2 * j + 2)
                    mix.did(dve.tensor_tensor(t1[:], py[j % 2][:].rearrange("p (k e c) -> p k e c", k=K, e=2),
                                              b2[:, pair].unsqueeze(1).to_broadcast([128, K, 2, C]), ALU.add), f"b{j}")
                    mix.wait(dve, f"b{j}", L)
                    mix.did(dve.tensor_tensor(t1[:], t1[:], gt[g][:, :, pair].unsqueeze(3)
                                              .to_broadcast([128, K, 2, C]), ALU.mult), f"g{j}")
                    mix.wait(dve, f"g{j}", L)
                    mix.did(dve.tensor_reduce(t2[:] if j else s[g % 2][:], t1[:].rearrange("p k e c -> p k c e"),
                                              AX.X, ALU.add), f"r{j}")
                    mix.wait(dve, f"r{j}", L)
                    if j:
                        mix.did(dve.tensor_tensor(s[g % 2][:], s[g % 2][:], t2[:], ALU.add), f"a{j}")
                if E > 1:
                    mix.wait(dve, f"a{PR - 1}", L)
                if extra is not None:
                    mix.did(dve.tensor_tensor(s[g % 2][:], s[g % 2][:], ex[g][:], ALU.add), "add")
                    mix.wait(dve, "add", L)
                else:
                    mix.did(dve.memset(spare[:], 0.0), "add")
                mix.did(dve.tensor_tensor(s[g % 2][:], s[g % 2][:], x[g][:], ALU.add), "sum")
                mix.wait(dve, "sum", L)
                if post:
                    stats(norm, st, mv[g % 2], ve, s[g % 2], g, L)
                    rs_s.wait(dve, L - 1)
                    norm.did(dve.tensor_scalar(ve[:], mv[g % 2][:, :, 1], EPS, None, ALU.add), "ve")

            def finish(i, g, L):
                stores[g].wait(dve, i - 1)
                if post:
                    rs_s.wait(dve, L)
                for k in range(K):
                    if post:
                        y_s.did(dve.tensor_scalar(y[g][:, k, :], s[g % 2][:, k, :], mv[g % 2][:, k, 0:1],
                                                  rstd[g % 2][:, k:k + 1], ALU.subtract, ALU.mult), f"y{k}")
                    else:
                        y_s.did(dve.tensor_copy(y[g][:, k, :], s[g % 2][:, k, :]), f"y{k}")
            pipeline(dve, LANES, G, [(5, finish), (4, combine)] + [(1, pre_norm), (0, pre_stats)] * pre, look=8)
    c.close()


H, DH, M = 8, 8, 64


def landmarks(nc, a, phase, layer, y_in, qk_out, v_out, a2_out, top_out):
    c = Core(nc, phase)
    G = 4
    y = [c.sb(f"y{k}", [128, 2, C]) for k in range(G)]
    st = c.sb("st", [128, 2, 6])
    mv = [c.sb(f"mv{k}", [128, 2, 2]) for k in range(2)]
    ve = c.sb("ve", [128, 2])
    rstd = [c.sb(f"rstd{k}", [128, 2]) for k in range(2)]
    xn = [c.sb(f"xn{k}", [128, 2, C]) for k in range(2)]
    xT = [c.sb(f"xT{k}", [C, 2, 128]) for k in range(2)]
    qk = [c.sb(f"qk{k}", [C, 2, P]) for k in range(G)]
    v = [c.sb(f"v{k}", [128, 2, C]) for k in range(G)]
    lm = [c.sb(f"lm{k}", [C, 2 * M]) for k in range(2)]
    kl = [c.sb(f"kl{k}", [C, M]) for k in range(2)]
    qbd = [c.sb(f"qbd{k}", [C, H, M]) for k in range(2)]
    mx = c.sb("mx", [128, 4])
    lg = [c.sb(f"lg{k}", [128, 4, M]) for k in range(2)]
    e2 = [c.sb(f"e2{k}", [128, 4, M]) for k in range(2)]
    sm = c.sb("sm", [128, 4])
    a2 = [c.sb(f"a2{k}", [128, 4, M]) for k in range(G)]
    rsum = c.sb("rsum", [128, B, 4])
    csum = c.sb("csum", [128, B])
    tops = c.sb("tops", [128, 2])
    mh = c.sb("mh", [128, 2])
    spare = c.sb("spare", [128, 1])
    ident = c.sb("ident", [128, 128])
    ones = c.sb("ones", [128, 128])
    mask = c.sb("mask", [C, H, M])
    w = c.sb("w", [C, 3, C])
    lnw = c.sb("lnw", [C, 2])

    pT = c.ps("pT", [C, 2, 128])
    pqk = [c.ps(f"pqk{k}", [C, 2, P]) for k in range(2)]
    pv = c.ps("pv", [128, 2, C])
    pa = [c.ps(f"pa{k}", [128, 4, M]) for k in range(2)]
    pcs = [c.ps(f"pcs{k}", [128, 4, M]) for k in range(2)]

    w_in, prep, mh_set, turn, turn_d = c.sem("w_in"), c.sem("prep"), c.sem("mh_set"), c.sem("turn"), c.sem("turn_d")
    ld = [c.loads(f"ld{k}") for k in range(G)]
    st_qk, st_v, st_a = ([c.loads(f"{n}{k}") for k in range(G)] for n in ("st_qk", "st_v", "st_a"))
    stat, rs_s, xn_s = c.steps("stat", "s0 s1 m0 m1 ve"), c.flag("rs_s"), c.steps("xn_s", "n0 n1")
    xT_p, xT_s, qk_p, qk_s, v_p, v_s = (c.flag(n) for n in ("xT_p", "xT_s", "qk_p", "qk_s", "v_p", "v_s"))
    lms, qbd_s = c.steps("lms", "lm kl"), c.flag("qbd_s")
    a_p, e_s = c.flag("a_p"), c.flag("e_s")
    soft = c.steps("soft", "mx sub")
    done = c.steps("done", "sm rc a2 rsum")
    cs_p, cs_s = c.flag("cs_p"), c.flag("cs_s")
    y_view = y_in.rearrange("(b k p) c -> b p k c", p=128, k=2)
    NW = 5

    with nc.Block() as block:
        @block.sync
        def _(sp):
            sp.dma_start(ident[:], a["eye"]).then_inc(w_in, 16)
            sp.dma_start(ones[:], a["ones_bd"]).then_inc(w_in, 16)
            sp.dma_start(mask[:].rearrange("c h m -> c (h m)"), a["head_mask"]).then_inc(w_in, 16)
            sp.dma_start(w[:], a["w_qkv"][layer]).then_inc(w_in, 16)
            sp.dma_start(lnw[:], a["ln1"][layer]).then_inc(w_in, 16)

            def load(i, g, L):
                xn_s.wait(sp, "n1", L - G)
                ld[g].inc(sp.dma_start(y[g][:], y_view[L]))

            def store_qkv(i, g, L):
                qk_s.wait(sp, L)
                st_qk[g].inc(sp.dma_start(qk_out[L], qk[g][:]))
                v_s.wait(sp, L)
                st_v[g].inc(sp.dma_start(v_out[L], v[g][:]))

            def store_a(i, g, L):
                done.wait(sp, "a2", L)
                st_a[g].inc(sp.dma_start(a2_out[L], a2[g][:]))
            pipeline(sp, B, G, [(0, load), (4, store_qkv), (9, store_a)])
            for g in range(G):
                for s in (st_qk, st_v, st_a):
                    s[g].wait(sp, B // G - 1)
            sp.wait_ge(turn_d, 2)
            sp.dma_start(top_out, tops[:]).then_inc(w_in, 16)
            sp.wait_ge(w_in, 16 * NW + 16)

        @block.tensor
        def _(pe):
            pe.wait_ge(w_in, 16 * NW)
            pe.wait_ge(prep, 2)

            def tr(i, g, L):
                xn_s.wait(pe, "n1", L)
                xT_s.wait(pe, L - 1)
                pe.sem_inc(turn, 1)
                for k in range(2):
                    mm = pe.transpose(pT[:, k, :], xn[g % 2][:, k, :], ident[:])
                xT_p.did(mm)

            def qkv(i, g, L):
                xT_s.wait(pe, L)
                qk_s.wait(pe, L - 2)
                pe.sem_inc(turn, 1)
                for t in range(2):
                    mm = pe.matmul(pqk[g % 2][:, t, :], w[:, t, :], xT[g % 2][:].rearrange("c k p -> c (k p)"),
                                   start=True, stop=True)
                qk_p.did(mm)
                v_s.wait(pe, L - 1)
                for k in range(2):
                    mm = pe.matmul(pv[:, k, :], xT[g % 2][:, k, :], w[:, 2, :], start=True, stop=True)
                v_p.did(mm)

            def a2s(i, g, L):
                lms.wait(pe, "kl", L)
                qbd_s.wait(pe, L)
                soft.wait(pe, "sub", L - 2)
                for p in range(4):
                    mm = pe.matmul(pa[g % 2][:, p, :], qbd[g % 2][:, 2 * p:2 * p + 2, :].rearrange("c h m -> c (h m)"),
                                   kl[g % 2][:], start=True, stop=True)
                a_p.did(mm)

            def columns(i, g, L):
                done.wait(pe, "a2", L)
                cs_s.wait(pe, L - 2)
                cs_p.did(pe.matmul(pcs[g % 2][:].rearrange("p h m -> p (h m)"), ones[:],
                                   a2[g][:].rearrange("p h m -> p (h m)"), start=True, stop=True))
            pipeline(pe, B, G, [(2, tr), (9, columns), (3, qkv), (5, a2s)])

        @block.scalar
        def _(act):
            act.wait_ge(w_in, 16 * NW)

            def copy_xT(i, g, L):
                xT_p.wait(act, L)
                v_p.wait(act, L - 2)
                xT_s.did(act.activation(xT[g % 2][:], pT[:], ACT.Identity, bias=lnw[:, 1:2], scale=lnw[:, 0:1]))

            def copy_qk(i, g, L):
                qk_p.wait(act, L)
                st_qk[g].wait(act, i - 1)
                lms.wait(act, "lm", L - G)
                qk_s.did(act.activation(qk[g][:], pqk[g % 2][:], ACT.Copy))

            def exps(i, g, L):
                soft.wait(act, "sub", L)
                done.wait(act, "a2", L - 2)
                e_s.did(act.activation(e2[g % 2][:], lg[g % 2][:], ACT.Exp))
            pipeline(act, B, G, [(7, exps), (2, copy_xT), (3, copy_qk)])

        @block.gpsimd
        def _(pool):
            pool.memset(mh[:], -0.5).then_inc(mh_set, 1)
            pool.wait_ge(mh_set, 1)
            pool.wait_ge(prep, 2)

            def rs(i, g, L):
                stat.wait(pool, "ve", L)
                xn_s.wait(pool, "n1", L - 2)
                rs_s.did(pool.tensor_tensor(rstd[g % 2][:], ve[:], mh[:], ALU.pow))
            def landmark_rows(i, g, L):
                lms.wait(pool, "lm", L)
                a_p.wait(pool, L - 2)
                qbd_s.did(pool.tensor_tensor(qbd[g % 2][:], lm[g % 2][:, 0:M].unsqueeze(1).to_broadcast([C, H, M]),
                                             mask[:], ALU.mult))
            pipeline(pool, B, G, [(0, rs), (4, landmark_rows)])

        @block.vector
        def _(dve):
            dve.wait_ge(w_in, 16 * NW)
            dve.tensor_scalar(w[:, 0, :], w[:, 0, :], float(DH) ** -0.5, None, ALU.mult).then_inc(prep, 1)
            dve.tensor_scalar(mask[:], mask[:], 0.25, None, ALU.mult).then_inc(prep, 1)

            def stats(i, g, L):
                ld[g].wait(dve, i)
                xn_s.wait(dve, "n1", L - 2)
                for k in range(2):
                    stat.did(dve.bn_stats(st[:, k, :], y[g][:, k, :]), f"s{k}")
                stat.wait(dve, "s1", L)
                dve.memset(spare[:], 0.0)
                for k in range(2):
                    stat.did(dve.bn_aggr(mv[g % 2][:, k, :], st[:, k, :]), f"m{k}")
                stat.wait(dve, "m1", L)
                rs_s.wait(dve, L - 1)
                stat.did(dve.tensor_scalar(ve[:], mv[g % 2][:, :, 1], EPS, None, ALU.add), "ve")

            def normed(i, g, L):
                rs_s.wait(dve, L)
                xT_p.wait(dve, L - 2)
                for k in range(2):
                    xn_s.did(dve.tensor_scalar(xn[g % 2][:, k, :], y[g][:, k, :], mv[g % 2][:, k, 0:1],
                                               rstd[g % 2][:, k:k + 1], ALU.subtract, ALU.mult), f"n{k}")

            def copy_v(i, g, L):
                v_p.wait(dve, L)
                st_v[g].wait(dve, i - 1)
                v_s.did(dve.tensor_copy(v[g][:], pv[:]))

            def means(i, g, L):
                qk_s.wait(dve, L)
                qbd_s.wait(dve, L - 2)
                lms.did(dve.tensor_reduce(lm[g % 2][:], qk[g][:].rearrange("c t (m l) -> c (t m) l", l=4), AX.X, ALU.add),
                        "lm")
                lms.wait(dve, "lm", L)
                a_p.wait(dve, L - 2)
                lms.did(dve.tensor_scalar(kl[g % 2][:], lm[g % 2][:, M:2 * M], 0.25, None, ALU.mult), "kl")

            def shift(i, g, L):
                a_p.wait(dve, L)
                soft.wait(dve, "sub", L - 1)
                e_s.wait(dve, L - 2)
                soft.did(dve.tensor_reduce(mx[:], pa[g % 2][:], AX.X, ALU.max), "mx")
                soft.wait(dve, "mx", L)
                soft.did(dve.tensor_tensor(lg[g % 2][:], pa[g % 2][:], mx[:].unsqueeze(2).to_broadcast([128, 4, M]),
                                           ALU.subtract), "sub")

            def divide(i, g, L):
                e_s.wait(dve, L)
                st_a[g].wait(dve, i - 1)
                cs_p.wait(dve, L - G)
                done.did(dve.tensor_reduce(sm[:], e2[g % 2][:], AX.X, ALU.add), "sm")
                done.wait(dve, "sm", L)
                done.did(dve.reciprocal(sm[:], sm[:]), "rc")
                done.wait(dve, "rc", L)
                done.did(dve.tensor_tensor(a2[g][:], e2[g % 2][:], sm[:].unsqueeze(2).to_broadcast([128, 4, M]),
                                           ALU.mult), "a2")
                done.wait(dve, "a2", L)
                done.did(dve.tensor_reduce(rsum[:, L] if isinstance(L, int) else rsum[:, bass.ds(L, 1)].rearrange(
                    "p a h -> p (a h)"), a2[g][:], AX.X, ALU.add), "rsum")

            def cmax(i, g, L):
                cs_p.wait(dve, L)
                cs_s.did(dve.tensor_reduce(csum[:, L:L + 1] if isinstance(L, int) else csum[:, bass.ds(L, 1)],
                                           pcs[g % 2][:].rearrange("p h m -> p (h m)"), AX.X, ALU.max))
            pipeline(dve, B, G, [(6, shift), (8, divide), (10, cmax), (4, means), (1, normed), (0, stats),
                                 (3, copy_v)])
            done.wait(dve, "rsum", B - 1)
            cs_s.wait(dve, B - 1)
            dve.tensor_reduce(tops[:, 0:1], rsum[:].rearrange("p b h -> p (b h)"), AX.X, ALU.max).then_inc(turn_d, 1)
            dve.tensor_reduce(tops[:, 1:2], csum[:], AX.X, ALU.max).then_inc(turn_d, 1)
    c.close()


def inverse(nc, a, phase, a2_in, top_in, zt_out):
    c = Core(nc, phase)
    G, IT, LANES = 4, 6, B // 4
    last = IT - 1
    wide = lambda n: [c.sb(f"{n}{k}", [128, 4, 128]) for k in range(G)]
    x = [[c.sb(f"x{b}{k}", [128, 4, 128]) for k in range(G)] for b in range(2)]
    xt, p, k1, k2, k3 = (wide(n) for n in ("xt", "p", "k1", "k2", "k3"))
    r = [wide(f"r{b}") for b in range(2)]
    zo = [c.sb(f"zo{k}", [128, 4, M]) for k in range(G)]
    ident = c.sb("ident", [128, 128])
    tops = c.sb("tops", [128, 128, 2])
    big = c.sb("big", [128, 2])
    inv = c.sb("inv", [128, 2])
    ps = [[c.ps(f"p{g}{k}", [128, 4, 128]) for k in range(2)] for g in range(G)]

    w_in, zeroed, ready, chain = c.sem("w_in"), c.sem("zeroed"), c.sem("ready"), c.sem("chain")
    ld = [c.loads(f"ld{b}", 2 * G) for b in range(2)]
    sts = c.loads("sts", G)
    by_image = lambda names: " ".join(f"{n}_{g}" for n in names.split() for g in range(G))
    iters = lambda names, end: by_image(" ".join(f"{n}{t}" for t in range(end) for n in names.split()))
    pe_s = c.steps("pe_s", by_image("xt a") + " " + iters("k1 k2 k3", IT))
    act_s = c.steps("act_s", by_image("xt p") + " " + " ".join(f"r{t}_{g} p{t}_{g}" for t in range(last) for g in range(G)))
    dve_s = c.steps("dve_s", by_image("rp") + " " + iters("k1 k2 k3", IT))
    pool_s = c.steps("pool_s", by_image("ry"))
    turn = c.sem("turn")
    halves = (slice(0, 64), slice(64, 128))

    with nc.Block() as block:
        @block.sync
        def _(sp):
            sp.dma_start(ident[:], a["eye"]).then_inc(w_in, 16)
            sp.dma_start(tops[:].rearrange("p a t -> p (a t)"),
                         top_in.rearrange("p t -> (p t)").partition_broadcast(128)).then_inc(w_in, 16)
            sp.wait_ge(zeroed, 2 * G)

            def load(i, b, L):
                pe_s.wait(sp, "xt_3", L - 2)
                pool_s.wait(sp, "ry_3", L - 2)
                for g in range(G):
                    for s in halves:
                        ld[b].inc(sp.dma_start(x[b][g][s, :, s], a2_in[4 * L + g, s]))

            def store(i, b, L):
                dve_s.wait(sp, f"k3{last}_3", L)
                for g in range(G):
                    sts.inc(sp.dma_start(zt_out[4 * L + g], zo[g][:]))
            pipeline(sp, LANES, 2, [(0, load), (1, store)], look=2)
            sts.wait(sp, LANES - 1)

        @block.tensor
        def _(pe):
            pe.wait_ge(w_in, 32)
            pe.wait_ge(ready, 1)

            def group(name, g, k, lhs, rhs):
                for q in range(4):
                    mm = pe.matmul(ps[g][k][:, q], lhs[:, q], rhs[:, q], start=True, stop=True)
                pe_s.did(mm, name)

            def lane(i, b, L):
                for g in range(G):
                    ld[b].wait(pe, i)
                    dve_s.wait(pe, f"k2{last}_{g}", L - 1)
                    for q in range(4):
                        mm = pe.transpose(ps[g][0][:, q], x[b][g][:, q], ident[:])
                    pe_s.did(mm, f"xt_{g}")
                for g in range(G):
                    act_s.wait(pe, f"xt_{g}", L)
                    dve_s.wait(pe, f"k3{last}_{g}", L - 1)
                    group(f"a_{g}", g, 1, xt[g], xt[g])
                for t in range(IT):
                    for g in range(G):
                        if t == 0:
                            pool_s.wait(pe, f"ry_{g}", L)
                            dve_s.wait(pe, f"rp_{g}", L)
                        else:
                            act_s.wait(pe, f"p{t - 1}_{g}", L)
                        group(f"k1{t}_{g}", g, t % 2, p[g], r[b][g])
                    for g in range(G):
                        dve_s.wait(pe, f"k1{t}_{g}", L)
                        group(f"k2{t}_{g}", g, 1 - t % 2, p[g], k1[g])
                    for g in range(G):
                        dve_s.wait(pe, f"k2{t}_{g}", L)
                        group(f"k3{t}_{g}", g, t % 2, p[g], k2[g])
            pipeline(pe, LANES, 2, [lane], look=2)

        @block.scalar
        def _(act):
            act.wait_ge(ready, 1)

            def lane(i, b, L):
                for g in range(G):
                    pe_s.wait(act, f"xt_{g}", L)
                    act_s.did(act.activation(xt[g][:], ps[g][0][:], ACT.Copy), f"xt_{g}")
                for g in range(G):
                    pe_s.wait(act, f"a_{g}", L)
                    act_s.did(act.activation(p[g][:], ps[g][1][:], ACT.Copy, scale=inv[:, 0:1]), f"p_{g}")
                for t in range(last):
                    for g in range(G):
                        dve_s.wait(act, f"k3{t}_{g}", L)
                        act_s.did(act.activation(r[b][g][:], k3[g][:], ACT.Copy, scale=0.25), f"r{t}_{g}")
                        for s in halves:
                            cp = act.activation(p[g][s, :, s], k3[g][s, :, 0:64], ACT.Copy)
                        act_s.did(cp, f"p{t}_{g}")
            pipeline(act, LANES, 2, [lane], look=2)

        @block.gpsimd
        def _(pool):
            pool.wait_ge(ready, 1)

            def lane(i, b, L):
                for g in range(G):
                    ld[b].wait(pool, i)
                    dve_s.wait(pool, f"k3{last}_{g}", L - 2)
                    pool.sem_inc(turn, 1)
                    for s in halves:
                        m = pool.tensor_scalar(r[b][g][s, :, 64:128], x[b][g][s, :, s], inv[s, 1:2], None, ALU.mult)
                    pool_s.did(m, f"ry_{g}")
            pipeline(pool, LANES, 2, [lane], look=2)

        @block.vector
        def _(dve):
            for b in range(2):
                for g in range(G):
                    dve.memset(x[b][g][:], 0.0).then_inc(zeroed, 1)
            dve.wait_ge(w_in, 32)
            dve.tensor_reduce(big[:], tops[:].rearrange("p a t -> p t a"), AX.X, ALU.max).then_inc(chain, 1)
            dve.wait_ge(chain, 1)
            dve.tensor_tensor(inv[:, 1:2], big[:, 0:1], big[:, 1:2], ALU.mult).then_inc(chain, 1)
            dve.wait_ge(chain, 2)
            dve.reciprocal(inv[:, 0:1], inv[:, 1:2]).then_inc(chain, 1)
            dve.wait_ge(chain, 3)
            dve.tensor_scalar(inv[:, 1:2], inv[:, 0:1], 0.25, None, ALU.mult).then_inc(ready, 1)

            def lane(i, b, L):
                def less(dst, scale, bank, cut=slice(0, 128)):
                    return dve.scalar_tensor_tensor(dst[:], r[b][g][:, :, cut], scale, bank[:, :, cut],
                                                    ALU.mult, ALU.subtract)
                for g in range(G):
                    act_s.wait(dve, f"p_{g}", L)
                    for s in halves:
                        m = dve.tensor_scalar(r[b][g][s, :, 0:64], p[g][s, :, s], 0.25, None, ALU.mult)
                    dve_s.did(m, f"rp_{g}")
                for t in range(IT):
                    for g in range(G):
                        pe_s.wait(dve, f"k1{t}_{g}", L)
                        dve_s.did(less(k1[g], 7.0, ps[g][t % 2]), f"k1{t}_{g}")
                    for g in range(G):
                        pe_s.wait(dve, f"k2{t}_{g}", L)
                        dve_s.did(less(k2[g], 15.0, ps[g][1 - t % 2]), f"k2{t}_{g}")
                    if t == last:
                        sts.wait(dve, L - 1)
                    for g in range(G):
                        pe_s.wait(dve, f"k3{t}_{g}", L)
                        if t < last:
                            dve_s.did(less(k3[g], 13.0, ps[g][t % 2]), f"k3{t}_{g}")
                        else:
                            dve_s.did(less(zo[g], 13.0, ps[g][t % 2], slice(64, 128)), f"k3{t}_{g}")
            pipeline(dve, LANES, 2, [lane], look=2)
    c.close()


def convolution(nc, a, phase, layer, v_in, res_out):
    c = Core(nc, phase)
    U = B // 16
    v = c.sb("v", [128, 2, B, C])
    vh = [c.sb(f"vh{k}", [128, 2, H, 16 * DH]) for k in range(2)]
    res = [c.sb(f"res{k}", [128, H, P]) for k in range(4)]
    band = c.sb("band", [128, H, 2, P])
    ps = [c.ps(f"p{k}", [128, P]) for k in range(4)]
    w_in, v_in_s = c.sem("w_in"), c.sem("v_in")
    out_st = [c.sem(f"out_st{k}") for k in range(4)]
    mm_s, cp_v, cp_a, vh_v, vh_a = (c.sem(n) for n in ("mm_s", "cp_v", "cp_a", "vh_v", "vh_a"))
    units = [(g, h) for g in range(U) for h in range(H)]

    with nc.Block() as block:
        @block.sync
        def _(sp):
            sp.dma_start(band[:].rearrange("p h k n -> p (h k n)"), a["band"][layer]).then_inc(w_in, 16)
            for k in range(2):
                sp.dma_start(v[:, k].rearrange("p b c -> p (b c)"), v_in[:, k].rearrange("p b c -> p (b c)"))\
                  .then_inc(v_in_s, 16)
            for g in range(U):
                sp.wait_ge(cp_v, (g + 1) * H // 2)
                sp.wait_ge(cp_a, (g + 1) * H // 2)
                sp.dma_start(res_out[16 * g:16 * g + 16].rearrange("b (d h) n -> (b d) (h n)", h=H),
                             res[g % 4][:].rearrange("p h n -> p (h n)")).then_inc(out_st[g % 4], 16)
            for k in range(4):
                sp.wait_ge(out_st[k], 16 * (U // 4))

        @block.tensor
        def _(pe):
            pe.wait_ge(w_in, 16)
            for u, (g, h) in enumerate(units):
                if h == 0:
                    pe.wait_ge(vh_v, g + 1)
                    pe.wait_ge(vh_a, g + 1)
                if u >= 4:
                    pe.wait_ge(cp_a if u % 2 else cp_v, (u - 4) // 2 + 1)
                for k in range(2):
                    mm = pe.matmul(ps[u % 4][:], vh[g % 2][:, k, h, :], band[:, h, k, :],
                                   start=k == 0, stop=k == 1)
                mm.then_inc(mm_s, 1)

        def copies(eng, copy, odd, done, sorted_):
            def by_heads(g):
                if g >= 2:
                    eng.wait_ge(mm_s, H * (g - 1))
                copy(vh[g % 2][:, odd].rearrange("p h (b d) -> p h b d", d=DH),
                     v[:, odd, 16 * g:16 * g + 16, :].rearrange("p b (h d) -> p h b d", d=DH)).then_inc(sorted_, 1)

            eng.wait_ge(v_in_s, 32)
            by_heads(0)
            for u, (g, h) in enumerate(units):
                if h == odd and g + 1 < U:
                    by_heads(g + 1)
                if u % 2 != odd:
                    continue
                eng.wait_ge(mm_s, u + 1)
                if g >= 4:
                    eng.wait_ge(out_st[g % 4], 16 * (g // 4))
                copy(res[g % 4][:, h, :], ps[u % 4][:]).then_inc(done, 1)

        @block.scalar
        def _(act):
            copies(act, lambda d, s: act.activation(d, s, ACT.Copy), 1, cp_a, vh_a)

        @block.vector
        def _(dve):
            copies(dve, dve.tensor_copy, 0, cp_v, vh_v)
    c.close()


def attend(nc, a, phase, layer, y_in, qk_in, v_in, zt_in, res_in, y_out):
    c = Core(nc, phase)
    G = 4
    qk = [c.sb(f"qk{k}", [C, 2, P]) for k in range(G)]
    v = [c.sb(f"v{k}", [128, 2, C]) for k in range(G)]
    zt = [c.sb(f"zt{k}", [128, 4, M]) for k in range(G)]
    res = [c.sb(f"res{k}", [C, P]) for k in range(G)]
    y = [c.sb(f"y{k}", [128, 2, C]) for k in range(G)]
    lm = [c.sb(f"lm{k}", [C, 2 * M]) for k in range(2)]
    qbd = [c.sb(f"qbd{k}", [C, H, M]) for k in range(2)]
    kbd = [c.sb(f"kbd{k}", [C, H, M]) for k in range(2)]
    mx3, nx3 = c.sb("mx3", [128, 4]), [c.sb(f"nx3{k}", [128, 4]) for k in range(2)]
    a3 = [c.sb(f"a3{k}", [128, 4, P]) for k in range(2)]
    sm3 = [c.sb(f"sm3{k}", [128, 4]) for k in range(4)]
    rc3 = c.sb("rc3", [128, 4])
    mx1 = c.sb("mx1", [128, 2, H])
    lg1 = [c.sb(f"lg1{k}", [128, 2, H, M]) for k in range(2)]
    a1 = [c.sb(f"a1{k}", [128, 2, H, M]) for k in range(2)]
    a3T = [c.sb(f"a3T{k}", [128, 2, 4, 128]) for k in range(2)]
    a1T = [c.sb(f"a1T{k}", [128, 4, 2, 128]) for k in range(4)]
    b3 = c.sb("b3", [128, 4, DH])
    wbd = [c.sb(f"wbd{k}", [128, 4 * 130]) for k in range(2)]
    rc1 = c.sb("rc1", [C, P])
    ao = [c.sb(f"ao{k}", [C, P]) for k in range(2)]
    yo = [c.sb(f"yo{k}", [128, 2, C]) for k in range(G)]
    ident = c.sb("ident", [128, 128])
    mask = c.sb("mask", [C, H, M])
    wout = c.sb("wout", [C, C])
    bout = c.sb("bout", [128, C])

    ps3 = c.ps("ps3", [128, 4, P])
    ps1 = c.ps("ps1", [128, 2, H, M])
    ptr = [c.ps(f"ptr{k}", [128, 4, 128]) for k in range(2)]
    psm = c.ps("psm", [128, 512])
    pso = c.ps("pso", [128, 512])

    w_in, turn = c.sem("w_in"), c.sem("turn")
    ld_qk, ld_vz, ld_ry = ([c.loads(f"{n}{k}", m) for k in range(G)]
                           for n, m in (("ld_qk", 1), ("ld_vz", 2), ("ld_ry", 2)))
    sts = [c.loads(f"sts{k}") for k in range(G)]
    prep, lm_s, bd_s = c.sem("prep"), c.flag("lm_s"), c.steps("bd_s", "qbd kbd")
    s_p = c.steps("s_p", "s3 s1")
    sf3, e3 = c.steps("sf3", "mx nx"), c.flag("e3")
    sf1, e1 = c.steps("sf1", "mx sub"), c.flag("e1")
    t_p, t_s = c.steps("t_p", "t0 t1 t2 t3"), c.steps("t_s", "t0 t1 t2 t3")
    b_p, b_s = c.flag("b_p"), c.steps("b_s", "rc b0 b1")
    w_p, w_s = c.flag("w_p"), c.steps("w_s", "w0 w1")
    o_p, o_s, res_s = c.flag("o_p"), c.steps("o_s", "rc div"), c.flag("res_s")
    y_p, y_s, bias_s = c.flag("y_p"), c.flag("y_s"), c.flag("bias_s")
    view = lambda t: t.rearrange("(b k p) c -> b p k c", p=128, k=2)
    NW = 6

    with nc.Block() as block:
        @block.sync
        def _(sp):
            sp.dma_start(ident[:], a["eye"]).then_inc(w_in, 16)
            sp.dma_start(mask[:].rearrange("c h m -> c (h m)"), a["head_mask"]).then_inc(w_in, 16)
            sp.dma_start(wout[:], a["w_out"][layer]).then_inc(w_in, 16)
            sp.dma_start(bout[:], a["b_out"][layer].partition_broadcast(128)).then_inc(w_in, 16)
            for k in range(2):
                sp.dma_start(wbd[k][:], a["sum_ones"]).then_inc(w_in, 16)

            def load_qk(i, g, L):
                s_p.wait(sp, "s1", L - G)
                ld_qk[g].inc(sp.dma_start(qk[g][:], qk_in[L]))

            def load_vz(i, g, L):
                w_p.wait(sp, L - G)
                ld_vz[g].inc(sp.dma_start(v[g][:], v_in[L]))
                ld_vz[g].inc(sp.dma_start(zt[g][:], zt_in[L]))

            def load_ry(i, g, L):
                y_s.wait(sp, L - G)
                res_s.wait(sp, L - G)
                ld_ry[g].inc(sp.dma_start(res[g][:], res_in[L]))
                ld_ry[g].inc(sp.dma_start(y[g][:], view(y_in)[L]))

            def store(i, g, L):
                bias_s.wait(sp, L)
                sts[g].inc(sp.dma_start(view(y_out)[L], yo[g][:]))
            pipeline(sp, B, G, [(0, load_qk), (2, load_vz), (4, load_ry), (9, store)])
            for g in range(G):
                sts[g].wait(sp, B // G - 1)

        @block.tensor
        def _(pe):
            pe.wait_ge(w_in, 16 * NW)

            def scores(i, g, L):
                bd_s.wait(pe, "kbd", L)
                e3.wait(pe, L - 1)
                for p in range(4):
                    mm = pe.matmul(ps3[:, p, :], qbd[g % 2][:, 2 * p:2 * p + 2, :].rearrange("c h m -> c (h m)"),
                                   qk[g][:, 1, :], start=True, stop=True)
                s_p.did(mm, "s3")
                sf1.wait(pe, "sub", L - 1)
                for k in range(2):
                    mm = pe.matmul(ps1[:, k].rearrange("p h m -> p (h m)"), qk[g][:, 0, 128 * k:128 * k + 128],
                                   kbd[g % 2][:].rearrange("c h m -> c (h m)"), start=True, stop=True)
                s_p.did(mm, "s1")

            def turn3(i, g, L):
                e3.wait(pe, L)
                for k in range(2):
                    t_s.wait(pe, f"t{k + 2}", L - 1)
                    for p in range(4):
                        mm = pe.transpose(ptr[k][:, p, :], a3[g % 2][:, p, 128 * k:128 * k + 128], ident[:])
                    t_p.did(mm, f"t{k}")

            def turn1(i, g, L):
                e1.wait(pe, L)
                for k in range(2):
                    t_s.wait(pe, f"t{k}", L)
                    for p in range(4):
                        mm = pe.transpose(ptr[k][:, p, :], a1[g % 2][:, k, 2 * p:2 * p + 2, :].rearrange(
                            "p h m -> p (h m)"), ident[:])
                    t_p.did(mm, f"t{k + 2}")

            def attn3_v(i, g, L):
                t_s.wait(pe, "t1", L)
                ld_vz[g].wait(pe, i)
                w_s.wait(pe, "w1", L - 1)
                for p in range(4):
                    for k in range(2):
                        mm = pe.matmul(psm[:, 16 * p:16 * p + 16], a3T[g % 2][:, k, p, :],
                                       v[g][:, k, 16 * p:16 * p + 16], start=k == 0, stop=k == 1)
                b_p.did(mm)

            def inverse_times(i, g, L):
                b_s.wait(pe, "b1", L)
                pe.sem_inc(turn, 1)
                for p in range(4):
                    for h in range(2):
                        r = slice(64 * h, 64 * h + 64)
                        mm = pe.matmul(psm[r, 128 + 8 * p:136 + 8 * p], zt[g][r, p, :], b3[r, p, :],
                                       start=True, stop=True)
                w_p.did(mm)

            def outs(i, g, L):
                w_s.wait(pe, "w1", L)
                t_s.wait(pe, "t3", L)
                y_s.wait(pe, L - 1)
                for p in range(4):
                    mm = pe.matmul(pso[:, 0:P], wbd[g % 2][:, 128 * p:128 * p + 128],
                                   a1T[g][:, p].rearrange("m k n -> m (k n)"), start=p == 0, stop=p == 3)
                o_p.did(mm)

            def project(i, g, L):
                res_s.wait(pe, L)
                for k in range(2):
                    mm = pe.matmul(pso[:, 384 + 64 * k:448 + 64 * k], ao[g % 2][:, 128 * k:128 * k + 128], wout[:],
                                   start=True, stop=True)
                y_p.did(mm)
            pipeline(pe, B, G, [(5, inverse_times), (7, project), (3, turn3), (6, outs), (4, attn3_v), (3, turn1),
                                (1, scores)])

        @block.gpsimd
        def _(pool):
            pool.wait_ge(prep, 1)
            pool.wait_ge(w_in, 16 * NW)

            def landmark_rows(i, g, L):
                lm_s.wait(pool, L)
                s_p.wait(pool, "s1", L - 2)
                for n, (t, dst) in enumerate((("qbd", qbd), ("kbd", kbd))):
                    bd_s.did(pool.tensor_tensor(dst[g % 2][:], lm[g % 2][:, M * n:M * n + M].unsqueeze(1)
                                                .to_broadcast([C, H, M]), mask[:], ALU.mult), t)

            def add_res(i, g, L):
                o_s.wait(pool, "div", L)
                ld_ry[g].wait(pool, i)
                res_s.did(pool.tensor_tensor(ao[g % 2][:], ao[g % 2][:], res[g][:], ALU.add))

            def add_bias(i, g, L):
                y_s.wait(pool, L)
                bias_s.did(pool.tensor_tensor(yo[g][:], yo[g][:], bout[:].unsqueeze(1).to_broadcast([128, 2, C]),
                                              ALU.add))
            pipeline(pool, B, G, [(7, add_bias), (6, add_res), (0, landmark_rows)])

        @block.scalar
        def _(act):
            def exps3(i, g, L):
                sf3.wait(act, "nx", L)
                t_p.wait(act, "t1", L - 2)
                b_s.wait(act, "rc", L - 4)
                for p in range(4):
                    ex = act.activation(a3[g % 2][:, p, :], ps3[:, p, :], ACT.Exp, bias=nx3[g % 2][:, p:p + 1],
                                        accum_out=sm3[g][:, p:p + 1])
                e3.did(ex)

            def exps1(i, g, L):
                sf1.wait(act, "sub", L)
                t_p.wait(act, "t3", L - 2)
                e1.did(act.activation(a1[g % 2][:], lg1[g % 2][:], ACT.Exp))

            def copies3(i, g, L):
                b_p.wait(act, L - 2)
                for k in range(2):
                    t_p.wait(act, f"t{k}", L)
                    t_s.did(act.activation(a3T[g % 2][:, k], ptr[k][:], ACT.Copy), f"t{k}")

            def copies1(i, g, L):
                o_p.wait(act, L - 4)
                for k in range(2):
                    t_p.wait(act, f"t{k + 2}", L)
                    t_s.did(act.activation(a1T[g][:, :, k, :], ptr[k][:], ACT.Copy), f"t{k + 2}")
            pipeline(act, B, G, [(2, exps3), (3, copies3), (2, exps1), (3, copies1)])

        @block.vector
        def _(dve):
            dve.wait_ge(w_in, 16 * NW)
            dve.tensor_scalar(mask[:], mask[:], 0.25, None, ALU.mult).then_inc(prep, 1)

            def means(i, g, L):
                ld_qk[g].wait(dve, i)
                bd_s.wait(dve, "kbd", L - 2)
                lm_s.did(dve.tensor_reduce(lm[g % 2][:], qk[g][:].rearrange("c t (m l) -> c (t m) l", l=4), AX.X,
                                           ALU.add))

            def maxima3(i, g, L):
                s_p.wait(dve, "s3", L)
                sf3.wait(dve, "nx", L - 1)
                sf3.did(dve.tensor_reduce(mx3[:], ps3[:], AX.X, ALU.max), "mx")
                sf3.wait(dve, "mx", L)
                e3.wait(dve, L - 2)
                sf3.did(dve.tensor_scalar(nx3[g % 2][:], mx3[:], -1.0, None, ALU.mult), "nx")

            def maxima1(i, g, L):
                s_p.wait(dve, "s1", L)
                sf1.wait(dve, "sub", L - 1)
                sf1.did(dve.tensor_reduce(mx1[:], ps1[:], AX.X, ALU.max), "mx")
                sf1.wait(dve, "mx", L)
                e1.wait(dve, L - 2)
                sf1.did(dve.tensor_tensor(lg1[g % 2][:].rearrange("p k h m -> p (k h) m"),
                                          ps1[:].rearrange("p k h m -> p (k h) m"),
                                          mx1[:].rearrange("p k h -> p (k h)").unsqueeze(2)
                                          .to_broadcast([128, 2 * H, M]), ALU.subtract), "sub")

            def divide3(i, g, L):
                e3.wait(dve, L)
                b_s.wait(dve, "b1", L - 1)
                b_s.did(dve.reciprocal(rc3[:], sm3[g][:]), "rc")
                b_s.wait(dve, "rc", L)
                b_p.wait(dve, L)
                w_p.wait(dve, L - 1)
                for h in range(2):
                    r = slice(64 * h, 64 * h + 64)
                    b_s.did(dve.tensor_tensor(
                        b3[r], psm[r, 0:64].rearrange("p (q h d) -> p q h d", h=2, d=DH)[:, :, h, :],
                        rc3[r].unsqueeze(2).to_broadcast([64, 4, DH]), ALU.mult), f"b{h}")

            def place(i, g, L):
                w_p.wait(dve, L)
                o_p.wait(dve, L - 2)
                for h in range(2):
                    r = slice(64 * h, 64 * h + 64)
                    w_s.did(dve.tensor_copy(wbd[g % 2][r].rearrange("p (q c) -> p q c", c=130)[:, :, h:h + 57:8],
                                            psm[r, 128:160].rearrange("p (q d) -> p q d", d=DH)), f"w{h}")

            def divide1(i, g, L):
                o_p.wait(dve, L)
                o_s.wait(dve, "div", L - 1)
                o_s.did(dve.reciprocal(rc1[:], pso[64:128, 0:P]), "rc")
                o_s.wait(dve, "rc", L)
                y_p.wait(dve, L - 2)
                o_s.did(dve.tensor_tensor(ao[g % 2][:], pso[0:64, 0:P], rc1[:], ALU.mult), "div")

            def result(i, g, L):
                y_p.wait(dve, L)
                ld_ry[g].wait(dve, i)
                sts[g].wait(dve, i - 1)
                y_s.did(dve.tensor_tensor(yo[g][:].rearrange("p k c -> p (k c)"), pso[:, 384:512],
                                          y[g][:].rearrange("p k c -> p (k c)"), ALU.add))
            pipeline(dve, B, G, [(2, maxima3), (5, place), (7, result), (2, maxima1), (6, divide1), (0, means),
                                 (4, divide3)])
    c.close()


def moe_gates(nc, a, x_in, gate_out):
    c = Core(nc, "gate8")
    G, K, E = 4, 4, 8
    LANES = T // 512
    KT = LANES * K
    x = [c.sb(f"x{k}", [128, K, C]) for k in range(G)]
    xT = [c.sb(f"xT{k}", [C, K, 128]) for k in range(2)]
    lg = c.sb("lg", [128, LANES, K, E])
    sel = c.sb("sel", [128, KT, E])
    u = c.sb("u", [128, KT, E])
    w = c.sb("w", [128, KT, E])
    m = c.sb("m", [128, KT])
    ident = c.sb("ident", [128, 128])
    gw = c.sb("gw", [C, E])
    gb = c.sb("gb", [128, E])
    pT = c.ps("pT", [C, K, 128])
    pl = c.ps("pl", [128, K, E])
    w_in, turn, dv, ex, st = c.sem("w_in"), c.sem("turn"), c.sem("dve_done"), c.sem("exp_done"), c.sem("st")
    ld = [c.loads(f"ld{k}") for k in range(G)]
    xT_p, xT_s, l_p, l_s = (c.flag(n) for n in ("xT_p", "xT_s", "l_p", "l_s"))
    rows = lambda t: t.rearrange("(l p k) c -> l p k c", p=128, k=K)

    with nc.Block() as block:
        @block.sync
        def _(sp):
            sp.dma_start(ident[:], a["eye"]).then_inc(w_in, 16)
            sp.dma_start(gw[:], a["gate_w"]).then_inc(w_in, 16)
            sp.dma_start(gb[:], a["gate_b"].partition_broadcast(128)).then_inc(w_in, 16)

            def load(i, g, L):
                xT_p.wait(sp, L - G)
                ld[g].inc(sp.dma_start(x[g][:], rows(x_in)[L]))
            pipeline(sp, LANES, G, [load])

        @block.tensor
        def _(pe):
            pe.wait_ge(w_in, 48)

            def tr(i, g, L):
                ld[g].wait(pe, i)
                xT_s.wait(pe, L - 1)
                pe.sem_inc(turn, 1)
                for k in range(K):
                    mm = pe.transpose(pT[:, k, :], x[g][:, k, :], ident[:])
                xT_p.did(mm)

            def logits(i, g, L):
                xT_s.wait(pe, L)
                l_s.wait(pe, L - 1)
                for k in range(K):
                    mm = pe.matmul(pl[:, k, :], xT[g % 2][:, k, :], gw[:], start=True, stop=True)
                l_p.did(mm)
            pipeline(pe, LANES, G, [tr, logits])

        @block.scalar
        def _(act):
            def copy(i, g, L):
                xT_p.wait(act, L)
                l_p.wait(act, L - 2)
                xT_s.did(act.activation(xT[g % 2][:], pT[:], ACT.Copy))
            pipeline(act, LANES, G, [copy])

        @block.vector
        def _(dve):
            dve.wait_ge(w_in, 48)

            def bias(i, g, L):
                l_p.wait(dve, L)
                out = lg[:, L] if isinstance(L, int) else lg[:, bass.ds(L, 1)].rearrange("p a k e -> p (a k) e")
                l_s.did(dve.tensor_tensor(out, pl[:], gb[:].unsqueeze(1).to_broadcast([128, K, E]), ALU.add))
            pipeline(dve, LANES, G, [None, bias])

    with nc.Block() as block:
        s = lg[:].rearrange("p l k e -> p (l k) e")
        rest = {}

        @block.vector
        def _(dve):
            n = [0]

            def link(ins):
                n[0] += 1
                ins.then_inc(dv, 1)
                dve.wait_ge(dv, n[0])

            wide = lambda t: t[:].unsqueeze(2).to_broadcast([128, KT, E])
            link(dve.tensor_reduce(m[:], s, AX.X, ALU.max))
            link(dve.tensor_tensor(s, s, wide(m), ALU.subtract))
            rest["logits"] = n[0]
            dve.wait_ge(ex, 1)
            link(dve.tensor_reduce(m[:], s, AX.X, ALU.add))
            link(dve.reciprocal(m[:], m[:]))
            link(dve.tensor_tensor(s, s, wide(m), ALU.mult))
            best_two(dve, link, s, sel, u, w, m, E, KT)
            link(dve.tensor_tensor(sel[:], sel[:], s, ALU.mult))
            rest["gates"] = n[0]

        @block.scalar
        def _(act):
            act.wait_ge(dv, rest["logits"])
            act.activation(s, s, ACT.Exp).then_inc(ex, 1)

        @block.sync
        def _(sp):
            sp.wait_ge(dv, rest["gates"])
            sp.dma_start(gate_out.rearrange("(l p k) e -> p l (k e)", p=128, k=K),
                         sel[:].rearrange("p (l k) e -> p l (k e)", k=K)).then_inc(st, 16)
            sp.wait_ge(st, 16)
    c.close()


def vit_tower(nc, a, out):
    def dram(name, *shape):
        return nc.dram_tensor(name, shape, F32).ap()

    images = lambda t: t.rearrange("(b p) c -> b p c", b=B)
    h = [dram(f"h{n}", T, C) for n in range(4)]
    gat, dst_rows, top = dram("gat", T, 20), dram("dst_rows", T, 4), dram("top", 128, 4)
    tables = [dram(f"table{n}", ROWS, 20) for n in range(TABLES)]
    gate4, gate8 = dram("gate4", T, 4), dram("gate8", T, 8)
    ya, yb = dram("ya", T, C), dram("yb", T, C)
    qk, a2, zt = dram("qk", B, C, 2, P), dram("a2", B, 128, 4, M), dram("zt", B, 128, 4, M)
    v, res, sums = dram("v", 128, 2, B, C), dram("res", B, C, P), dram("sums", 128, 2)
    by_image = lambda t: t.rearrange("p k b c -> b p k c")

    tokenizer(nc, a, images(h[0]))
    retention(nc, a, images(h[0]), images(h[1]), gat, dst_rows, top)
    edges(nc, a, a["src_idx"], a["dst_idx"], gat, dst_rows, top, tables)
    gat_gates(nc, a, gat, dst_rows, top, tables, gate4)
    dense(nc, a, "moe4", h[1], h[2], 4, gate=gate4)
    for layer, y in ((0, h[2]), (1, yb)):
        landmarks(nc, a, f"lmk{layer}", layer, y, qk, by_image(v), a2, sums)
        inverse(nc, a, f"inv{layer}", a2, sums, zt)
        convolution(nc, a, f"conv{layer}", layer, v, res)
        attend(nc, a, f"att{layer}", layer, y, qk, by_image(v), zt, res, ya)
        if layer == 0:
            dense(nc, a, "mlp0", ya, yb, 1, pre=True, post=False)
        else:
            dense(nc, a, "mlp1", ya, h[3], 1, pre=True, extra=h[2])
    moe_gates(nc, a, h[3], gate8)
    dense(nc, a, "moe8", h[3], out, 8, gate=gate8)


def constants():
    d = {}
    eye = np.eye(128)
    d["eye"] = eye
    d["eye16"] = eye[:64, :64] / 16
    d["avg"] = np.kron(np.eye(2), np.full((64, 64), 1 / 64))
    pick = np.zeros((2, C, 2, N, 2, N, 2))
    for t in range(2):
        for n in range(N):
            for b in range(2):
                pick[b, :, t, n, t, n, b] = 1 / C
    d["pick"] = pick.reshape(128, 8 * N * N)
    d["ones_bd"] = np.kron(np.eye(2), np.ones((64, 64)))
    d["head_mask"] = np.repeat(np.repeat(np.eye(8), 8, 0), 64, 1)
    ones = np.zeros((2, M, 4 * 130))
    for q in range(4):
        for h in range(2):
            ones[h, :, 128 * q + 64 + 2 * q + h:128 * q + 128:8] = 1
    d["sum_ones"] = ones.reshape(128, 4 * 130)
    d["col_no"] = np.arange(128.0)
    d["low"] = np.tril(np.ones((128, 128)), -1)
    d["spare_row"] = T + np.arange(128.0)[:, None]
    pos, even = np.arange(float(P)), np.arange(0, C, 2)
    ang = np.float32(pos)[:, None] * np.float32(1.0 / 10000.0 ** (even / C))[None]
    zoom = ((even + 0.4 * C) / (1.4 * C))[None] ** (pos[:, None] / 512.0)
    sign = np.where(np.arange(C) % 2, 1.0, -1.0)[:, None]
    rows = lambda t: np.repeat(t, 2, 1).T
    d["cosT"] = np.concatenate([rows(np.cos(ang) * zoom), rows(np.cos(ang) / zoom)])
    d["sinT"] = np.concatenate([rows(np.sin(ang) * zoom) * sign, rows(np.sin(ang) / zoom) * sign])
    diff = np.arange(P)[None] - np.arange(128)[:, None]
    fade = np.where(diff >= 0, 0.96875 ** np.maximum(diff, 0), 0.0)
    d["decay"] = np.concatenate([fade, fade[:, :128]], 1)
    return {k: v.astype(np.float32) for k, v in d.items()}


def lay_out(i):
    d = constants()
    x = i["x"].reshape(B // 2, 128, 16, 4, 16, 4).transpose(0, 1, 3, 5, 2, 4)
    d["x"] = x.reshape(B // 2, 128, N * P)
    d["wkv_t"] = i["L0_tok_Wkv"].T
    d["wq_t"] = i["L0_tok_Wq"].T
    d["proj_t"] = i["L0_tok_proj_w"].T
    d["proj_b"] = i["L0_tok_proj_b"]
    two = lambda v: np.concatenate([v, v])
    d["tok_ln"] = np.stack([two(i[f"L0_tok_ln_{k}"]) for k in ("kv_w", "q_w", "kv_b", "q_b")], 1)
    wq, wk = i["L0_attn_W_Q"], i["L0_attn_W_K"]
    swap = np.arange(C) ^ 1
    d["wqk"] = np.stack([np.concatenate([wq, wk], 1), np.concatenate([wq[:, swap], wk[:, swap]], 1)], 1)
    d["wv"] = i["L0_attn_W_V"]
    d["w_gat"] = i["L0_ffn_W_gat"]
    d["att_src"], d["att_dst"] = i["L0_ffn_att_src"].reshape(16), i["L0_ffn_att_dst"].reshape(16)
    d["b_gat"], d["gat_g"], d["gat_b"] = i["L0_ffn_b_gat"], i["L0_ffn_ln_gamma"], i["L0_ffn_ln_beta"]
    e = i["L0_ffn_edge_index"].reshape(2, 128, -1, CH).transpose(0, 2, 1, 3)
    d["src_idx"], d["dst_idx"] = e[0], e[1]
    for phase, name in (("moe4", "L0_ffn_"), ("moe8", "L1_ffn_")):
        for n in ("W1", "W2", "b2"):
            d[f"{phase}_{n.lower()}"] = i[name + n]
        d[phase + "_b1"] = i[name + "b1"].T
    for l in range(2):
        for n in ("w1", "w2", "b2"):
            d[f"mlp{l}_{n}"] = i["L1_attn_" + n][l:l + 1]
        d[f"mlp{l}_b1"] = i["L1_attn_b1"][l:l + 1].T
        d[f"mlp{l}_ln"] = np.stack([i["L1_attn_ln2_g"][l], i["L1_attn_ln2_b"][l]], 1)
    d["w_qkv"] = i["L1_attn_w_qkv"].reshape(2, C, 3, C)
    d["ln1"] = np.stack([i["L1_attn_ln1_g"], i["L1_attn_ln1_b"]], 2)
    pad = np.zeros((2, H, 2 * P - 1), np.float32)
    pad[:, :, P - 17:P + 16] = i["L1_attn_res_w"].reshape(2, H, 33)
    at = np.arange(P)[:, None] - np.arange(P)[None] + P - 1
    d["band"] = pad[:, :, at].reshape(2, H, 2, 128, P).transpose(0, 3, 1, 2, 4).reshape(2, 128, H * 2 * P)
    d["w_out"] = i["L1_attn_w_out"].reshape(2, H, DH, C).transpose(0, 2, 1, 3).reshape(2, C, C)
    d["b_out"] = i["L1_attn_b_out"]
    d["gate_w"], d["gate_b"] = i["L1_ffn_gate_w"], i["L1_ffn_gate_b"]
    return {k: np.ascontiguousarray(v) for k, v in d.items()}


def kernel(**inputs):
    import concourse.bacc as bacc
    from concourse.bass_utils import run_bass_kernel_spmd

    nc = bacc.Bacc("TRN2", target_bir_lowering=False, num_devices=1)
    arrays = lay_out({k: np.asarray(v) for k, v in inputs.items()})
    a = {k: nc.dram_tensor(f"in_{k}", v.shape, mybir.dt.from_np(v.dtype), kind="ExternalInput").ap()
         for k, v in arrays.items()}
    out = nc.dram_tensor("out", (T, C), F32, kind="ExternalOutput").ap()
    vit_tower(nc, a, out)
    r = run_bass_kernel_spmd(nc, [{f"in_{k}": v for k, v in arrays.items()}], core_ids=[0])
    return r.results[0]["out"].reshape(B, P, C)
```
